# Optimizing a Trainium2 kernel written in Bass

```python
import numpy as np
import jax
import jax.numpy as jnp

def _softmax(x, axis=-1):
    return jax.nn.softmax(x, axis=axis)

def _gelu(x):
    return jax.nn.gelu(x, approximate=True)

def _silu(x):
    return jax.nn.silu(x)

def _sigmoid(x):
    return jax.nn.sigmoid(x)

def _layernorm(x, axis=-1, eps=1e-05):
    m = jnp.mean(x, axis=axis, keepdims=True)
    v = jnp.var(x, axis=axis, keepdims=True)
    return (x - m) / jnp.sqrt(v + eps)

def _scatter_add(tgt, idx, src, axis=0):
    return tgt.at[idx].add(src)

def _segment_sum(src, seg, n):
    return jax.ops.segment_sum(src, seg, n)
kernel_name = 'mk_gnn_resnorm_d4_gnn_r64_90af4f'

def setup_inputs(seed: int=0):
    np.random.seed(seed)
    _w = jnp.asarray

    def _rec_inputs():
        import jax
        import jax.numpy as jnp
        _gk = jax.random.key(seed)
        x = -0.000202 + 1 * jax.random.normal(jax.random.fold_in(_gk, 1), (50000, 128), jnp.float32)
        src = jax.random.randint(jax.random.fold_in(_gk, 2), (25000,), 0, 50000, jnp.int32)
        dst = jnp.minimum((50000 * jax.random.uniform(jax.random.fold_in(_gk, 3), (25000,)) ** 2.0).astype(jnp.int32), 49999)
        _o = jnp.argsort(dst, stable=True)
        src = src[_o]
        dst = dst[_o]
        edge_attr_128 = -8.513e-05 + 0.999844 * jax.random.normal(jax.random.fold_in(_gk, 13), (25000, 128), jnp.float32)
        edge_weight = jax.random.uniform(jax.random.fold_in(_gk, 15), (25000,), jnp.float32, 0.0, 0.999999)
        return (x, src, dst, edge_attr_128, edge_weight)
    x, src, dst, edge_attr_128, edge_weight = _rec_inputs()

    def _L0_gnn_setup():
        import jax, jax.numpy as jnp
        import numpy as np
        N_NODES = 50000
        N_EDGES = 12500
        HIDDEN = 128
        key = jax.random.key(seed)
        k1, k2, k3, k4, k5, k6 = jax.random.split(key, 6)
        stdv = 1.0 / np.sqrt(HIDDEN)
        h = jax.random.normal(k1, (N_NODES, HIDDEN), dtype=jnp.float32)
        edge_src = jax.random.randint(k2, (N_EDGES,), 0, N_NODES, dtype=jnp.int32)
        edge_dst = jax.random.randint(k3, (N_EDGES,), 0, N_NODES, dtype=jnp.int32)
        edge_val = jax.random.uniform(k4, (N_EDGES,), dtype=jnp.float32)
        weight = jax.random.uniform(k5, (HIDDEN, HIDDEN), dtype=jnp.float32, minval=-stdv, maxval=stdv)
        bias = jax.random.uniform(k6, (HIDDEN,), dtype=jnp.float32, minval=-stdv, maxval=stdv)
        return {'h': h, 'edge_src': edge_src, 'edge_dst': edge_dst, 'edge_val': edge_val, 'weight': weight, 'bias': bias}
    _L0_gnn_all = _L0_gnn_setup()
    _L0_gnn_in = {k: v for k, v in _L0_gnn_all.items() if k in ('weight', 'bias')}
    del _L0_gnn_all

    def _L1_gnn_setup():
        import jax, jax.numpy as jnp
        import numpy as np
        N_PIX, N_SUP, E, D, L = (250000, 50000, 12500, 128, 5)
        GAMA = 0.9
        RHP = 5
        BN_EPS = 1e-05
        LEAKY_SLOPE = 0.01
        key = jax.random.key(seed)
        ks = jax.random.split(key, 6)
        x = jax.random.normal(ks[0], (N_PIX, D), jnp.float32)
        seg_ids = jax.random.randint(ks[1], (N_PIX,), 0, N_SUP)
        edge_index = jax.random.randint(ks[2], (2, E), 0, N_SUP)
        edge_weight = jax.random.uniform(ks[3], (E,), jnp.float32) / 8.0
        W = jax.random.normal(ks[4], (L, D, D), jnp.float32) / np.sqrt(D)
        b = jnp.zeros((L, D), jnp.float32)
        gamma = jnp.ones((L, D), jnp.float32)
        beta = jnp.zeros((L, D), jnp.float32)
        return dict(x=x, W=W, b=b, gamma=gamma, beta=beta, edge_weight=edge_weight, seg_ids=seg_ids, edge_index=edge_index)
    _L1_gnn_all = _L1_gnn_setup()
    _L1_gnn_in = {k: v for k, v in _L1_gnn_all.items() if k in ('W', 'b', 'gamma', 'beta')}
    del _L1_gnn_all

    def _L2_gnn_setup():
        import jax, jax.numpy as jnp
        import numpy as np
        N_NODES = 100000
        N_EDGES = 10000
        D_IN = 128
        D_OUT = 128
        key = jax.random.key(seed)
        k1, k2, k3, k4, k5, k6 = jax.random.split(key, 6)
        nfeat = jax.random.normal(k1, (N_NODES, D_IN), dtype=jnp.float32)
        efeat = jax.random.normal(k2, (N_EDGES, D_IN), dtype=jnp.float32)
        src = jax.random.randint(k3, (N_EDGES,), 0, N_NODES, dtype=jnp.int64)
        dst = jax.random.randint(k4, (N_EDGES,), 0, N_NODES, dtype=jnp.int64)
        W = jax.random.normal(k5, (D_IN, D_OUT), dtype=jnp.float32) * (1.0 / np.sqrt(D_IN))
        b = jnp.zeros((D_OUT,), dtype=jnp.float32)
        We = jax.random.normal(k6, (D_IN, D_OUT), dtype=jnp.float32) * (1.0 / np.sqrt(D_IN))
        be = jnp.zeros((D_OUT,), dtype=jnp.float32)
        return {'nfeat': nfeat, 'efeat': efeat, 'src': src, 'dst': dst, 'W': W, 'b': b, 'We': We, 'be': be}
    _L2_gnn_all = _L2_gnn_setup()
    _L2_gnn_in = {k: v for k, v in _L2_gnn_all.items() if k in ('W', 'b', 'We', 'be')}
    del _L2_gnn_all

    def _L3_gnn_setup():
        import jax, jax.numpy as jnp
        import numpy as np
        N = 50000
        E = 9375
        IN = 128
        H = 4
        C = 32
        B = 3
        NEG_SLOPE = 0.2
        key = jax.random.key(seed)
        ks = jax.random.split(key, 6)
        x = jax.random.normal(ks[0], (N, IN), dtype=jnp.float32)
        edge_index = jax.random.randint(ks[1], (2, E), 0, N)
        coeffs_t = jnp.array([0.25, 0.5, 0.25], dtype=jnp.float32)
        glorot_w = float(np.sqrt(2.0) * np.sqrt(6.0 / (H * C + IN)))
        glorot_a = float(np.sqrt(2.0) * np.sqrt(6.0 / (1 + C)))
        lin_weight = jax.random.uniform(ks[2], (B, H * C, IN), jnp.float32, -glorot_w, glorot_w)
        lin_bias = jnp.zeros((B, H * C), dtype=jnp.float32)
        att_src = jax.random.uniform(ks[3], (B, 1, H, C), jnp.float32, -glorot_a, glorot_a)
        att_dst = jax.random.uniform(ks[4], (B, 1, H, C), jnp.float32, -glorot_a, glorot_a)
        return {'x': x, 'edge_index': edge_index, 'coeffs_t': coeffs_t, 'lin_weight': lin_weight, 'lin_bias': lin_bias, 'att_src': att_src, 'att_dst': att_dst}
    _L3_gnn_all = _L3_gnn_setup()
    _L3_gnn_in = {k: v for k, v in _L3_gnn_all.items() if k in ('coeffs_t', 'lin_weight', 'lin_bias', 'att_src', 'att_dst')}
    del _L3_gnn_all
    return {'x': x, 'src': src, 'dst': dst, 'edge_attr_128': edge_attr_128, 'edge_weight': edge_weight, 'L0_gnn_weight': _L0_gnn_in['weight'], 'L0_gnn_bias': _L0_gnn_in['bias'], 'L1_gnn_W': _L1_gnn_in['W'], 'L1_gnn_b': _L1_gnn_in['b'], 'L1_gnn_gamma': _L1_gnn_in['gamma'], 'L1_gnn_beta': _L1_gnn_in['beta'], 'L2_gnn_W': _L2_gnn_in['W'], 'L2_gnn_b': _L2_gnn_in['b'], 'L2_gnn_We': _L2_gnn_in['We'], 'L2_gnn_be': _L2_gnn_in['be'], 'L3_gnn_coeffs_t': _L3_gnn_in['coeffs_t'], 'L3_gnn_lin_weight': _L3_gnn_in['lin_weight'], 'L3_gnn_lin_bias': _L3_gnn_in['lin_bias'], 'L3_gnn_att_src': _L3_gnn_in['att_src'], 'L3_gnn_att_dst': _L3_gnn_in['att_dst']}

def reference(x, src, dst, edge_attr_128, edge_weight, L0_gnn_weight, L0_gnn_bias, L1_gnn_W, L1_gnn_b, L1_gnn_gamma, L1_gnn_beta, L2_gnn_W, L2_gnn_b, L2_gnn_We, L2_gnn_be, L3_gnn_coeffs_t, L3_gnn_lin_weight, L3_gnn_lin_bias, L3_gnn_att_src, L3_gnn_att_dst):
    import jax
    import jax.numpy as jnp

    def _L0_gnn_ref(h, edge_src, edge_dst, edge_val, weight, bias):
        import jax, jax.numpy as jnp
        import numpy as np
        N_NODES = 50000
        N_EDGES = 12500
        HIDDEN = 128
        support = jnp.matmul(h, weight)
        msgs = edge_val[:, None] * support[edge_src]
        out = jax.ops.segment_sum(msgs, edge_dst, num_segments=N_NODES)
        out = out + bias
        out = jax.nn.relu(out)
        return out

    def _L1_gnn_ref(x, W, b, gamma, beta, edge_weight, seg_ids, edge_index):
        import jax, jax.numpy as jnp
        import numpy as np
        N_PIX, N_SUP, E, D, L = (250000, 50000, 12500, 128, 5)
        GAMA = 0.9
        RHP = 5
        BN_EPS = 1e-05
        LEAKY_SLOPE = 0.01
        src, dst = (edge_index[0], edge_index[1])
        counts = jax.ops.segment_sum(jnp.ones((x.shape[0],), x.dtype), seg_ids, num_segments=N_SUP)
        pooled = jax.ops.segment_sum(x, seg_ids, num_segments=N_SUP)
        h = pooled / jnp.maximum(counts, 1.0)[:, None]

        def prop(z):
            return jax.ops.segment_sum(edge_weight[:, None] * z[src], dst, num_segments=N_SUP)
        for i in range(L):
            z = h @ W[i] + b[i]
            x_start = prop(z)
            xi = h
            for _ in range(RHP):
                xi = (prop(xi) + x_start) / (2.0 + GAMA)
            mean = jnp.mean(xi, axis=0)
            var = jnp.var(xi, axis=0)
            out = gamma[i] * (xi - mean) / jnp.sqrt(var + BN_EPS) + beta[i]
            h = jnp.where(out > 0, out, LEAKY_SLOPE * out)
        return h[seg_ids]

    def _L2_gnn_ref(nfeat, efeat, src, dst, W, b, We, be):
        import jax, jax.numpy as jnp
        import numpy as np
        N_NODES = 100000
        N_EDGES = 10000
        D_IN = 128
        D_OUT = 128
        N = nfeat.shape[0]
        ones_e = jnp.ones(src.shape, dtype=nfeat.dtype)
        in_deg = jax.ops.segment_sum(ones_e, dst, num_segments=N)
        out_deg = jax.ops.segment_sum(ones_e, src, num_segments=N)
        norm_src = jnp.clip(out_deg, 1.0, None) ** (-0.5)
        norm_dst = jnp.clip(in_deg, 1.0, None) ** (-0.5)
        h = nfeat * norm_src[:, None]
        agg = jax.ops.segment_sum(h[src], dst, num_segments=N)
        conv = agg @ W * norm_dst[:, None] + b
        sfeat = (nfeat @ W + b) / (in_deg + 1.0)[:, None]
        out = conv + sfeat
        e = efeat @ We + be
        esum = jax.ops.segment_sum(e, dst, num_segments=N)
        h_e = esum / jnp.clip(in_deg, 1.0, None)[:, None]
        return out + h_e

    def _L3_gnn_ref(x, edge_index, coeffs_t, lin_weight, lin_bias, att_src, att_dst):
        import jax, jax.numpy as jnp
        import numpy as np
        N = 50000
        E = 9375
        IN = 128
        H = 4
        C = 32
        B = 3
        NEG_SLOPE = 0.2
        W = jnp.einsum('b,boi->oi', coeffs_t, lin_weight)
        bias = jnp.einsum('b,bo->o', coeffs_t, lin_bias)
        a_src = jnp.einsum('b,bqhc->qhc', coeffs_t, att_src)
        a_dst = jnp.einsum('b,bqhc->qhc', coeffs_t, att_dst)
        n = x.shape[0]
        xt = (x @ W.T + bias).reshape(n, H, C)
        alpha_src = jnp.sum(xt * a_src, axis=-1)
        alpha_dst = jnp.sum(xt * a_dst, axis=-1)
        row, col = (edge_index[0], edge_index[1])
        alpha = alpha_src[row] + alpha_dst[col]
        alpha = jax.nn.leaky_relu(alpha, NEG_SLOPE)
        amax = jax.ops.segment_max(alpha, col, num_segments=n)
        ex = jnp.exp(alpha - amax[col])
        denom = jax.ops.segment_sum(ex, col, num_segments=n)
        alpha = ex / (denom[col] + 1e-16)
        msg = xt[row] * alpha[..., None]
        out = jax.ops.segment_sum(msg, col, num_segments=n)
        return out.reshape(n, H * C)
    edge_index = jnp.stack([src, dst])
    batch0 = jnp.zeros((50000,), jnp.int32)
    x = _layernorm(x + _L0_gnn_ref(x, src, dst, edge_weight, L0_gnn_weight, L0_gnn_bias), axis=-1)
    x = _layernorm(x + _L1_gnn_ref(x, L1_gnn_W, L1_gnn_b, L1_gnn_gamma, L1_gnn_beta, edge_weight, batch0, edge_index), axis=-1)
    x = _layernorm(x + _L2_gnn_ref(x, edge_attr_128, src, dst, L2_gnn_W, L2_gnn_b, L2_gnn_We, L2_gnn_be), axis=-1)
    x = _layernorm(x + _L3_gnn_ref(x, edge_index, L3_gnn_coeffs_t, L3_gnn_lin_weight, L3_gnn_lin_bias, L3_gnn_att_src, L3_gnn_att_dst), axis=-1)
    return x

_drawn_inputs = setup_inputs


def setup_inputs(seed=0):
    import zlib

    import numpy as np

    out = dict(_drawn_inputs(seed))
    spreads = {'L1_gnn_b': (0.0, 0.1),
     'L1_gnn_gamma': (1.0, 0.2),
     'L1_gnn_beta': (0.0, 0.1),
     'L2_gnn_b': (0.0, 0.1),
     'L2_gnn_be': (0.0, 0.326),
     'L3_gnn_lin_bias': (0.0, 0.327)}
    factors = {'L0_gnn_weight': 8.0, 'L0_gnn_bias': 8.0, 'L3_gnn_att_src': 6.286, 'L3_gnn_att_dst': 8.0}
    for name, (base, spread) in spreads.items():
        noise = np.random.default_rng([zlib.crc32(name.encode()), seed]).standard_normal(out[name].shape)
        drawn = base * np.exp(spread * noise) if base else spread * noise
        out[name] = jnp.asarray(drawn.astype(out[name].dtype))
    for name, factor in factors.items():
        out[name] = (out[name] * factor).astype(out[name].dtype)
    return out
```

```python
import concourse.bass as bass
from concourse import mybir
from contextlib import ExitStack

F32, BF16, I32, U8 = mybir.dt.float32, mybir.dt.bfloat16, mybir.dt.int32, mybir.dt.uint8
ALU, ACT, AX = mybir.AluOpType, mybir.ActivationFunctionType, mybir.AxisListType

P, D = 128, 128
N, E = 50000, 25000
TE = 125
T = E // TE
GR = 4
U = 2 * GR
IT = T // U
TG = T // 2
TP = T + U
POS = T * P
NL = 5
HEADS, CH = 4, D // 4
NC_ = N // P
TAIL0 = NC_ * P
TAIL = N - TAIL0
NJ = 13
CHUNKS = NC_ // NJ
GAMA = 0.9
CC = 1.0 / (2.0 + GAMA)
EPS = 1e-5
BIG = 1.0e30


def build(nc, x0, src, dst, ea, ew, w0, b0, w1, b1, gamma, beta, w2, b2, we, be, coef, linw, linb, asrc, adst, out):
    assert T * TE == E and IT * U == T and CHUNKS * NJ == NC_ and CHUNKS % 2 == 0
    ctx = ExitStack()

    def sb(name, shape, dt=F32):
        return ctx.enter_context(nc.sbuf_tensor(name, shape, dt))

    phase = []

    def sem(name):
        phase.append(nc.alloc_semaphore(name=name))
        return phase[-1]

    def end_phase():
        with nc.Block() as block:
            @block.gpsimd
            def _(pool):
                nc.clear_and_free_semaphores(phase)
        phase.clear()

    def sems(name, n):
        return [sem(f"{name}{i}") for i in range(n)]

    def pool_sems(name, n):
        return [ctx.enter_context(nc.semaphore(f"{name}{i}")) for i in range(n)]

    def dram(name, shape, dt=F32):
        return nc.dram_tensor(name, shape, dt).ap()

    with ctx:
        keys_d = dram("keys_d", (T, P), U8)
        agg = dram("agg", (N, D))
        x1 = dram("x1", (N, D))
        x2n = dram("x2n", (N, D + 1))
        x3 = dram("x3", (N, D))
        xt_d = dram("xt_d", (N, D + HEADS))
        ad_d = dram("ad_d", (N, HEADS))
        lastpos = dram("lastpos", (N, 1), I32)
        tabs = [dram(f"tab{i}", (POS, D)) for i in range(3)]

        big = sb("big", [P, T * (D + HEADS)])
        keyrow = sb("keyrow", [P, TP * P], U8)
        ident = sb("ident", [P, P])
        iota_i = sb("iota_i", [P, NC_ + 1], I32)
        iota_f = sb("iota_f", [P, NC_ + 1])
        part_i = sb("part_i", [P, 1], I32)
        part_f = sb("part_f", [P, 1])
        ones = sb("ones", [P, P])
        minus_half = sb("minus_half", [P, NC_ + 1])
        zcol = sb("zcol", [P, P])
        keycol = sb("keycol", [P, TP])
        wcol = sb("wcol", [P, TP])
        wccol = sb("wccol", [P, TP])
        src_i = sb("src_i", [P, TP], I32)
        dst_i = sb("dst_i", [P, TP], I32)
        put_i = sb("put_i", [P, TP], I32)
        gidx = sb("gidx", [P, TP], I32)
        ends = sb("ends", [P, T, 2])
        isnode0 = sb("isnode0", [P, TP])
        issrc0 = sb("issrc0", [P, TP])
        newseg = sb("newseg", [TG, 2, P])
        endrow = sb("endrow", [TG, 2, P])
        deg = sb("deg", [P, 2, NC_ + 1])
        nsrc = sb("nsrc", [P, NC_ + 1])
        rin = sb("rin", [P, NC_ + 1])
        G = sb("G", [P, U, D + HEADS])
        Y = sb("Y", [P, U, D])
        M = sb("M", [P, U, P])
        HR = sb("HR", [P, U, D])
        HT = sb("HT", [P, GR, P])
        OT = sb("OT", [P, GR, P])
        UT = sb("UT", [P, GR, P])
        UO = sb("UO", [P, GR, P])
        ridx = sb("ridx", [P, U], I32)
        sidx = sb("sidx", [P, U], I32)
        wmat = sb("wmat", [P, D])
        wplus = sb("wplus", [P, D])
        bias = sb("bias", [P, D])
        row_a = sb("row_a", [P, D])
        row_b = sb("row_b", [P, D])
        gb = sb("gb", [P, 2, NL])
        col = sb("col", [P, 8])
        scol = sb("scol", [P, 1])
        tcol = sb("tcol", [P, 1])
        mcol = sb("mcol", [P, 1])
        rcol = sb("rcol", [P, 1])
        st6 = sb("st6", [P, NJ, 6])
        mv = sb("mv", [P, 2, NJ, 2])
        rs = sb("rs", [P, 2, NJ])
        nb = sb("nb", [P, 2, NJ])

        PS = ctx.enter_context(nc.psum_tensor("PS", [P, 8, 4, P], F32))
        CAR, SUM, PA, PB, PC, ACC1, ACC2 = 0, 1, 3, 5, 7, 6, 7

        def bank(b, n=512):
            return PS[:, b, :, :].rearrange("p a b -> p (a b)")[:, 0:n]

        def steady(eng, *values):
            for v in values:
                if not isinstance(v, int):
                    eng.lower_val(v)
            eng.wait_ge(s_go, 1)

        chain = {}

        def link(eng, name, ins):
            s, v = chain[name]
            ins.then_inc(s, 1)
            chain[name] = (s, v + 1)
            eng.wait_ge(s, v + 1)

        s_dve, s_go = (ctx.enter_context(nc.semaphore(n)) for n in ("s_dve", "s_go"))
        chain["dve"] = (s_dve, 0)

        DI = big[0:TG, 0:2 * P].bitcast(I32).rearrange("p (g i) -> p g i", g=2)
        SI = big[0:TG, 256:256 + 2 * P].bitcast(I32).rearrange("p (g i) -> p g i", g=2)

        def tview(k):
            return big[0:TG, 512 + 256 * k:768 + 256 * k].rearrange("p (g i) -> p g i", g=2)

        WF, DF, SF, LID, KT, PUT, DGI, SEL, N0, S0, KR = [tview(k) for k in range(11)]
        RT = big[0:TG, 4096:4096 + 64].bitcast(U8).rearrange("p (g i) -> p g i", g=2)
        ZB = big[:, 8192:8192 + NJ * D]
        s_ms, s_ld, s_id, s_tr, s_ky, s_tp, s_zf = (sem(n) for n in ("s_ms", "s_ld", "s_id", "s_tr", "s_ky", "s_tp", "s_zf"))

        with nc.Block() as block:
            @block.sync
            def _(sp):
                sp.wait_ge(s_ms, 3)
                n = 0
                for g in range(2):
                    lo = g * TG * TE
                    for t_, v in ((DI, dst), (SI, src), (WF, ew)):
                        sp.dma_start(t_[:, g, 1:TE + 1],
                                     v[lo:lo + TG * TE].rearrange("(t e) -> t e", e=TE)).then_inc(s_ld, 16)
                        n += 1
                prev = dst[0:E].rearrange("(t e) -> t e", e=TE)
                with nc.allow_non_contiguous_dma(reason="one edge of each tile"):
                    sp.dma_start(DI[1:TG, 0, 0:1], prev[0:TG - 1, TE - 1:TE]).then_inc(s_ld, 16)
                    sp.dma_start(DI[:, 1, 0:1], prev[TG - 1:T - 1, TE - 1:TE]).then_inc(s_ld, 16)
                    sp.dma_start(DI[:, 0, TE + 1:TE + 2], prev[1:TG + 1, 0:1]).then_inc(s_ld, 16)
                    sp.dma_start(DI[0:TG - 1, 1, TE + 1:TE + 2], prev[TG + 1:T, 0:1]).then_inc(s_ld, 16)
                sp.wait_ge(s_ky, 1)
                sp.dma_start(keys_d.rearrange("(g t) i -> t g i", g=2), RT).then_inc(s_tp, 16)
                sp.wait_ge(s_tp, 16)
                flat = keys_d.rearrange("t i -> (t i)")
                sp.dma_start(keyrow[:, 0:T * P], flat.partition_broadcast(P)).then_inc(s_tp, 16)
                sp.dma_start(keyrow[:, T * P:TP * P], flat[0:U * P].partition_broadcast(P)).then_inc(s_tp, 16)
                sp.wait_ge(s_tp, 48)

            @block.scalar
            def _(act):
                act.wait_ge(s_zf, 1)
                av = agg[0:TAIL0, :].rearrange("(p n) f -> p n f", n=NC_)
                zv = ZB.rearrange("p (n f) -> p n f", f=D)
                for c in range(CHUNKS):
                    act.dma_start(av[:, c * NJ:(c + 1) * NJ, :], zv).then_inc(s_zf, 16)
                act.dma_start(agg[TAIL0:N, :], ZB[0:TAIL, 0:D]).then_inc(s_zf, 16)
                act.wait_ge(s_zf, 1 + 16 * (CHUNKS + 1))

            @block.gpsimd
            def _(pool):
                pool.iota(iota_i[:], pattern=[[1, NC_ + 1]], base=0, channel_multiplier=0).then_inc(s_id, 1)
                pool.iota(part_i[:], pattern=[[0, 1]], base=0, channel_multiplier=1).then_inc(s_id, 1)

            @block.vector
            def _(dve):
                nc.vector.memset(ZB, 0.0).then_inc(s_zf, 1)
                nc.vector.memset(DI, -1).then_inc(s_ms, 1)
                nc.vector.memset(SI, 0).then_inc(s_ms, 1)
                nc.vector.memset(WF, 0.0).then_inc(s_ms, 1)
                nc.vector.memset(ones[:], 1.0)
                nc.vector.memset(zcol[:], 0.0)
                nc.vector.memset(minus_half[:], -0.5)
                nc.vector.memset(KT, 255.0)
                nc.vector.memset(KR, 254.0)
                nc.vector.memset(newseg[:], 0.0)
                nc.vector.memset(endrow[:], 0.0)
                nc.vector.memset(S0, 0.0)
                link(dve, "dve", nc.vector.memset(N0, 0.0))
                link(dve, "dve", nc.vector.memset(N0[0:1, 0, P - 1:P], 1.0))
                dve.wait_ge(s_id, 2)
                nc.vector.tensor_copy(iota_f[:], iota_i[:])
                link(dve, "dve", nc.vector.tensor_copy(part_f[:], part_i[:]))
                nc.vector.tensor_scalar(ident[:], iota_f[:, 0:P], part_f[:, 0:1], None, ALU.is_equal)
                dve.wait_ge(s_ld, 16 * 10)
                e = slice(1, TE + 1)
                nc.vector.memset(WF[:, :, 0:1], 1.0)
                nc.vector.tensor_copy(DF, DI)
                link(dve, "dve", nc.vector.tensor_copy(SF, SI))
                for g in range(2):
                    nc.vector.tensor_tensor(newseg[:, g, e], DF[:, g, e], DF[:, g, 0:TE], ALU.not_equal)
                    nc.vector.tensor_tensor(endrow[:, g, e], DF[:, g, e], DF[:, g, 2:TE + 2], ALU.not_equal)
                    nc.vector.tensor_scalar(N0[:, g, e], DF[:, g, e], 0.0, None, ALU.is_equal)
                    nc.vector.tensor_scalar(S0[:, g, e], SF[:, g, e], 0.0, None, ALU.is_equal)
                    nc.vector.tensor_scalar(PUT[:, g, :], DF[:, g, :], float(N), None, ALU.subtract)
                    link(dve, "dve", nc.vector.tensor_scalar(DGI[:, g, :], DF[:, g, :], 0.0, None, ALU.max))
                for g in range(2):
                    link(dve, "dve", nc.vector.tensor_tensor_scan(LID[:, g, 0:TE + 1], ones[0:TG, 0:TE + 1],
                                                                 newseg[:, g, 0:TE + 1], 0.0, ALU.mult, ALU.add))
                    nc.vector.tensor_copy(KT[:, g, 0:TE + 1], LID[:, g, 0:TE + 1])
                    nc.vector.tensor_copy(KR[:, g, 0:1], LID[:, g, TE:TE + 1])
                    nc.vector.tensor_copy(KR[:, g, e], LID[:, g, e])
                    nc.vector.tensor_tensor(SEL[:, g, :], endrow[:, g, :], N0[:, g, :], ALU.mult)
                    link(dve, "dve", nc.vector.tensor_tensor(PUT[:, g, :], PUT[:, g, :], endrow[:, g, :], ALU.mult))
                    link(dve, "dve", nc.vector.tensor_scalar(PUT[:, g, :], PUT[:, g, :], float(N), None, ALU.add))
                nc.vector.tensor_copy(RT, KR).then_inc(s_ky, 1)
                link(dve, "dve", nc.vector.tensor_copy(mv[:, 0, 0, 0:1], ones[:, 0:1]))
                nc.vector.memset(col[:], 0.0).then_inc(s_ky, 1)
                dve.wait_ge(s_tr, 18)
                slots = PS[:].rearrange("p b s c -> p (b s) c")
                outs = [keycol, wcol, src_i, dst_i, put_i, None, None, isnode0, issrc0]
                for k, o in enumerate(outs):
                    v = slots[:, 2 * k:2 * k + 2, 0:TG]
                    if o is None:
                        nc.vector.tensor_copy(ends[:, :, k - 5].rearrange("p (g t) -> p g t", g=2), v)
                    else:
                        nc.vector.tensor_copy(o[:, 0:T].rearrange("p (g t) -> p g t", g=2), v)
                        nc.vector.tensor_copy(o[:, T:TP], slots[:, 2 * k, 0:U])
                link(dve, "dve", nc.vector.tensor_scalar(wccol[:, 0:T].rearrange("p (g t) -> p g t", g=2),
                                                         slots[:, 2:4, 0:TG], CC, None, ALU.mult))
                link(dve, "dve", nc.vector.tensor_copy(wccol[:, T:TP], wccol[:, 0:U]))
                link(dve, "dve", nc.vector.memset(wccol[0:1, :], 1.0))
                nc.vector.memset(PS[:], 0.0).then_inc(s_go, 1)

            @block.tensor
            def _(pe):
                pe.wait_ge(s_ky, 2)
                for k, v in enumerate((KT, WF, SF, DGI, PUT, endrow, SEL, N0, S0)):
                    for g in range(2):
                        nc.tensor.transpose(PS[:, (2 * k + g) // 4, (2 * k + g) % 4, 0:TG], v[:, g, :], ident[0:TG, 0:TG]).then_inc(s_tr, 1)
        end_phase()

        hi = big[:, 0:2 * T].rearrange("p (k t) -> p k t", k=2)
        lo = big[:, 400:400 + 2 * T].rearrange("p (k t) -> p k t", k=2)
        tmp = big[:, 800:800 + 2 * T].rearrange("p (k t) -> p k t", k=2)
        tmp_i = big[:, 1200:1200 + 2 * T].bitcast(I32).rearrange("p (k t) -> p k t", k=2)
        nod = big[:, 1600:1600 + 2 * T].rearrange("p (k t) -> p k t", k=2)
        tail_m = big[:, 2000:2000 + 2 * T].rearrange("p (k t) -> p k t", k=2)
        edge_p = big[:, 2400:2404]
        HA = big[:, 3000:3256].bitcast(BF16).rearrange("p (s i) -> p s i", s=4)
        HB = big[:, 3300:3300 + 4 * 196].bitcast(BF16).rearrange("p (s i) -> p s i", s=4)
        NCOL = NC_ + 1

        s_w, s_tb, s_q = sem("s_w"), sem("s_tb"), sem("s_q")
        a_idx, a_sidx, a_mask, a_row, a_aggT, a_aggC, a_y, a_yc, a_car, a_hot, a_hist = (sem(n) for n in (
            "a_idx", "a_sidx", "a_mask", "a_row", "a_aggT", "a_aggC", "a_y", "a_yc", "a_car", "a_hot", "a_hist"))
        a_got, a_put = pool_sems("a_got", U), pool_sems("a_put", U)

        def edge_mask(t, slot, weights):
            return nc.vector.tensor_scalar(M[:, slot, :], keyrow[:, bass.ds(t * P, P)], keycol[:, bass.ds(t, 1)],
                                           weights[:, bass.ds(t, 1)], ALU.is_equal, ALU.mult)

        with nc.Block() as block:
            @block.sync
            def _(sp):
                sp.dma_start(wmat[:], w0).then_inc(s_w, 16)
                sp.wait_ge(s_w, 16)

            @block.gpsimd
            def _(pool):
                last_node = pool.to_reg(N - 1)
                with pool.Fori(0, IT) as i:
                    for j in range(U):
                        steady(pool, i + 1, 2 * i)
                        if j % GR == 0:
                            pool.wait_ge(a_idx, i + 1)
                            pool.wait_ge(a_yc, 2 * i)
                        pool.indirect_dma_start(G[:, j, 0:D], None, x0, bass.IndirectOffsetOnAxis(
                            ap=ridx[:, j:j + 1], axis=0)).then_inc(a_got[j], 16)
                    for j in range(U):
                        steady(pool, i + 1, 2 * i + j // GR + 1)
                        if j == 0:
                            pool.wait_ge(a_sidx, i + 1)
                        if j % GR == 0:
                            pool.wait_ge(a_yc, 2 * i + j // GR + 1)
                        pool.indirect_dma_start(agg, bass.IndirectOffsetOnAxis(ap=sidx[:, j:j + 1], axis=0),
                                                Y[:, j, :], None, bounds_check=last_node,
                                                oob_is_err=False).then_inc(a_put[j], 16)
                for j in range(U):
                    pool.wait_ge(a_put[j], 16 * IT)

            @block.vector
            def _(dve):
                nc.vector.tensor_copy(nod[:, 0, :], src_i[:, 0:T])
                link(dve, "dve", nc.vector.tensor_copy(nod[:, 1, :], dst_i[:, 0:T]))
                link(dve, "dve", nc.vector.tensor_scalar(tmp, nod, 1.0 / NC_, None, ALU.mult))
                link(dve, "dve", nc.vector.tensor_copy(tmp_i, tmp))
                link(dve, "dve", nc.vector.tensor_copy(hi, tmp_i))
                link(dve, "dve", nc.vector.scalar_tensor_tensor(lo, hi, -float(NC_), nod, ALU.mult, ALU.add))
                for op, lim, sg in ((ALU.is_lt, 0.0, 1.0), (ALU.is_ge, float(NC_), -1.0)):
                    link(dve, "dve", nc.vector.tensor_scalar(tmp, lo, lim, sg, op, ALU.mult))
                    link(dve, "dve", nc.vector.tensor_tensor(hi, hi, tmp, ALU.subtract))
                    link(dve, "dve", nc.vector.scalar_tensor_tensor(lo, tmp, float(NC_), lo, ALU.mult, ALU.add))
                link(dve, "dve", nc.vector.tensor_scalar(tail_m, nod, float(TAIL0), None, ALU.is_ge))
                link(dve, "dve", nc.vector.tensor_scalar(nod, nod, float(TAIL0), None, ALU.subtract))
                link(dve, "dve", nc.vector.tensor_tensor(nod, nod, hi, ALU.subtract))
                link(dve, "dve", nc.vector.tensor_tensor(nod, nod, tail_m, ALU.mult))
                link(dve, "dve", nc.vector.tensor_tensor(hi, hi, nod, ALU.add))
                link(dve, "dve", nc.vector.tensor_scalar(tmp, lo, -1.0, float(NC_), ALU.mult, ALU.add))
                link(dve, "dve", nc.vector.tensor_tensor(tmp, tmp, tail_m, ALU.mult))
                link(dve, "dve", nc.vector.tensor_tensor(lo, lo, tmp, ALU.add))
                link(dve, "dve", nc.vector.tensor_scalar(edge_p[:, 0:1], part_f[:, 0:1], 0.5, None, ALU.is_gt))
                link(dve, "dve", nc.vector.tensor_scalar(edge_p[:, 1:2], part_f[:, 0:1], TE + 0.5, None, ALU.is_lt))
                link(dve, "dve", nc.vector.tensor_tensor(edge_p[:, 0:1], edge_p[:, 0:1], edge_p[:, 1:2], ALU.mult))
                link(dve, "dve", nc.vector.tensor_scalar(edge_p[:, 2:3], edge_p[:, 0:1], 1.0, None, ALU.subtract))
                link(dve, "dve", nc.vector.tensor_scalar(hi, hi, edge_p[:, 0:1], edge_p[:, 2:3], ALU.mult, ALU.add))
                nc.vector.tensor_copy(ridx[:], src_i[:, 0:U]).then_inc(a_idx, 1)
                for j in range(GR):
                    ins = edge_mask(j, j, wcol)
                ins.then_inc(a_mask, 1)
                with dve.Fori(0, IT) as i:
                    for h in range(2):
                        g = 2 * i + h
                        steady(dve, 16 * i, 16 * i + 16)
                        for q in range(GR * h, GR * h + GR):
                            dve.wait_ge(a_got[q], 16 * i + 16)
                        if h == 0:
                            for q in range(U):
                                dve.wait_ge(a_put[q], 16 * i)
                            nc.vector.tensor_copy(sidx[:], put_i[:, bass.ds(U * i, U)]).then_inc(a_sidx, 1)
                        ins = nc.vector.tensor_copy(ridx[:, GR * h:GR * h + GR],
                                                    src_i[:, bass.ds(U * i + U + GR * h, GR)])
                        if h == 1:
                            ins.then_inc(a_idx, 1)
                        for j in range(GR):
                            ins = edge_mask(U * i + GR * (h + 1) + j, GR * (1 - h) + j, wcol)
                        ins.then_inc(a_mask, 1)
                        for j in range(GR * h, GR * h + GR):
                            for k in range(2):
                                s = 2 * (j % 2) + k
                                dve.wait_ge(a_hist, 2 * (U * i + j))
                                nc.vector.tensor_scalar(HA[:, s, :], iota_f[:, 0:P], hi[:, k, bass.ds(U * i + j, 1)],
                                                        None, ALU.is_equal)
                                nc.vector.tensor_scalar(HB[:, s, 0:NCOL], iota_f[:, 0:NCOL],
                                                        lo[:, k, bass.ds(U * i + j, 1)],
                                                        None, ALU.is_equal).then_inc(a_hot, 1)
                        dve.wait_ge(a_y, g + 1)
                        nc.vector.tensor_copy(Y[:, GR * h:GR * h + GR, :], PS[:, SUM + h, :, :]).then_inc(a_yc, 1)
                dve.wait_ge(a_hist, 2 * T + 5)
                nc.vector.tensor_copy(deg[:, 0, :], bank(ACC1, NCOL))
                nc.vector.tensor_copy(deg[:, 1, :], bank(ACC2, NCOL))
                nc.vector.memset(col[:], 0.0).then_inc(s_q, 1)

            @block.scalar
            def _(act):
                with act.Fori(0, IT) as i:
                    for h in range(2):
                        for j in range(GR * h, GR * h + GR):
                            act.wait_ge(a_got[j], 16 * i + 16)
                            act.wait_ge(a_row, U * i + j)
                            nc.scalar.copy(G[0:1, j, 0:D], PS[0:1, CAR, 0, :]).then_inc(a_car, 1)
                        act.wait_ge(a_aggT, 2 * i + h + 1)
                        act.wait_ge(a_y, 2 * i + h)
                        nc.scalar.copy(HT[:], PS[:, PA + h, :, :]).then_inc(a_aggC, 1)

            @block.tensor
            def _(pe):
                accs = [bank(a, NCOL) for a in (ACC1, ACC2)]
                zb = zcol[:].bitcast(BF16)
                zr = zcol[:, 0:1].bitcast(BF16)[:, 0:1]
                for a in accs:
                    nc.tensor.matmul(a, zb[:, 0:P], zr.to_broadcast([P, NCOL]), start=True, stop=False,
                                     skip_group_check=True).then_inc(a_hist, 1)
                pe.wait_ge(s_w, 16)
                with pe.Fori(0, IT) as i:
                    for h in range(2):
                        g = 2 * i + h
                        for j in range(GR * h, GR * h + GR):
                            t = U * i + j
                            if j % GR == 0:
                                pe.wait_ge(a_mask, g + 1)
                            pe.wait_ge(a_car, t + 1)
                            nc.tensor.matmul(PS[0:1, CAR, 0, :], M[:, j, 0:1], G[:, j, 0:D],
                                             start=True, stop=True).then_inc(a_row, 1)
                            ins = nc.tensor.matmul(PS[:, PA + h, j % GR, :], G[:, j, 0:D], M[:, j, :],
                                                   start=True, stop=True)
                            if j % GR == GR - 1:
                                ins.then_inc(a_aggT, 1)
                            for k in range(2):
                                s = 2 * (j % 2) + k
                                pe.wait_ge(a_hot, 2 * t + k + 1)
                                nc.tensor.matmul(accs[k], HA[:, s, :], HB[:, s, 0:NCOL], start=False, stop=False,
                                                 skip_group_check=True).then_inc(a_hist, 1)
                        pe.wait_ge(a_aggC, g + 1)
                        for j in range(GR):
                            ins = nc.tensor.matmul(PS[:, SUM + h, j, :], HT[:, j, :], wmat[:], start=True, stop=True)
                        ins.then_inc(a_y, 1)
                pe.wait_ge(s_w, 16)
                for a in accs:
                    nc.tensor.matmul(a, zb[:, 0:P], zr.to_broadcast([P, NCOL]), start=False, stop=True,
                                     skip_group_check=True).then_inc(a_hist, 1)
                nc.tensor.matmul(PS[0:1, CAR, 0, 0:1], ones[:, 0:1], ones[:, 0:1], start=True, stop=True).then_inc(a_hist, 1)
        end_phase()

        cum = big[:, 0:NCOL]
        has = big[:, 400:400 + NCOL]
        qf = big[:, 800:800 + NCOL]
        qi = big[:, 1200:1200 + NCOL].bitcast(I32)
        rest = big[:, 1600:1600 + NCOL]
        lp_i = big[:, 2000:2000 + NCOL].bitcast(I32)
        before = big[:, 2400:2400 + P]
        upto = big[:, 2600:2600 + P]
        s_rows, s_pre, s_lp, s_lps, s_ns = (sem(n) for n in ("s_rows", "s_pre", "s_lp", "s_lps", "s_ns"))
        EMPTY = TE + 1

        with nc.Block() as block:
            @block.vector
            def _(dve):
                nc.vector.tensor_scalar(nsrc[:], deg[:, 0, :], 1.0, None, ALU.max).then_inc(s_ns, 1)
                link(dve, "dve", nc.vector.tensor_scalar(rin[:], deg[:, 1, :], 1.0, None, ALU.add))
                nc.vector.reciprocal(rin[:], rin[:])
                nc.vector.tensor_reduce(col[:, 0:1], deg[:, 1, 0:NC_], AX.X, ALU.add)
                nc.vector.tensor_scalar(before, iota_f[:, 0:P], part_f[:, 0:1], None, ALU.is_gt)
                nc.vector.tensor_scalar(upto, iota_f[:, 0:P], part_f[:, 0:1], None, ALU.is_ge).then_inc(s_rows, 1)
                dve.wait_ge(s_pre, 1)
                link(dve, "dve", nc.vector.tensor_copy(col[:, 1:3], PS[:, 0, 0, 0:2]))
                nc.vector.tensor_scalar(qf, iota_f[:, 0:NCOL], 0.0, 1.0, ALU.mult, ALU.add)
                link(dve, "dve", nc.vector.tensor_copy(cum[:, NC_:NCOL], col[:, 2:3]))
                link(dve, "dve", nc.vector.tensor_tensor_scan(cum[:, 0:NC_], qf[:, 0:NC_], deg[:, 1, 0:NC_],
                                                             col[:, 1:2], ALU.mult, ALU.add))
                link(dve, "dve", nc.vector.tensor_scalar(cum, cum, 1.0, None, ALU.subtract))
                link(dve, "dve", nc.vector.tensor_scalar(qf, cum, 1.0 / TE, None, ALU.mult))
                link(dve, "dve", nc.vector.tensor_copy(qi, qf))
                link(dve, "dve", nc.vector.tensor_copy(qf, qi))
                link(dve, "dve", nc.vector.scalar_tensor_tensor(rest, qf, -float(TE), cum, ALU.mult, ALU.add))
                link(dve, "dve", nc.vector.tensor_scalar(has, rest, 0.0, None, ALU.is_lt))
                link(dve, "dve", nc.vector.tensor_tensor(qf, qf, has, ALU.subtract))
                link(dve, "dve", nc.vector.tensor_scalar(has, rest, float(TE), None, ALU.is_ge))
                link(dve, "dve", nc.vector.tensor_tensor(qf, qf, has, ALU.add))
                link(dve, "dve", nc.vector.scalar_tensor_tensor(cum, qf, float(P - TE), cum, ALU.mult, ALU.add))
                link(dve, "dve", nc.vector.tensor_scalar(has, deg[:, 1, :], 0.5, None, ALU.is_gt))
                link(dve, "dve", nc.vector.tensor_scalar(cum, cum, 1.0 - EMPTY, None, ALU.add))
                link(dve, "dve", nc.vector.tensor_tensor(cum, cum, has, ALU.mult))
                link(dve, "dve", nc.vector.tensor_scalar(cum, cum, float(EMPTY), None, ALU.add))
                link(dve, "dve", nc.vector.tensor_tensor(cum[0:1, 0:1], cum[0:1, 0:1], has[0:1, 0:1], ALU.subtract))
                link(dve, "dve", nc.vector.tensor_scalar(cum[0:1, 0:1], cum[0:1, 0:1], 1.0, None, ALU.add))
                nc.vector.tensor_copy(lp_i, cum).then_inc(s_lp, 1)

            @block.tensor
            def _(pe):
                pe.wait_ge(s_rows, 1)
                nc.tensor.matmul(PS[:, 0, 0, 0:1], before, col[:, 0:1], start=True, stop=True)
                nc.tensor.matmul(PS[:, 0, 0, 1:2], upto, deg[:, 1, NC_:NCOL], start=True, stop=False)
                nc.tensor.matmul(PS[:, 0, 0, 1:2], ones[:], col[:, 0:1], start=False, stop=True).then_inc(s_pre, 1)

            @block.gpsimd
            def _(pool):
                pool.wait_ge(s_ns, 1)
                nc.gpsimd.tensor_tensor(nsrc[:], nsrc[:], minus_half[:], ALU.pow).then_inc(s_ns, 1)

            @block.sync
            def _(sp):
                sp.wait_ge(s_lp, 1)
                with nc.allow_non_contiguous_dma(reason="the tail's column"):
                    sp.dma_start(lastpos[0:TAIL0, :].rearrange("(p n) o -> p (n o)", n=NC_),
                                 lp_i[:, 0:NC_]).then_inc(s_lps, 16)
                    sp.dma_start(lastpos[TAIL0:N, :], lp_i[0:TAIL, NC_:NCOL]).then_inc(s_lps, 16)
                sp.wait_ge(s_lps, 32)
        g_id, g_cp = sem("g_id"), sem("g_cp")
        g_got = pool_sems("g_got", U)

        with nc.Block() as block:
            @block.gpsimd
            def _(pool):
                with pool.Fori(0, IT) as i:
                    steady(pool, i)
                    pool.wait_ge(g_cp, i)
                    nc.gpsimd.tensor_copy(ridx[:], src_i[:, bass.ds(U * i, U)]).then_inc(g_id, 1)
                    for j in range(U):
                        steady(pool, i + 1)
                        if j == 0:
                            pool.wait_ge(g_id, i + 1)
                        pool.indirect_dma_start(sidx[:, j:j + 1], None, lastpos, bass.IndirectOffsetOnAxis(
                            ap=ridx[:, j:j + 1], axis=0)).then_inc(g_got[j], 16)
                    steady(pool, 16 * i + 16)
                    for j in range(U):
                        pool.wait_ge(g_got[j], 16 * i + 16)
                    nc.gpsimd.tensor_copy(gidx[:, bass.ds(U * i, U)], sidx[:]).then_inc(g_cp, 1)
                pool.wait_ge(g_cp, IT)
                nc.gpsimd.tensor_copy(gidx[:, T:TP], gidx[:, 0:U]).then_inc(g_cp, 1)

        end_phase()

        def chunk(t, c, w):
            if c is None:
                return t[TAIL0:N, 0:w].unsqueeze(1)
            return t[0:TAIL0, :].rearrange("(p n) f -> p n f", n=NC_)[:, bass.ds(c * NJ, NJ), 0:w]

        def size(c):
            return (TAIL, 1) if c is None else (P, NJ)

        def columns(table, c):
            return table[0:TAIL, NC_:NCOL] if c is None else table[:, bass.ds(c * NJ, NJ)]

        def chunks(eng):
            with eng.Fori(0, CHUNKS // 2) as i:
                for s in range(2):
                    yield 2 * i + s, s, i
            yield None, 0, CHUNKS // 2

        def areas(widths, at=0):
            got = []
            for w in widths:
                got.append([big[:, at + s * NJ * w:at + (s + 1) * NJ * w].rearrange("p (n f) -> p n f", f=w)
                            for s in range(2)])
                at += 2 * NJ * w
            return got

        def ln_stats(dve, V, c, s, n, st):
            np_, nj = size(c)
            for j in range(nj):
                ins = nc.vector.bn_stats(st6[0:np_, j, :], V[0:np_, j, :])
            ins.then_inc(st[s], 1)
            steady(dve, 2 * n + 1)
            dve.wait_ge(st[s], 2 * n + 1)
            for j in range(nj):
                ins = nc.vector.bn_aggr(mv[0:np_, s, j, :], st6[0:np_, j, :])
            ins.then_inc(st[s], 1)

        def ln_scale(pool, c, s, n, st, ps, ready):
            np_, nj = size(c)
            steady(pool, 2 * n + 2)
            pool.wait_ge(st[s], 2 * n + 2)
            nc.gpsimd.tensor_scalar(rs[0:np_, s, 0:nj], mv[0:np_, s, 0:nj, 1], EPS, None, ALU.add)
            nc.gpsimd.tensor_scalar(nb[0:np_, s, 0:nj], mv[0:np_, s, 0:nj, 0], -1.0, None, ALU.mult).then_inc(ps[s], 1)
            pool.wait_ge(ps[s], 2 * n + 1)
            nc.gpsimd.tensor_tensor(rs[0:np_, s, 0:nj], rs[0:np_, s, 0:nj], minus_half[0:np_, 0:nj],
                                    ALU.pow).then_inc(ps[s], 1)
            pool.wait_ge(ps[s], 2 * n + 2)
            nc.gpsimd.tensor_tensor(nb[0:np_, s, 0:nj], nb[0:np_, s, 0:nj], rs[0:np_, s, 0:nj],
                                    ALU.mult).then_inc(ready[s], 1)

        def ln_apply(act, V, X, c, s, n, ready, stored, done):
            np_, nj = size(c)
            steady(act, n + 1, 16 * n)
            act.wait_ge(ready[s], n + 1)
            act.wait_ge(stored[s], 16 * n)
            for j in range(nj):
                ins = nc.scalar.activation(X[0:np_, j, 0:D], V[0:np_, j, :], ACT.Identity,
                                           scale=rs[0:np_, s, j:j + 1], bias=nb[0:np_, s, j:j + 1])
            ins.then_inc(done[s], 1)

        def norm_pass(tag, loads, V, X, xw, into, make_v, extra_x=None, pe_part=None, prelude=None):
            ld, vr, rdy, done, stored, st, xtra, used, ps = (sems(tag + n, 2) for n in (
                "_ld", "_v", "_rdy", "_x", "_st", "_s", "_xt", "_us", "_ps"))
            pre = sem(tag + "_pre")
            with nc.Block() as block:
                @block.sync
                def _(sp):
                    if prelude:
                        prelude[0](sp, pre)
                    for c, s, n in chunks(sp):
                        np_, nj = size(c)
                        sp.wait_ge(vr[s], n)
                        for buf, t, w in loads:
                            sp.dma_start(buf[s][0:np_, 0:nj, :], chunk(t, c, w)).then_inc(ld[s], 16)

                @block.vector
                def _(dve):
                    if prelude:
                        dve.wait_ge(pre, prelude[1])
                    for c, s, n in chunks(dve):
                        steady(dve, 16 * len(loads) * (n + 1), n)
                        dve.wait_ge(ld[s], 16 * len(loads) * (n + 1))
                        dve.wait_ge(done[s], n)
                        make_v(dve, c, s, n, used, vr)
                        dve.wait_ge(vr[s], n + 1)
                        ln_stats(dve, V[s], c, s, n, st)

                @block.scalar
                def _(act):
                    for c, s, n in chunks(act):
                        np_, nj = size(c)
                        if pe_part:
                            act.wait_ge(used[s], n)
                        ln_apply(act, V[s], X[s], c, s, n, rdy, stored, done)
                        if extra_x:
                            extra_x(act, c, s, n, xtra)
                            act.wait_ge(xtra[s], n + 1)
                        act.wait_ge(done[s], n + 1)
                        act.dma_start(chunk(into, c, xw), X[s][0:np_, 0:nj, 0:xw]).then_inc(stored[s], 16)
                    act.wait_ge(stored[0], 16 * (CHUNKS // 2 + 1))
                    act.wait_ge(stored[1], 16 * (CHUNKS // 2))

                if pe_part:
                    @block.tensor
                    def _(pe):
                        pe_part(pe, done, used)
                @block.gpsimd
                def _(pool):
                    for c, s, n in chunks(pool):
                        ln_scale(pool, c, s, n, st, ps, rdy)

        def wide(c_bias, np_, nj):
            return c_bias[0:np_, 0:D].unsqueeze(1).to_broadcast([np_, nj, D])

        XA, YA, XN, V = areas([D, D, D, D])
        m_sum = sem("m_sum")
        a_rel = sems("a_rel", 2)

        def load_bias0(sp, pre):
            sp.dma_start(bias[:], b0.partition_broadcast(P)).then_inc(pre, 16)

        def make_x1(dve, c, s, n, used, vr):
            np_, nj = size(c)
            y, x = YA[s][0:np_, 0:nj, :], XA[s][0:np_, 0:nj, :]
            nc.vector.tensor_tensor(y, y, wide(bias, np_, nj), ALU.add).then_inc(a_rel[s], 1)
            dve.wait_ge(a_rel[s], n + 1)
            nc.vector.scalar_tensor_tensor(V[s][0:np_, 0:nj, :], y, 0.0, x, ALU.max, ALU.add).then_inc(vr[s], 1)

        def sum_nodes(pe, done, used):
            nc.tensor.matmul(PS[:, ACC1, 0, 0:1], zcol[:], ones[:, 0:1], start=True, stop=False,
                             skip_group_check=True).then_inc(m_sum, 1)
            for c, s, n in chunks(pe):
                np_, nj = size(c)
                pe.wait_ge(done[s], n + 1)
                for j in range(nj):
                    ins = nc.tensor.matmul(PS[:, ACC1, 0, 0:1], XN[s][0:np_, j, :], ones[0:np_, 0:1], start=False,
                                           stop=False, skip_group_check=True)
                ins.then_inc(used[s], 1)
            nc.tensor.matmul(PS[:, ACC1, 0, 0:1], zcol[:], ones[:, 0:1], start=False, stop=True,
                             skip_group_check=True).then_inc(m_sum, 1)

        norm_pass("A", [(XA, x0, D), (YA, agg, D)], V, XN, D, x1, make_x1, pe_part=sum_nodes,
                  prelude=(load_bias0, 16))
        end_phase()

        zt = big[:, 0:T * D]
        SQ = big[:, T * D:T * D + GR * D].rearrange("p (s f) -> p s f", f=D)
        l_w, l_wr, l_col, l_base, l_idx, l_mask, l_car, l_row, l_sum, l_ev, l_hg, l_ht, l_ot, l_uo, l_ut, l_g, l_gc, l_z, l_zc, l_xt, l_xc, l_sq, l_stat = (
            sem("l_" + n) for n in "w wr col base idx mask car row sum ev hg ht ot uo ut g gc z zc xt xc sq stat".split())
        l_got = pool_sems("l_got", U)
        l_tab = sems("l_tab", 2)

        def tab_in(k):
            return tabs[2] if k == 0 else tabs[(k + 1) % 2]

        def tab_out(k):
            return tabs[2] if k == NL - 1 else tabs[k % 2]

        def rounds(l, k):
            return (l * NL + k) * IT, (l * NL + k - 1) * IT

        def is_start(l, k):
            return k == 0 and isinstance(l, int)

        def group_of(ring, h):
            return ring[:, GR * h:GR * h + GR, :]

        def zt_group(i, h):
            return zt[:, bass.ds((U * i + GR * h) * D, GR * D)].rearrange("p (s f) -> p s f", f=D)

        def l1_store(sp, l, k):
            r0, _ = rounds(l, k)
            with sp.Fori(0, IT) as i:
                for h in range(2):
                    sp.wait_ge(l_ev, 2 * (r0 + i) + h + 1)
                    sp.dma_start(tab_out(k)[bass.ds((U * i + GR * h) * P, GR * P), :]
                                 .rearrange("(j p) f -> p j f", p=P), group_of(Y, h)).then_inc(l_tab[h], 16)

        def l1_gather(pool, l, k):
            r0, q0 = rounds(l, k)
            steady(pool, 16 * r0)
            for h in range(2):
                pool.wait_ge(l_tab[h], 16 * r0)
            with pool.Fori(0, IT) as i:
                for j in range(U):
                    g = 2 * (r0 + i) + j // GR
                    steady(pool, 2 * (q0 + i) + j // GR + 1, g - 1)
                    if j % GR == 0:
                        pool.wait_ge(l_idx, 2 * (q0 + i) + j // GR + 1)
                        pool.wait_ge(l_sum, g - 1)
                    pool.indirect_dma_start(G[:, j, 0:D], None, tab_in(k), bass.IndirectOffsetOnAxis(
                        ap=ridx[:, j:j + 1], axis=0)).then_inc(l_got[j], 16)

        def l1_dve(dve, l, k):
            r0, q0 = rounds(l, k)
            first, last, start = k == 0, k == NL - 1, is_start(l, k)
            if start:
                nc.vector.tensor_copy(ridx[:], gidx[:, 0:U]).then_inc(l_idx, 2)
                for j in range(GR):
                    ins = edge_mask(j, j, wccol)
                ins.then_inc(l_mask, 1)
            with dve.Fori(0, IT) as i:
                for h in range(2):
                    g = 2 * (r0 + i) + h
                    gl = 2 * (IT * l + i) + h
                    if start:
                        for j in range(GR * h, GR * h + GR):
                            ins = nc.vector.scalar_tensor_tensor(HR[:, j, :], row_b[:],
                                                                 issrc0[:, bass.ds(U * i + j, 1)],
                                                                 bias[:], ALU.mult, ALU.add)
                        ins.then_inc(l_gc, 1)
                        for j in range(GR * h, GR * h + GR):
                            ins = nc.vector.scalar_tensor_tensor(zt[:, bass.ds((U * i + j) * D, D)], row_a[:],
                                                                 isnode0[:, bass.ds(U * i + j, 1)],
                                                                 bias[:], ALU.mult, ALU.add)
                        ins.then_inc(l_zc, 1)
                    else:
                        steady(dve, 16 * (q0 + i) + 16)
                        for j in range(GR * h, GR * h + GR):
                            dve.wait_ge(l_got[j], 16 * (q0 + i) + 16)
                        nc.vector.tensor_copy(ridx[:, GR * h:GR * h + GR],
                                              gidx[:, bass.ds(U * i + U + GR * h, GR)]).then_inc(l_idx, 1)
                    for j in range(GR):
                        ins = edge_mask(U * i + GR * (h + 1) + j, GR * (1 - h) + j, wccol)
                    ins.then_inc(l_mask, 1)
                    if first and not start:
                        gn = 2 * (IT * (l - 1) + i) + h
                        for u, o, made, used, now in ((UO, OT, l_uo, l_z, l_ot), (UT, HT, l_ut, l_g, l_ht)):
                            dve.wait_ge(made, gn + 1)
                            dve.wait_ge(used, gn)
                            nc.vector.scalar_tensor_tensor(o[:], u[:], 0.01, u[:], ALU.mult, ALU.max).then_inc(now, 1)
                        dve.wait_ge(l_z, 2 * (IT * (l - 1) + i) + h + 1)
                        nc.vector.tensor_tensor(zt_group(i, h), PS[:, PC, :, :], wide(bias, P, GR),
                                                ALU.add).then_inc(l_zc, 1)
                        dve.wait_ge(l_g, 2 * (IT * (l - 1) + i) + h + 1)
                        nc.vector.tensor_tensor(group_of(HR, h), PS[:, PB, :, :], wide(bias, P, GR),
                                                ALU.add).then_inc(l_gc, 1)
                    dve.wait_ge(l_tab[h], 16 * (r0 + i))
                    if first:
                        dve.wait_ge(l_zc, gl + 1)
                    dve.wait_ge(l_sum, g + 1)
                    if last:
                        nc.vector.tensor_copy(group_of(Y, h), PS[:, SUM + h, :, :]).then_inc(l_ev, 1)
                        dve.wait_ge(l_ev, g + 1)
                        nc.vector.tensor_tensor(SQ, group_of(Y, h), group_of(Y, h), ALU.mult).then_inc(l_sq, 1)
                    else:
                        nc.vector.tensor_tensor(group_of(Y, h), PS[:, SUM + h, :, :], zt_group(i, h),
                                                ALU.add).then_inc(l_ev, 1)

        def l1_act(act, l, k):
            r0, q0 = rounds(l, k)
            first, last, start = k == 0, k == NL - 1, is_start(l, k)
            with act.Fori(0, IT) as i:
                for h in range(2):
                    if first and not start:
                        gn = 2 * (IT * (l - 1) + i) + h
                        steady(act, gn)
                        act.wait_ge(l_ot, gn)
                        nc.scalar.activation(UO[:], zt_group(i, h), ACT.Identity, scale=scol[:, 0:1],
                                             bias=tcol[:, 0:1]).then_inc(l_uo, 1)
                        act.wait_ge(l_hg, gn + 1)
                        act.wait_ge(l_ht, gn)
                        nc.scalar.activation(UT[:], PS[:, PA, :, :], ACT.Identity, scale=scol[:, 0:1],
                                             bias=tcol[:, 0:1]).then_inc(l_ut, 1)
                    for j in range(GR * h, GR * h + GR):
                        if first:
                            if j % GR == 0:
                                act.wait_ge(l_gc, 2 * (IT * l + i) + h + 1)
                            into = HR[0:1, j, :]
                        else:
                            act.wait_ge(l_got[j], 16 * (q0 + i) + 16)
                            into = G[0:1, j, 0:D]
                        act.wait_ge(l_row, U * (r0 + i) + j)
                        nc.scalar.copy(into, PS[0:1, CAR, 0, :]).then_inc(l_car, 1)
                    if last:
                        steady(act, 2 * (IT * l + i) + h + 1)
                        act.wait_ge(l_xt, 2 * (IT * l + i) + h + 1)
                        nc.scalar.copy(zt_group(i, h), PS[:, PA + h, :, :]).then_inc(l_xc, 1)

        def l1_pe(pe, l, k):
            r0, q0 = rounds(l, k)
            first, last, start = k == 0, k == NL - 1, is_start(l, k)
            with pe.Fori(0, IT) as i:
                for h in range(2):
                    g = 2 * (r0 + i) + h
                    gl = 2 * (IT * l + i) + h
                    js = range(GR * h, GR * h + GR)
                    if first and not start:
                        gn = 2 * (IT * (l - 1) + i) + h
                        for j in js:
                            pe.wait_ge(l_got[j], 16 * (q0 + i) + 16)
                            ins = nc.tensor.transpose(PS[:, PA, j % GR, :], G[:, j, 0:D], ident[:])
                        ins.then_inc(l_hg, 1)
                        pe.wait_ge(l_ot, gn + 1)
                        pe.wait_ge(l_zc, gl)
                        for j in range(GR):
                            ins = nc.tensor.matmul(PS[:, PC, j, :], OT[:, j, :], wmat[:], start=True, stop=True)
                        ins.then_inc(l_z, 1)
                        pe.wait_ge(l_ht, gn + 1)
                        for j in range(GR):
                            ins = nc.tensor.matmul(PS[:, PB, j, :], HT[:, j, :], wplus[:], start=True, stop=True)
                        ins.then_inc(l_g, 1)
                    for j in js:
                        rows = HR[:, j, :] if first else G[:, j, 0:D]
                        if j % GR == 0:
                            pe.wait_ge(l_mask, g + 1)
                            pe.wait_ge(l_ev, g - 1 if not start else 2 * i)
                            if last:
                                pe.wait_ge(l_xc, gl - 1 if not isinstance(l, int) else 2 * i)
                        pe.wait_ge(l_car, U * (r0 + i) + j + 1)
                        nc.tensor.matmul(PS[0:1, CAR, 0, :], M[:, j, 0:1], rows,
                                         start=True, stop=True).then_inc(l_row, 1)
                        if last:
                            ins = nc.tensor.matmul(PS[:, PA + h, j % GR, :], rows, M[:, j, :], start=True, stop=True)
                            if j % GR == GR - 1:
                                ins.then_inc(l_xt, 1)
                        ins = nc.tensor.matmul(PS[:, SUM + h, j % GR, :], M[:, j, :], rows, start=True, stop=True)
                        if j % GR == GR - 1:
                            ins.then_inc(l_sum, 1)
                    if last:
                        pe.wait_ge(l_sq, gl + 1)
                        for j in js:
                            here = ends[:, bass.ds(U * i + j, 1), :].rearrange("p a b -> p (a b)")
                            nc.tensor.matmul(PS[:, ACC1, 0, 0:2], Y[:, j, :], here, start=False, stop=False,
                                             skip_group_check=True)
                            ins = nc.tensor.matmul(PS[:, ACC2, 0, 0:2], SQ[:, j % GR, :], here, start=False, stop=False,
                                                   skip_group_check=True)
                        ins.then_inc(l_stat, 1)

        l_acc, l_m = sem("l_acc"), sem("l_m")
        NCOEF = 7
        l_pw = sem("l_pw")

        def inverse_deviation(pool, l):
            steady(pool, NCOEF * (l - 1) + 4)
            pool.wait_ge(l_col, NCOEF * (l - 1) + 4)
            nc.gpsimd.tensor_tensor(col[:, 3:4], col[:, 1:2], minus_half[:, 0:1], ALU.pow).then_inc(l_pw, 1)


        def coefficients(dve, l):
            v = NCOEF * (l - 1)
            dve.wait_ge(l_acc, 4 * (l - 1) + 4)
            nc.vector.tensor_scalar(col[:, 0:1], PS[:, ACC1, 0, 0:1], 1.0 / N, None, ALU.mult)
            nc.vector.tensor_copy(rcol[:], PS[:, ACC1, 0, 1:2])
            nc.vector.tensor_scalar(col[:, 1:2], PS[:, ACC2, 0, 0:1], 1.0 / N, None, ALU.mult).then_inc(l_col, 1)
            dve.wait_ge(l_col, v + 1)
            nc.vector.tensor_tensor(col[:, 2:3], col[:, 0:1], col[:, 0:1], ALU.mult).then_inc(l_col, 1)
            dve.wait_ge(l_col, v + 2)
            nc.vector.tensor_tensor(col[:, 1:2], col[:, 1:2], col[:, 2:3], ALU.subtract).then_inc(l_col, 1)
            dve.wait_ge(l_col, v + 3)
            nc.vector.tensor_scalar(col[:, 1:2], col[:, 1:2], EPS, None, ALU.add).then_inc(l_col, 1)
            dve.wait_ge(l_pw, l)
            nc.vector.tensor_tensor(scol[:], col[:, 3:4], gb[:, 0, bass.ds(l - 1, 1)], ALU.mult).then_inc(l_col, 1)
            dve.wait_ge(l_col, v + 5)
            nc.vector.tensor_tensor(col[:, 2:3], col[:, 0:1], scol[:], ALU.mult).then_inc(l_col, 1)
            dve.wait_ge(l_col, v + 6)
            nc.vector.tensor_tensor(tcol[:], gb[:, 1, bass.ds(l - 1, 1)], col[:, 2:3], ALU.subtract).then_inc(l_col, 1)
            dve.wait_ge(l_col, v + 7)

        def over_layers(eng, program):
            program(0)
            with eng.Fori(1, NL) as l:
                program(l)

        s_gb, l_rb, l_fin = sem("s_gb"), sem("l_rb"), sem("l_fin")
        with nc.Block() as block:
            @block.sync
            def _(sp):
                with nc.allow_non_contiguous_dma(reason="ten short columns"):
                    sp.dma_start(gb[:, 0, :], gamma.rearrange("l f -> f l")).then_inc(s_gb, 16)
                    sp.dma_start(gb[:, 1, :], beta.rearrange("l f -> f l")).then_inc(s_gb, 16)

                def layer(l):
                    if isinstance(l, int):
                        wl, bl = w1[l], b1[l]
                    else:
                        wl = w1.rearrange("l i o -> (l i) o")[bass.ds(l * D, D), :]
                        bl = b1[bass.ds(l, 1), :].rearrange("a f -> (a f)")
                    sp.wait_ge(l_ev, 2 * NL * IT * l)
                    sp.dma_start(wmat[:], wl).then_inc(l_w, 16)
                    sp.dma_start(bias[:], bl.partition_broadcast(P)).then_inc(l_w, 16)
                    for k in range(NL):
                        l1_store(sp, l, k)
                over_layers(sp, layer)
                for h in range(2):
                    sp.wait_ge(l_tab[h], 16 * NL * NL * IT)

            @block.gpsimd
            def _(pool):
                def layer(l):
                    if not isinstance(l, int):
                        inverse_deviation(pool, l)
                    for k in range(1 if isinstance(l, int) else 0, NL):
                        l1_gather(pool, l, k)
                over_layers(pool, layer)
                inverse_deviation(pool, NL)

            @block.vector
            def _(dve):
                dve.wait_ge(s_gb, 32)

                def layer(l):
                    if isinstance(l, int):
                        link(dve, "dve", nc.vector.tensor_scalar(mcol[:], PS[:, ACC1, 0, 0:1], 1.0 / N, None, ALU.mult))
                        nc.vector.tensor_scalar(HT[:, 0, :], ones[:], mcol[:, 0:1], None, ALU.mult).then_inc(l_base, 1)
                        dve.wait_ge(l_w, 32)
                        nc.vector.tensor_tensor(wplus[:], wmat[:], ident[:], ALU.add).then_inc(l_wr, 1)
                        dve.wait_ge(l_m, 2)
                        nc.vector.tensor_copy(row_a[:], PS[:, PB, 0, :])
                        link(dve, "dve", nc.vector.tensor_copy(row_b[:], PS[:, PB, 1, :]))
                    else:
                        coefficients(dve, l)
                        dve.wait_ge(l_w, 32 * l + 32)
                        nc.vector.tensor_tensor(wplus[:], wmat[:], ident[:], ALU.add).then_inc(l_wr, 1)
                    for k in range(NL):
                        l1_dve(dve, l, k)
                over_layers(dve, layer)
                coefficients(dve, NL)
                link(dve, "dve", nc.vector.tensor_tensor(col[:, 4:5], rcol[:], scol[:], ALU.mult))
                link(dve, "dve", nc.vector.tensor_tensor(col[:, 4:5], col[:, 4:5], tcol[:], ALU.add))
                link(dve, "dve", nc.vector.tensor_scalar(col[:, 5:6], col[:, 4:5], 0.01, None, ALU.mult))
                link(dve, "dve", nc.vector.tensor_tensor(col[:, 4:5], col[:, 4:5], col[:, 5:6], ALU.max))
                nc.vector.tensor_scalar(HT[:, 0, :], ones[:], col[:, 4:5], None, ALU.mult).then_inc(l_rb, 1)
                dve.wait_ge(l_fin, 1)
                nc.vector.tensor_copy(row_a[:], PS[:, PB, 0, :])

            @block.scalar
            def _(act):
                def layer(l):
                    if not isinstance(l, int):
                        steady(act, NCOEF * l)
                        act.wait_ge(l_col, NCOEF * l)
                    for k in range(NL):
                        l1_act(act, l, k)
                over_layers(act, layer)

            @block.tensor
            def _(pe):
                def layer(l):
                    if isinstance(l, int):
                        pe.wait_ge(l_wr, 1)
                        pe.wait_ge(l_base, 1)
                        nc.tensor.matmul(PS[:, PB, 0, :], HT[:, 0, :], wmat[:], start=True, stop=True).then_inc(l_m, 1)
                        nc.tensor.matmul(PS[:, PB, 1, :], HT[:, 0, :], wplus[:], start=True,
                                         stop=True).then_inc(l_m, 1)
                    else:
                        steady(pe, l + 1)
                        pe.wait_ge(l_wr, l + 1)
                    for k in range(NL):
                        if k == NL - 1:
                            for a in (ACC1, ACC2):
                                nc.tensor.matmul(PS[:, a, 0, 0:2], zcol[:], ones[:, 0:2], start=True, stop=False,
                                                 skip_group_check=True).then_inc(l_acc, 1)
                        l1_pe(pe, l, k)
                    for a in (ACC1, ACC2):
                        nc.tensor.matmul(PS[:, a, 0, 0:2], zcol[:], ones[:, 0:2], start=False, stop=True,
                                         skip_group_check=True).then_inc(l_acc, 1)
                over_layers(pe, layer)
                pe.wait_ge(l_rb, 1)
                nc.tensor.matmul(PS[:, PB, 0, :], HT[:, 0, :], ident[:], start=True, stop=True).then_inc(l_fin, 1)
        end_phase()

        XB, VB, X2 = areas([D, D, D + 1])

        def make_x2(dve, c, s, n, used, vr):
            np_, nj = size(c)
            x = XB[s][0:np_, 0:nj, :]
            nc.vector.tensor_tensor(VB[s][0:np_, 0:nj, :], x, wide(row_a, np_, nj), ALU.add).then_inc(vr[s], 1)

        def norm_column(act, c, s, n, xtra):
            np_, nj = size(c)
            steady(act)
            nc.scalar.copy(X2[s][0:np_, 0:nj, D], columns(nsrc, c)).then_inc(xtra[s], 1)

        norm_pass("B", [(XB, x1, D)], VB, X2, D + 1, x2n, make_x2, extra_x=norm_column)
        end_phase()

        CW = 2 * D + 1
        CMB = big[:, 0:U * CW].rearrange("p (s f) -> p s f", f=CW)
        at = U * CW
        AT, ET, T1, T2 = (big[:, at + 512 * k:at + 512 * k + 512].rearrange("p (s f) -> p s f", f=D) for k in range(4))
        at += 2048
        W2, WE, B2, BE = (big[:, at + D * k:at + D * k + D] for k in range(4))
        cnt, root, inv = (big[:, at + 512 + 16 * k:at + 520 + 16 * k] for k in range(3))
        c_w, c_one, c_idx, c_sidx, c_mask, c_gs, c_car, c_row, c_sum, c_evac, c_cnt, c_root, c_inv, c_wm, c_t, c_y = (
            sem("c_" + n) for n in "w one idx sidx mask gs car row sum evac cnt root inv wm t y".split())
        c_got, c_put, c_ea = pool_sems("c_got", U), pool_sems("c_put", U), sems("c_ea", 2)

        def plain_mask(t, slot):
            return nc.vector.tensor_scalar(M[:, slot, :], keyrow[:, bass.ds(t * P, P)], keycol[:, bass.ds(t, 1)],
                                           None, ALU.is_equal)

        with nc.Block() as block:
            @block.sync
            def _(sp):
                sp.dma_start(W2, w2).then_inc(c_w, 16)
                sp.dma_start(WE, we).then_inc(c_w, 16)
                sp.dma_start(BE, be.partition_broadcast(P)).then_inc(c_w, 16)
                sp.wait_ge(c_one, 1)
                with sp.Fori(0, IT) as i:
                    for h in range(2):
                        sp.wait_ge(c_sum, 2 * i + h)
                        sp.dma_start(CMB[1:TE + 1, GR * h:GR * h + GR, D:2 * D],
                                     ea[bass.ds((U * i + GR * h) * TE, GR * TE), :]
                                     .rearrange("(j p) f -> p j f", p=TE)).then_inc(c_ea[h], 16)

            @block.gpsimd
            def _(pool):
                last_node = pool.to_reg(N - 1)
                with pool.Fori(0, IT) as i:
                    for j in range(U):
                        steady(pool, i + 1, 2 * i)
                        if j % GR == 0:
                            pool.wait_ge(c_idx, i + 1)
                            pool.wait_ge(c_gs, 2 * i)
                        pool.indirect_dma_start(G[:, j, 0:D + 1], None, x2n, bass.IndirectOffsetOnAxis(
                            ap=ridx[:, j:j + 1], axis=0)).then_inc(c_got[j], 16)
                    for j in range(U):
                        steady(pool, i + 1, 2 * i + j // GR + 1)
                        if j == 0:
                            pool.wait_ge(c_sidx, i + 1)
                        if j % GR == 0:
                            pool.wait_ge(c_y, 2 * i + j // GR + 1)
                        pool.indirect_dma_start(agg, bass.IndirectOffsetOnAxis(ap=sidx[:, j:j + 1], axis=0),
                                                Y[:, j, :], None, bounds_check=last_node,
                                                oob_is_err=False).then_inc(c_put[j], 16)
                for j in range(U):
                    pool.wait_ge(c_put[j], 16 * IT)

            @block.vector
            def _(dve):
                nc.vector.memset(CMB, 1.0).then_inc(c_one, 1)
                nc.vector.tensor_copy(ridx[:], src_i[:, 0:U]).then_inc(c_idx, 1)
                for j in range(GR):
                    ins = plain_mask(j, j)
                ins.then_inc(c_mask, 1)
                dve.wait_ge(c_w, 48)
                dve.wait_ge(c_one, 1)
                with dve.Fori(0, IT) as i:
                    for h in range(2):
                        g = 2 * i + h
                        js = range(GR * h, GR * h + GR)
                        steady(dve, 16 * i, 16 * i + 16)
                        for q in js:
                            dve.wait_ge(c_got[q], 16 * i + 16)
                        if h == 0:
                            for q in range(U):
                                dve.wait_ge(c_put[q], 16 * i)
                            nc.vector.tensor_copy(sidx[:], put_i[:, bass.ds(U * i, U)]).then_inc(c_sidx, 1)
                        ins = nc.vector.tensor_copy(ridx[:, GR * h:GR * h + GR],
                                                    src_i[:, bass.ds(U * i + U + GR * h, GR)])
                        if h == 1:
                            ins.then_inc(c_idx, 1)
                        dve.wait_ge(c_sum, g)
                        for j in js:
                            ins = nc.vector.tensor_scalar(CMB[:, j, 0:D], G[:, j, 0:D], G[:, j, D:D + 1], None,
                                                          ALU.mult)
                        ins.then_inc(c_gs, 1)
                        for j in range(GR):
                            ins = plain_mask(U * i + GR * (h + 1) + j, GR * (1 - h) + j)
                        ins.then_inc(c_mask, 1)
                        dve.wait_ge(c_sum, g + 1)
                        nc.vector.tensor_copy(cnt[:, 0:GR], PS[:, 5, 0, 0:GR])
                        nc.vector.tensor_scalar(root[:, 0:GR], PS[:, 5, 0, 0:GR], 1.0, None, ALU.max).then_inc(c_cnt, 1)
                        dve.wait_ge(c_root, g + 1)
                        nc.vector.reciprocal(inv, root).then_inc(c_inv, 1)
                        dve.wait_ge(c_wm, g + 1)
                        for j in range(GR):
                            nc.vector.scalar_tensor_tensor(T1[:, j, :], BE, cnt[:, j:j + 1], PS[:, PC, j, :],
                                                           ALU.mult, ALU.add)
                        dve.wait_ge(c_inv, g + 1)
                        for j in range(GR):
                            ins = nc.vector.tensor_scalar(T2[:, j, :], PS[:, 6, j, :], inv[:, GR + j:GR + j + 1], None,
                                                          ALU.mult)
                        ins.then_inc(c_t, 1)
                        dve.wait_ge(c_t, g + 1)
                        for j in range(GR):
                            ins = nc.vector.scalar_tensor_tensor(Y[:, GR * h + j, :], T1[:, j, :], inv[:, j:j + 1],
                                                                 T2[:, j, :], ALU.mult, ALU.add)
                        ins.then_inc(c_y, 1)

            @block.scalar
            def _(act):
                with act.Fori(0, IT) as i:
                    for h in range(2):
                        g = 2 * i + h
                        act.wait_ge(c_gs, g + 1)
                        act.wait_ge(c_ea[h], 16 * i + 16)
                        for j in range(GR * h, GR * h + GR):
                            act.wait_ge(c_row, U * i + j)
                            nc.scalar.copy(CMB[0:1, j, :], bank(CAR, CW)[0:1, :]).then_inc(c_car, 1)
                        act.wait_ge(c_sum, g + 1)
                        act.wait_ge(c_wm, g)
                        nc.scalar.copy(AT, PS[:, PA + h, :, :])
                        nc.scalar.copy(ET, PS[:, SUM + h, :, :]).then_inc(c_evac, 1)
                        act.wait_ge(c_cnt, g + 1)
                        nc.scalar.sqrt(root[:, GR:2 * GR], root[:, 0:GR]).then_inc(c_root, 1)

            @block.tensor
            def _(pe):
                pe.wait_ge(c_w, 48)
                with pe.Fori(0, IT) as i:
                    for h in range(2):
                        g = 2 * i + h
                        for j in range(GR * h, GR * h + GR):
                            if j % GR == 0:
                                pe.wait_ge(c_mask, g + 1)
                                pe.wait_ge(c_cnt, g)
                            pe.wait_ge(c_car, U * i + j + 1)
                            nc.tensor.matmul(bank(CAR, CW)[0:1, :], M[:, j, 0:1], CMB[:, j, :],
                                             start=True, stop=True).then_inc(c_row, 1)
                            nc.tensor.matmul(PS[:, PA + h, j % GR, :], CMB[:, j, 0:D], M[:, j, :],
                                             start=True, stop=True)
                            nc.tensor.matmul(PS[:, SUM + h, j % GR, :], CMB[:, j, D:2 * D], M[:, j, :],
                                             start=True, stop=True)
                            ins = nc.tensor.matmul(PS[:, 5, 0, j % GR:j % GR + 1], M[:, j, :], CMB[:, j, 2 * D:CW],
                                                   start=True, stop=True)
                        ins.then_inc(c_sum, 1)
                        pe.wait_ge(c_evac, g + 1)
                        pe.wait_ge(c_y, g)
                        for j in range(GR):
                            nc.tensor.matmul(PS[:, 6, j, :], AT[:, j, :], W2, start=True, stop=True)
                            ins = nc.tensor.matmul(PS[:, PC, j, :], ET[:, j, :], WE, start=True, stop=True)
                        ins.then_inc(c_wm, 1)
        end_phase()

        DX = D + 2 * HEADS
        X2L, YL, VC, X3, O3 = areas([D + 1, D, D, D, DX])
        at = 2 * NJ * (4 * D + 1 + DX)
        W2 = big[:, at:at + D]
        B2 = big[:, at + D:at + 2 * D]
        LW = big[:, at + 2 * D:at + 5 * D].rearrange("p (b i) -> p b i", b=3)
        W3 = big[:, at + 5 * D:at + 6 * D]
        W3X = big[:, at + 6 * D:at + 6 * D + DX]
        B3X = big[:, at + 8 * D:at + 8 * D + DX]
        IDA = big[:, at + 10 * D:at + 10 * D + DX]
        B3C = big[:, at + 12 * D:at + 13 * D]
        at += 13 * D
        AC = big[:, at:at + 9].rearrange("p (k b) -> p k b", k=3)
        CF = big[:, at + 16:at + 19]
        A3 = big[:, at + 32:at + 35]
        d_w, d_p, d_m, d_ready = (sem("d_" + n) for n in "w p m ready".split())
        d_ld, d_x2y, d_used, d_v, d_st, d_ps, d_rdy, d_x3, d_o, d_sx, d_so = (sems("dd_" + n, 2) for n in (
            "ld x2y used v st ps rdy x3 o sx so".split()))
        d_t, d_tc, d_z, d_v1, d_v2, d_u, d_uc, d_q, d_oc = (sem("d_" + n) for n in "t tc z v1 v2 u uc q oc".split())
        QA, QB = -(-NJ // 4), -(-NJ // 3)

        def groups(c, w):
            nj = size(c)[1]
            return [(q, range(w * q, min(nj, w * q + w))) for q in range(-(-nj // w))]

        def before_chunk(c, per):
            return per * (CHUNKS if c is None else c)

        def lagged(eng, one, two):
            one(0, 0, 0)
            with eng.Fori(0, CHUNKS // 2 - 1) as i:
                for s in range(2):
                    one(2 * i + s + 1, 1 - s, i + s)
                    two(2 * i + s, s, i)
            m = CHUNKS // 2 - 1
            one(CHUNKS - 1, 1, m)
            two(CHUNKS - 2, 0, m)
            one(None, 0, m + 1)
            two(CHUNKS - 1, 1, m)
            two(None, 0, m + 1)

        with nc.Block() as block:
            @block.sync
            def _(sp):
                with nc.allow_non_contiguous_dma(reason="short columns"):
                    sp.dma_start(W2, w2).then_inc(d_w, 16)
                    sp.dma_start(B2, b2.partition_broadcast(P)).then_inc(d_w, 16)
                    sp.dma_start(LW, linw.rearrange("b o i -> o b i")).then_inc(d_w, 16)
                    sp.dma_start(CF, coef.partition_broadcast(P)).then_inc(d_w, 16)
                    sp.dma_start(AC[:, 0, :], asrc.rearrange("b q h c -> (q h c) b")).then_inc(d_w, 16)
                    sp.dma_start(AC[:, 1, :], adst.rearrange("b q h c -> (q h c) b")).then_inc(d_w, 16)
                    sp.dma_start(AC[:, 2, :], linb.rearrange("b o -> o b")).then_inc(d_w, 16)
                for c, s, n in chunks(sp):
                    np_, nj = size(c)
                    sp.wait_ge(d_used[s], n)
                    sp.wait_ge(d_v[s], n)
                    sp.dma_start(X2L[s][0:np_, 0:nj, :], chunk(x2n, c, D + 1)).then_inc(d_ld[s], 16)
                    sp.dma_start(YL[s][0:np_, 0:nj, :], chunk(agg, c, D)).then_inc(d_ld[s], 16)

            @block.gpsimd
            def _(pool):
                def add(c, s, n):
                    np_, nj = size(c)
                    steady(pool, 32 * n + 32)
                    pool.wait_ge(d_ld[s], 32 * n + 32)
                    nc.gpsimd.tensor_tensor(YL[s][0:np_, 0:nj, :], YL[s][0:np_, 0:nj, :], X2L[s][0:np_, 0:nj, 0:D],
                                            ALU.add).then_inc(d_x2y[s], 1)

                def scale(c, s, n):
                    ln_scale(pool, c, s, n, d_st, d_ps, d_rdy)
                lagged(pool, add, scale)

            @block.vector
            def _(dve):
                dve.wait_ge(d_w, 16 * 7)
                nc.vector.tensor_scalar(W3, LW[:, 0, :], CF[:, 0:1], None, ALU.mult)
                link(dve, "dve", nc.vector.tensor_scalar(A3, AC[:, :, 0], CF[:, 0:1], None, ALU.mult))
                for b in (1, 2):
                    nc.vector.scalar_tensor_tensor(W3, LW[:, b, :], CF[:, b:b + 1], W3, ALU.mult, ALU.add)
                    link(dve, "dve", nc.vector.scalar_tensor_tensor(A3, AC[:, :, b], CF[:, b:b + 1], A3,
                                                                    ALU.mult, ALU.add))
                nc.vector.tensor_scalar(B3C, ones[:], A3[:, 2:3], None, ALU.mult)
                nc.vector.tensor_copy(IDA[:, 0:D], ident[:])
                nc.vector.tensor_scalar(nsrc[:], rin[:], 1.0, None, ALU.add)
                link(dve, "dve", nc.vector.memset(IDA[:, D:DX], 0.0))
                for k in range(2):
                    for q in range(HEADS):
                        r = slice(CH * q, CH * q + CH)
                        link(dve, "dve", nc.vector.tensor_copy(IDA[r, D + HEADS * k + q:D + HEADS * k + q + 1],
                                                               A3[r, k:k + 1]))
                nc.vector.tensor_copy(col[:, 6:7], ones[:, 0:1]).then_inc(d_p, 1)
                dve.wait_ge(d_m, 1)
                nc.vector.tensor_copy(W3X, bank(PA, DX))
                nc.vector.tensor_copy(B3X, bank(PA + 1, DX)).then_inc(d_ready, 1)
                dve.wait_ge(d_ready, 1)

                def rows(c, s, n):
                    np_, nj = size(c)
                    steady(dve, n, n + 1)
                    dve.wait_ge(d_x3[s], n)
                    dve.wait_ge(d_x2y[s], n + 1)
                    for q, js in groups(c, 4):
                        dve.wait_ge(d_z, before_chunk(c, QA) + q + 1)
                        for j in js:
                            rc = rin[0:np_, NC_:NCOL] if c is None else rin[:, bass.ds(c * NJ + j, 1)]
                            ins = nc.vector.scalar_tensor_tensor(VC[s][0:np_, j, :], PS[0:np_, SUM + q % 2, j % 4, :],
                                                                 rc, YL[s][0:np_, j, :], ALU.mult, ALU.add)
                        ins.then_inc(d_v1, 1)
                    dve.wait_ge(d_v1, before_chunk(c, QA) + len(groups(c, 4)))
                    for j in range(nj):
                        r1 = nsrc[0:np_, NC_:NCOL] if c is None else nsrc[:, bass.ds(c * NJ + j, 1)]
                        ins = nc.vector.scalar_tensor_tensor(VC[s][0:np_, j, :], B2[0:np_, :], r1,
                                                             VC[s][0:np_, j, :], ALU.mult, ALU.add)
                    ins.then_inc(d_v[s], 1)
                    dve.wait_ge(d_v[s], n + 1)
                    ln_stats(dve, VC[s], c, s, n, d_st)

                def transformed(c, s, n):
                    np_, nj = size(c)
                    dve.wait_ge(d_so[s], 32 * n)
                    for q, js in groups(c, 3):
                        dve.wait_ge(d_q, before_chunk(c, QB) + q + 1)
                        ins = nc.vector.tensor_tensor(
                            O3[s][0:np_, js[0]:js[-1] + 1, :],
                            bank(6 + q % 2, 3 * DX).rearrange("p (j f) -> p j f", f=DX)[0:np_, 0:len(js), :],
                            B3X[0:np_, :].unsqueeze(1).to_broadcast([np_, len(js), DX]), ALU.add)
                        ins.then_inc(d_oc, 1)
                    dve.wait_ge(d_oc, before_chunk(c, QB) + len(groups(c, 3)))
                    nc.vector.memset(col[0:1, 7:8], 0.0).then_inc(d_o[s], 1)
                lagged(dve, rows, transformed)

            @block.scalar
            def _(act):
                def turned(c, s, n):
                    np_, nj = size(c)
                    for q, js in groups(c, 4):
                        g = before_chunk(c, QA) + q
                        act.wait_ge(d_t, g + 1)
                        if not isinstance(g, int) or g:
                            act.wait_ge(d_z, g)
                        nc.scalar.copy(HT[:, 0:len(js), 0:np_],
                                       PS[:, PA + q % 2, 0:len(js), 0:np_]).then_inc(d_tc, 1)

                def normed(c, s, n):
                    np_, nj = size(c)
                    act.wait_ge(d_o[s], n)
                    ln_apply(act, VC[s], X3[s], c, s, n, d_rdy, d_sx, d_x3)
                    act.wait_ge(d_x3[s], n + 1)
                    act.dma_start(chunk(x3, c, D), X3[s][0:np_, 0:nj, :]).then_inc(d_sx[s], 16)
                    for q, js in groups(c, 3):
                        g = before_chunk(c, QB) + q
                        act.wait_ge(d_u, g + 1)
                        act.wait_ge(d_q, g)
                        nc.scalar.copy(UT[:, 0:len(js), 0:np_], PS[:, 5, 0:len(js), 0:np_]).then_inc(d_uc, 1)
                    act.wait_ge(d_o[s], n + 1)
                    act.dma_start(chunk(xt_d, c, D + HEADS), O3[s][0:np_, 0:nj, 0:D + HEADS]).then_inc(d_so[s], 16)
                    act.dma_start(chunk(ad_d, c, HEADS), O3[s][0:np_, 0:nj, D + HEADS:DX]).then_inc(d_so[s], 16)
                lagged(act, turned, normed)
                for s in range(2):
                    act.wait_ge(d_sx[s], 16 * (CHUNKS // 2 + 1 - s))
                    act.wait_ge(d_so[s], 32 * (CHUNKS // 2 + 1 - s))

            @block.tensor
            def _(pe):
                pe.wait_ge(d_p, 1)
                nc.tensor.transpose(PS[:, PA, 0, :], W3, ident[:])
                nc.tensor.matmul(PS[:, PA, 1, 0:2 * HEADS], W3, IDA[:, D:DX], start=True, stop=True)
                nc.tensor.matmul(bank(PA + 1, DX), B3C, IDA, start=True, stop=True).then_inc(d_m, 1)
                pe.wait_ge(d_ready, 1)

                def turn(c, s, n):
                    np_, nj = size(c)
                    pe.wait_ge(d_ld[s], 32 * n + 32)
                    for q, js in groups(c, 4):
                        g = before_chunk(c, QA) + q
                        for j in js:
                            ins = nc.tensor.transpose(PS[:, PA + q % 2, j % 4, 0:np_], X2L[s][0:np_, j, 0:D],
                                                      ident[0:np_, 0:np_])
                        ins.then_inc(d_t, 1)
                        if q == len(groups(c, 4)) - 1:
                            ins2 = nc.tensor.matmul(PS[0:1, CAR, 0, 0:1], ones[:, 0:1], ones[:, 0:1],
                                                    start=True, stop=True).then_inc(d_used[s], 1)
                        pe.wait_ge(d_tc, g + 1)
                        if not isinstance(g, int):
                            pe.wait_ge(d_v1, g - 1 if q else g)
                        elif g:
                            pe.wait_ge(d_v1, g - 1)
                        for j in js:
                            ins = nc.tensor.matmul(PS[0:np_, SUM + q % 2, j % 4, :], HT[:, j % 4, 0:np_], W2,
                                                   start=True, stop=True)
                        ins.then_inc(d_z, 1)

                def transform(c, s, n):
                    np_, nj = size(c)
                    pe.wait_ge(d_x3[s], n + 1)
                    for q, js in groups(c, 3):
                        g = before_chunk(c, QB) + q
                        for j in js:
                            ins = nc.tensor.transpose(PS[:, 5, j % 3, 0:np_], X3[s][0:np_, j, :],
                                                      ident[0:np_, 0:np_])
                        ins.then_inc(d_u, 1)
                        pe.wait_ge(d_uc, g + 1)
                        if not isinstance(g, int):
                            pe.wait_ge(d_oc, g - 1 if q else g)
                        elif g:
                            pe.wait_ge(d_oc, g - 1 if q else g)
                        for j in js:
                            ins = nc.tensor.matmul(bank(6 + q % 2, 512)[0:np_, (j % 3) * DX:(j % 3 + 1) * DX],
                                                   UT[:, j % 3, 0:np_], W3X, start=True, stop=True)
                        ins.then_inc(d_q, 1)
                lagged(pe, turn, transform)
        end_phase()

        XW = D + HEADS
        xts = big[:, 0:T * XW].rearrange("p (t f) -> p t f", f=XW)
        AL = sb("AL", [P, T, HEADS])
        AD = sb("AD", [P, U, HEADS])
        e_idx, e_cp, e_al = sem("e_idx"), sem("e_cp"), sem("e_al")
        e_got, e_gad = pool_sems("e_got", U), pool_sems("e_gad", U)
        with nc.Block() as block:
            @block.gpsimd
            def _(pool):
                with pool.Fori(0, IT) as i:
                    for j in range(U):
                        steady(pool, 2 * i + j // GR + 1, 2 * i)
                        if j % GR == 0:
                            pool.wait_ge(e_idx, 2 * i + j // GR + 1)
                            pool.wait_ge(e_cp, 2 * i)
                            pool.wait_ge(e_al, 2 * i)
                        pool.indirect_dma_start(G[:, j, 0:XW], None, xt_d, bass.IndirectOffsetOnAxis(
                            ap=ridx[:, j:j + 1], axis=0)).then_inc(e_got[j], 16)
                        steady(pool)
                        pool.indirect_dma_start(AD[:, j, :], None, ad_d, bass.IndirectOffsetOnAxis(
                            ap=sidx[:, j:j + 1], axis=0)).then_inc(e_gad[j], 16)

            @block.vector
            def _(dve):
                nc.vector.tensor_copy(ridx[:], src_i[:, 0:U])
                nc.vector.tensor_copy(sidx[:], dst_i[:, 0:U]).then_inc(e_idx, 2)
                with dve.Fori(0, IT) as i:
                    for h in range(2):
                        js = slice(GR * h, GR * h + GR)
                        steady(dve, 16 * i + 16)
                        for q in range(GR * h, GR * h + GR):
                            dve.wait_ge(e_got[q], 16 * i + 16)
                            dve.wait_ge(e_gad[q], 16 * i + 16)
                        nc.vector.tensor_copy(ridx[:, js], src_i[:, bass.ds(U * i + U + GR * h, GR)])
                        nc.vector.tensor_copy(sidx[:, js], dst_i[:, bass.ds(U * i + U + GR * h, GR)]).then_inc(e_idx, 1)
                        nc.vector.tensor_tensor(AL[:, bass.ds(U * i + GR * h, GR), :], G[:, js, D:XW], AD[:, js, :],
                                                ALU.add).then_inc(e_al, 1)

            @block.scalar
            def _(act):
                with act.Fori(0, IT) as i:
                    for h in range(2):
                        steady(act, 16 * i + 16)
                        for q in range(GR * h, GR * h + GR):
                            act.wait_ge(e_got[q], 16 * i + 16)
                        nc.scalar.copy(xts[:, bass.ds(U * i + GR * h, GR), :], G[:, GR * h:GR * h + GR, :]).then_inc(e_cp, 1)

        HG = 2 * HEADS
        ALT = sb("ALT", [TG, 2, HEADS, P])
        FW = sb("FW", [TG, 2, HEADS, P])
        pen = sb("pen", [TG, 2, P])
        tpen = sb("tpen", [TG, 2, HEADS])
        tval = sb("tval", [TG, 2, HEADS])
        run4 = sb("run4", [HEADS, 3, T])
        cin = sb("cin", [TG, 2, HEADS])
        em = sb("em", [P, 4])
        f_al, f_t, f_v, f_tv, f_c, f_b, f_s, f_st, f_x, f_e = (sem("f_" + n) for n in "al t v tv c b s st x e".split())
        with nc.Block() as block:
            @block.vector
            def _(dve):
                a2 = AL[:].rearrange("p t h -> p (t h)")
                link(dve, "dve", nc.vector.scalar_tensor_tensor(a2, a2, 0.2, a2, ALU.mult, ALU.max))
                link(dve, "dve", nc.vector.tensor_scalar(em[:, 0:1], part_f[:, 0:1], 0.5, None, ALU.is_gt))
                link(dve, "dve", nc.vector.tensor_scalar(em[:, 1:2], part_f[:, 0:1], TE + 0.5, None, ALU.is_lt))
                link(dve, "dve", nc.vector.tensor_tensor(em[:, 0:1], em[:, 0:1], em[:, 1:2], ALU.mult))
                link(dve, "dve", nc.vector.tensor_scalar(em[:, 2:3], em[:, 0:1], -1.0, BIG, ALU.add, ALU.mult))
                nc.vector.tensor_scalar(a2, a2, em[:, 0:1], em[:, 2:3], ALU.mult, ALU.add).then_inc(f_al, 1)
                dve.wait_ge(f_t, 1)
                nc.vector.tensor_copy(ALT[:], PS[0:TG, 0:2, :, :])
                link(dve, "dve", nc.vector.memset(FW[:], 0.0))
                first, last = 1, TE
                for back in range(2):
                    link(dve, "dve", nc.vector.tensor_scalar(pen[:], (endrow if back else newseg)[:], -BIG, None,
                                                             ALU.mult))
                    sl = slice(last, first - 1, -1) if back else slice(first, last + 1)
                    for rescan in range(2):
                        for g in range(2):
                            for q in range(HEADS):
                                o = FW[:, g, q, sl]
                                nc.vector.tensor_tensor_scan(
                                    o, pen[:, g, sl], (FW if back else ALT)[:, g, q, sl],
                                    cin[:, g, q:q + 1] if rescan else -BIG, ALU.add, ALU.max)
                        link(dve, "dve", nc.vector.memset(col[:, 7:8], 0.0))
                        if rescan:
                            continue
                        nc.vector.tensor_copy(tval[:], FW[:, :, :, (first if back else last)])
                        for q in range(HEADS):
                            nc.vector.tensor_reduce(tpen[:, :, q], pen[:, :, first:last + 1], AX.X, ALU.min)
                        nc.vector.memset(col[:, 7:8], 0.0).then_inc(f_v, 1)
                        dve.wait_ge(f_tv, back + 1)
                        link(dve, "dve", nc.vector.tensor_copy(run4[:, 0:2, :], PS[0:HEADS, 2:4, :, :].rearrange(
                            "p a b c -> p a (b c)")[:, :, 0:T]))
                        t_all = slice(T - 1, None, -1) if back else slice(0, T)
                        link(dve, "dve", nc.vector.tensor_tensor_scan(run4[:, 2, t_all], run4[:, 0, t_all],
                                                                     run4[:, 1, t_all], -BIG, ALU.add, ALU.max))
                        if back:
                            nc.vector.tensor_copy(run4[:, 0, 0:T - 1], run4[:, 2, 1:T])
                            nc.vector.memset(run4[:, 0, T - 1:T], -BIG).then_inc(f_c, 1)
                        else:
                            nc.vector.tensor_copy(run4[:, 0, 1:T], run4[:, 2, 0:T - 1])
                            nc.vector.memset(run4[:, 0, 0:1], -BIG).then_inc(f_c, 1)
                        dve.wait_ge(f_b, back + 1)
                        link(dve, "dve", nc.vector.tensor_copy(cin[:].rearrange("p g q -> p (g q)"),
                                                               PS[0:TG, 4, 0, 0:HG]))
                nc.vector.memset(col[:, 7:8], 0.0).then_inc(f_s, 1)
                dve.wait_ge(f_st, 1)
                for g in range(2):
                    for q in range(HEADS):
                        ins = nc.vector.tensor_tensor(AL[:, TG * g:TG * g + TG, q], AL[:, TG * g:TG * g + TG, q],
                                                      PS[:, 5 + g, q, 0:TG], ALU.subtract)
                ins.then_inc(f_x, 1)

            @block.tensor
            def _(pe):
                pe.wait_ge(f_al, 1)
                for g in range(2):
                    for q in range(HEADS):
                        ins = nc.tensor.transpose(PS[0:TG, g, q, :], AL[:, TG * g:TG * g + TG, q], ident[:])
                ins.then_inc(f_t, 1)
                for back in range(2):
                    pe.wait_ge(f_v, back + 1)
                    for k, v in enumerate((tpen, tval)):
                        for g in range(2):
                            ins = nc.tensor.transpose(bank(2 + k)[0:HEADS, TG * g:TG * g + TG], v[:, g, :],
                                                      ident[0:TG, 0:TG])
                    ins.then_inc(f_tv, 1)
                    pe.wait_ge(f_c, back + 1)
                    for g in range(2):
                        ins = nc.tensor.transpose(PS[0:TG, 4, 0, HEADS * g:HEADS * g + HEADS],
                                                  run4[:, 0, TG * g:TG * g + TG], ident[0:HEADS, 0:HEADS])
                    ins.then_inc(f_b, 1)
                pe.wait_ge(f_s, 1)
                for g in range(2):
                    for q in range(HEADS):
                        ins = nc.tensor.transpose(PS[:, 5 + g, q, 0:TG], FW[:, g, q, :], ident[0:TG, 0:TG])
                ins.then_inc(f_st, 1)

            @block.scalar
            def _(act):
                act.wait_ge(f_x, 1)
                nc.scalar.activation(AL[:].rearrange("p t h -> p (t h)"), AL[:].rearrange("p t h -> p (t h)"),
                                     ACT.Exp).then_inc(f_e, 1)

        den = sb("den", [P, 2, GR * HEADS])
        h_mask, h_z, h_car, h_row, h_sum, h_d, h_y, h_sidx = (sem("h_" + n) for n in "mask z car row sum d y sidx".split())
        h_put = pool_sems("h_put", U)
        with nc.Block() as block:
            @block.gpsimd
            def _(pool):
                last_node = pool.to_reg(N - 1)
                with pool.Fori(0, IT) as i:
                    for j in range(U):
                        steady(pool, i + 1, 2 * i + j // GR + 1)
                        if j == 0:
                            pool.wait_ge(h_sidx, i + 1)
                        if j % GR == 0:
                            pool.wait_ge(h_y, 2 * i + j // GR + 1)
                        pool.indirect_dma_start(agg, bass.IndirectOffsetOnAxis(ap=sidx[:, j:j + 1], axis=0),
                                                Y[:, j, :], None, bounds_check=last_node,
                                                oob_is_err=False).then_inc(h_put[j], 16)
                for j in range(U):
                    pool.wait_ge(h_put[j], 16 * IT)

            @block.vector
            def _(dve):
                for j in range(GR):
                    ins = plain_mask(j, j)
                ins.then_inc(h_mask, 1)
                with dve.Fori(0, IT) as i:
                    for h in range(2):
                        g = 2 * i + h
                        if h == 0:
                            steady(dve, 16 * i)
                            for q in range(U):
                                dve.wait_ge(h_put[q], 16 * i)
                            nc.vector.tensor_copy(sidx[:], put_i[:, bass.ds(U * i, U)]).then_inc(h_sidx, 1)
                        for j in range(GR * h, GR * h + GR):
                            t = U * i + j
                            nc.vector.tensor_tensor(
                                G[:, j, 0:D].rearrange("p (q c) -> p q c", c=CH),
                                big[:, bass.ds(t * XW, D)].rearrange("p (q c) -> p q c", c=CH),
                                AL[:, bass.ds(t, 1), :].rearrange("p a q -> p (a q)").unsqueeze(2)
                                .to_broadcast([P, HEADS, CH]), ALU.mult)
                        steady(dve)
                        nc.vector.tensor_copy(G[:, GR * h:GR * h + GR, D:XW],
                                              AL[:, bass.ds(U * i + GR * h, GR), :]).then_inc(h_z, 1)
                        for j in range(GR):
                            ins = plain_mask(U * i + GR * (h + 1) + j, GR * (1 - h) + j)
                        ins.then_inc(h_mask, 1)
                        dve.wait_ge(h_sum, g + 1)
                        nc.vector.tensor_scalar(den[:, h, :], PS[:, PA + h, 0, 0:GR * HEADS], 1e-16, None,
                                                ALU.add).then_inc(h_d, 1)
                        dve.wait_ge(h_d, 2 * g + 1)
                        nc.vector.reciprocal(den[:, h, :], den[:, h, :]).then_inc(h_d, 1)
                        dve.wait_ge(h_d, 2 * g + 2)
                        nc.vector.tensor_tensor(
                            Y[:, GR * h:GR * h + GR, :].rearrange("p s (q c) -> p (s q) c", c=CH),
                            bank(SUM + h).rearrange("p (s c) -> p s c", c=CH),
                            den[:, h, :].unsqueeze(2).to_broadcast([P, GR * HEADS, CH]), ALU.mult).then_inc(h_y, 1)

            @block.scalar
            def _(act):
                with act.Fori(0, IT) as i:
                    for h in range(2):
                        act.wait_ge(h_z, 2 * i + h + 1)
                        for j in range(GR * h, GR * h + GR):
                            act.wait_ge(h_row, U * i + j)
                            nc.scalar.copy(G[0:1, j, :], bank(CAR, XW)[0:1, :]).then_inc(h_car, 1)

            @block.tensor
            def _(pe):
                with pe.Fori(0, IT) as i:
                    for h in range(2):
                        g = 2 * i + h
                        for j in range(GR * h, GR * h + GR):
                            if j % GR == 0:
                                pe.wait_ge(h_mask, g + 1)
                            pe.wait_ge(h_car, U * i + j + 1)
                            nc.tensor.matmul(bank(CAR, XW)[0:1, :], M[:, j, 0:1], G[:, j, :],
                                             start=True, stop=True).then_inc(h_row, 1)
                            nc.tensor.matmul(PS[:, PA + h, 0, HEADS * (j % GR):HEADS * (j % GR) + HEADS], M[:, j, :],
                                             G[:, j, D:XW], start=True, stop=True)
                            ins = nc.tensor.matmul(PS[:, SUM + h, j % GR, :], M[:, j, :], G[:, j, 0:D],
                                                   start=True, stop=True)
                        ins.then_inc(h_sum, 1)
        end_phase()

        XA, YA, XN, V = areas([D, D, D, D])

        def make_out(dve, c, s, n, used, vr):
            np_, nj = size(c)
            nc.vector.tensor_tensor(V[s][0:np_, 0:nj, :], XA[s][0:np_, 0:nj, :], YA[s][0:np_, 0:nj, :],
                                    ALU.add).then_inc(vr[s], 1)

        norm_pass("D", [(XA, x3, D), (YA, agg, D)], V, XN, D, out, make_out)


_INS = ["x", "src", "dst", "edge_attr_128", "edge_weight", "L0_gnn_weight", "L0_gnn_bias", "L1_gnn_W", "L1_gnn_b",
        "L1_gnn_gamma", "L1_gnn_beta", "L2_gnn_W", "L2_gnn_b", "L2_gnn_We", "L2_gnn_be", "L3_gnn_coeffs_t",
        "L3_gnn_lin_weight", "L3_gnn_lin_bias", "L3_gnn_att_src", "L3_gnn_att_dst"]


def kernel(**inputs):
    import numpy as _np
    import concourse.bacc as _bacc
    from concourse import mybir as _mybir
    from concourse.bass_utils import run_bass_kernel_spmd as _run

    nc = _bacc.Bacc("TRN2", target_bir_lowering=False, num_devices=1)
    arrays, args = {}, []
    for name in _INS:
        a = _np.ascontiguousarray(inputs[name])
        arrays[f"in_{name}"] = a
        args.append(nc.dram_tensor(f"in_{name}", a.shape, _mybir.dt.from_np(a.dtype), kind="ExternalInput").ap())
    out = nc.dram_tensor("out_0", (N, D), F32, kind="ExternalOutput").ap()
    build(nc, *args, out)
    r = _run(nc, [arrays], core_ids=[0])
    return r.results[0]["out_0"]
```

```python
import concourse.bass as bass
from concourse import mybir
from contextlib import ExitStack

F32, BF16, I32, U8 = mybir.dt.float32, mybir.dt.bfloat16, mybir.dt.int32, mybir.dt.uint8
ALU, ACT, AX = mybir.AluOpType, mybir.ActivationFunctionType, mybir.AxisListType

P, D = 128, 128
N, E = 50000, 25000
TE = 125
T = E // TE
GR = 4
U = 2 * GR
IT = T // U
TG = T // 2
TP = T + U
POS = T * P
NL = 5
HEADS, CH = 4, D // 4
NC_ = N // P
TAIL0 = NC_ * P
TAIL = N - TAIL0
NJ = 13
CHUNKS = NC_ // NJ
GAMA = 0.9
CC = 1.0 / (2.0 + GAMA)
EPS = 1e-5
BIG = 1.0e30


def build(nc, x0, src, dst, ea, ew, w0, b0, w1, b1, gamma, beta, w2, b2, we, be, coef, linw, linb, asrc, adst, out):
    assert T * TE == E and IT * U == T and CHUNKS * NJ == NC_ and CHUNKS % 2 == 0
    ctx = ExitStack()

    def sb(name, shape, dt=F32):
        return ctx.enter_context(nc.sbuf_tensor(name, shape, dt))

    phase = []

    def sem(name):
        phase.append(nc.alloc_semaphore(name=name))
        return phase[-1]

    def end_phase():
        with nc.Block() as block:
            @block.gpsimd
            def _(pool):
                nc.clear_and_free_semaphores(phase)
        phase.clear()

    def sems(name, n):
        return [sem(f"{name}{i}") for i in range(n)]

    def pool_sems(name, n):
        return [ctx.enter_context(nc.semaphore(f"{name}{i}")) for i in range(n)]

    def dram(name, shape, dt=F32):
        return nc.dram_tensor(name, shape, dt).ap()

    with ctx:
        keys_d = dram("keys_d", (T, P), U8)
        agg = dram("agg", (N, D))
        x1 = dram("x1", (N, D))
        x2n = dram("x2n", (N, D + 1))
        x3 = dram("x3", (N, D))
        xt_d = dram("xt_d", (N, D + HEADS))
        ad_d = dram("ad_d", (N, HEADS))
        lastpos = dram("lastpos", (N, 1), I32)
        tabs = [dram(f"tab{i}", (POS, D)) for i in range(3)]

        big = sb("big", [P, T * (D + HEADS)])
        keyrow = sb("keyrow", [P, TP * P], U8)
        ident = sb("ident", [P, P])
        iota_i = sb("iota_i", [P, NC_ + 1], I32)
        iota_f = sb("iota_f", [P, NC_ + 1])
        iota_h = sb("iota_h", [P, NC_ + 2], mybir.dt.float16)
        part_i = sb("part_i", [P, 1], I32)
        part_f = sb("part_f", [P, 1])
        ones = sb("ones", [P, P])
        minus_half = sb("minus_half", [P, NC_ + 1])
        zcol = sb("zcol", [P, P])
        keycol = sb("keycol", [P, TP])
        wcol = sb("wcol", [P, TP])
        wccol = sb("wccol", [P, TP])
        src_i = sb("src_i", [P, TP], I32)
        dst_i = sb("dst_i", [P, TP], I32)
        put_i = sb("put_i", [P, TP], I32)
        PIDX = sb("PIDX", [P, 16], I32)
        PGOT = sb("PGOT", [P, 16], I32)
        gidx = sb("gidx", [P, TP], I32)
        ends = sb("ends", [P, GR + T, 2])
        isnode0 = sb("isnode0", [P, TP])
        newseg = sb("newseg", [TG, 2, P])
        endrow = sb("endrow", [TG, 2, P])
        deg = sb("deg", [P, 2, NC_ + 1])
        nsrc = sb("nsrc", [P, NC_ + 1])
        rin = sb("rin", [P, NC_ + 1])
        G = sb("G", [P, U, D + HEADS])
        Y = sb("Y", [P, U, D])
        M = sb("M", [P, U, P])
        HT = sb("HT", [P, GR, P])
        OT = sb("OT", [P, GR, P])
        UT = sb("UT", [P, GR, P])
        UO = sb("UO", [P, GR, P])
        ridx = sb("ridx", [P, U], I32)
        sidx = sb("sidx", [P, U], I32)
        lastc = sb("lastc", [P, TP])
        whole = sb("whole", [1, TP])
        lring = sb("lring", [P, U])
        carry = sb("carry", [1, 2 * D])
        wmat = sb("wmat", [P, D])
        wplus = sb("wplus", [P, D])
        bias = sb("bias", [P, D])
        row_a = sb("row_a", [P, D])
        row_b = sb("row_b", [P, D])
        gb = sb("gb", [P, 2, NL])
        col = sb("col", [P, 8])
        scol = sb("scol", [P, 1])
        note = sb("note", [1, 16])
        tcol = sb("tcol", [P, 1])
        mcol = sb("mcol", [P, 1])
        rcol = sb("rcol", [P, 1])
        st6 = sb("st6", [P, NJ, 6])
        mv = sb("mv", [P, 2, NJ, 2])
        rs = sb("rs", [P, 2, NJ])
        nb = sb("nb", [P, 2, NJ])

        PS = ctx.enter_context(nc.psum_tensor("PS", [P, 8, 4, P], F32))
        CAR, SUM, PA, PB, PC, ACC1, ACC2 = 0, 1, 3, 5, 7, 6, 7

        def bank(b, n=512):
            return PS[:, b, :, :].rearrange("p a b -> p (a b)")[:, 0:n]

        def steady(eng, *values):
            for v in values:
                if not isinstance(v, int):
                    eng.lower_val(v)
            eng.wait_ge(s_go, 1)

        credits = []

        def credit(s, n):
            credits.append(s)
            nc.vector.memset(note[:, len(credits) - 1:len(credits)], 0.0).then_inc(s, n)

        chain = {}

        def link(eng, name, ins):
            s, v = chain[name]
            ins.then_inc(s, 1)
            chain[name] = (s, v + 1)
            eng.wait_ge(s, v + 1)

        s_dve, s_go = (ctx.enter_context(nc.semaphore(n)) for n in ("s_dve", "s_go"))
        chain["dve"] = (s_dve, 0)

        DI = big[0:TG, 0:2 * P].bitcast(I32).rearrange("p (g i) -> p g i", g=2)
        SI = big[0:TG, 256:256 + 2 * P].bitcast(I32).rearrange("p (g i) -> p g i", g=2)

        def tview(k):
            return big[0:TG, 512 + 256 * k:768 + 256 * k].rearrange("p (g i) -> p g i", g=2)

        WF, DF, SF, LID, KT, PUT, DGI, SEL, N0, KR = [tview(k) for k in range(10)]
        RT = big[0:TG, 4096:4096 + 64].bitcast(U8).rearrange("p (g i) -> p g i", g=2)
        ZB = big[:, 8192:8192 + NJ * D]
        s_ms, s_ld, s_id, s_tr, s_ky, s_tp, s_zf = (sem(n) for n in ("s_ms", "s_ld", "s_id", "s_tr", "s_ky", "s_tp", "s_zf"))

        with nc.Block() as block:
            @block.sync
            def _(sp):
                sp.wait_ge(s_ms, 3)
                n = 0
                for g in range(2):
                    lo = g * TG * TE
                    for t_, v in ((DI, dst), (SI, src), (WF, ew)):
                        sp.dma_start(t_[:, g, 1:TE + 1],
                                     v[lo:lo + TG * TE].rearrange("(t e) -> t e", e=TE)).then_inc(s_ld, 16)
                        n += 1
                prev = dst[0:E].rearrange("(t e) -> t e", e=TE)
                with nc.allow_non_contiguous_dma(reason="one edge of each tile"):
                    sp.dma_start(DI[1:TG, 0, 0:1], prev[0:TG - 1, TE - 1:TE]).then_inc(s_ld, 16)
                    sp.dma_start(DI[:, 1, 0:1], prev[TG - 1:T - 1, TE - 1:TE]).then_inc(s_ld, 16)
                    sp.dma_start(DI[:, 0, TE + 1:TE + 2], prev[1:TG + 1, 0:1]).then_inc(s_ld, 16)
                    sp.dma_start(DI[0:TG - 1, 1, TE + 1:TE + 2], prev[TG + 1:T, 0:1]).then_inc(s_ld, 16)
                sp.wait_ge(s_ky, 1)
                sp.dma_start(keys_d.rearrange("(g t) i -> t g i", g=2), RT).then_inc(s_tp, 16)
                sp.wait_ge(s_tp, 16)
                flat = keys_d.rearrange("t i -> (t i)")
                sp.dma_start(keyrow[:, 0:T * P], flat.partition_broadcast(P)).then_inc(s_tp, 16)
                sp.dma_start(keyrow[:, T * P:TP * P], flat[0:U * P].partition_broadcast(P)).then_inc(s_tp, 16)
                sp.wait_ge(s_tp, 48)

            @block.scalar
            def _(act):
                act.wait_ge(s_zf, 1)
                av = agg[0:TAIL0, :].rearrange("(p n) f -> p n f", n=NC_)
                zv = ZB.rearrange("p (n f) -> p n f", f=D)
                for c in range(CHUNKS):
                    act.dma_start(av[:, c * NJ:(c + 1) * NJ, :], zv).then_inc(s_zf, 16)
                act.dma_start(agg[TAIL0:N, :], ZB[0:TAIL, 0:D]).then_inc(s_zf, 16)
                act.wait_ge(s_zf, 1 + 16 * (CHUNKS + 1))

            @block.gpsimd
            def _(pool):
                pool.iota(iota_i[:], pattern=[[1, NC_ + 1]], base=0, channel_multiplier=0).then_inc(s_id, 1)
                pool.iota(part_i[:], pattern=[[0, 1]], base=0, channel_multiplier=1).then_inc(s_id, 1)

            @block.vector
            def _(dve):
                nc.vector.memset(ZB, 0.0).then_inc(s_zf, 1)
                nc.vector.memset(DI, -1).then_inc(s_ms, 1)
                nc.vector.memset(SI, 0).then_inc(s_ms, 1)
                nc.vector.memset(WF, 0.0).then_inc(s_ms, 1)
                nc.vector.memset(ones[:], 1.0)
                nc.vector.memset(zcol[:], 0.0)
                nc.vector.memset(minus_half[:], -0.5)
                nc.vector.memset(KT, 255.0)
                nc.vector.memset(KR, 254.0)
                nc.vector.memset(newseg[:], 0.0)
                nc.vector.memset(endrow[:], 0.0)
                nc.vector.memset(ends[:, 0:GR, :], 0.0)
                link(dve, "dve", nc.vector.memset(N0, 0.0))
                link(dve, "dve", nc.vector.memset(N0[0:1, 0, P - 1:P], 1.0))
                dve.wait_ge(s_id, 2)
                nc.vector.tensor_copy(iota_f[:], iota_i[:])
                nc.vector.tensor_copy(iota_h[:, 0:NC_ + 1], iota_i[:])
                link(dve, "dve", nc.vector.tensor_copy(part_f[:], part_i[:]))
                nc.vector.tensor_scalar(ident[:], iota_f[:, 0:P], part_f[:, 0:1], None, ALU.is_equal)
                dve.wait_ge(s_ld, 16 * 10)
                e = slice(1, TE + 1)
                nc.vector.memset(WF[:, :, 0:1], 1.0)
                nc.vector.tensor_copy(DF, DI)
                link(dve, "dve", nc.vector.tensor_copy(SF, SI))
                for g in range(2):
                    nc.vector.tensor_tensor(newseg[:, g, e], DF[:, g, e], DF[:, g, 0:TE], ALU.not_equal)
                    nc.vector.tensor_tensor(endrow[:, g, e], DF[:, g, e], DF[:, g, 2:TE + 2], ALU.not_equal)
                    nc.vector.tensor_scalar(N0[:, g, e], DF[:, g, e], 0.0, None, ALU.is_equal)
                    nc.vector.tensor_scalar(PUT[:, g, :], DF[:, g, :], float(N), None, ALU.subtract)
                    link(dve, "dve", nc.vector.tensor_scalar(DGI[:, g, :], DF[:, g, :], 0.0, None, ALU.max))
                for g in range(2):
                    link(dve, "dve", nc.vector.tensor_tensor_scan(LID[:, g, 0:TE + 1], ones[0:TG, 0:TE + 1],
                                                                 newseg[:, g, 0:TE + 1], 0.0, ALU.mult, ALU.add))
                    nc.vector.tensor_copy(KT[:, g, 0:TE + 1], LID[:, g, 0:TE + 1])
                    nc.vector.tensor_copy(KR[:, g, 0:1], LID[:, g, TE:TE + 1])
                    nc.vector.tensor_copy(KR[:, g, e], LID[:, g, e])
                    nc.vector.tensor_tensor(SEL[:, g, :], endrow[:, g, :], N0[:, g, :], ALU.mult)
                    link(dve, "dve", nc.vector.tensor_tensor(PUT[:, g, :], PUT[:, g, :], endrow[:, g, :], ALU.mult))
                    link(dve, "dve", nc.vector.tensor_scalar(PUT[:, g, :], PUT[:, g, :], float(N), None, ALU.add))
                nc.vector.tensor_copy(RT, KR).then_inc(s_ky, 1)
                link(dve, "dve", nc.vector.tensor_copy(mv[:, 0, 0, 0:1], ones[:, 0:1]))
                nc.vector.memset(col[:], 0.0).then_inc(s_ky, 1)
                dve.wait_ge(s_tr, 16)
                slots = PS[:].rearrange("p b s c -> p (b s) c")
                outs = [keycol, wcol, src_i, dst_i, put_i, None, None, isnode0]
                for k, o in enumerate(outs):
                    v = slots[:, 2 * k:2 * k + 2, 0:TG]
                    if o is None:
                        nc.vector.tensor_copy(ends[:, GR:GR + T, k - 5].rearrange("p (g t) -> p g t", g=2), v)
                    else:
                        nc.vector.tensor_copy(o[:, 0:T].rearrange("p (g t) -> p g t", g=2), v)
                        nc.vector.tensor_copy(o[:, T:TP], slots[:, 2 * k, 0:U])
                link(dve, "dve", nc.vector.tensor_scalar(wccol[:, 0:T].rearrange("p (g t) -> p g t", g=2),
                                                         slots[:, 2:4, 0:TG], CC, None, ALU.mult))
                link(dve, "dve", nc.vector.tensor_copy(wccol[:, T:TP], wccol[:, 0:U]))
                link(dve, "dve", nc.vector.memset(wccol[0:1, :], 1.0))
                nc.vector.memset(PS[:], 0.0).then_inc(s_go, 1)

            @block.tensor
            def _(pe):
                pe.wait_ge(s_ky, 2)
                for k, v in enumerate((KT, WF, SF, DGI, PUT, endrow, SEL, N0)):
                    for g in range(2):
                        nc.tensor.transpose(PS[:, (2 * k + g) // 4, (2 * k + g) % 4, 0:TG], v[:, g, :], ident[0:TG, 0:TG]).then_inc(s_tr, 1)
        end_phase()

        hip = big[:, 2500:2500 + 2 * TP].rearrange("p (k t) -> p k t", k=2)
        lop = big[:, 8200:8200 + 2 * TP].rearrange("p (k t) -> p k t", k=2)
        hi, lo = hip[:, :, 0:T], lop[:, :, 0:T]
        tmp = big[:, 800:800 + 2 * T].rearrange("p (k t) -> p k t", k=2)
        tmp_i = big[:, 1200:1200 + 2 * T].bitcast(I32).rearrange("p (k t) -> p k t", k=2)
        nod = big[:, 1600:1600 + 2 * T].rearrange("p (k t) -> p k t", k=2)
        tail_m = big[:, 2000:2000 + 2 * T].rearrange("p (k t) -> p k t", k=2)
        edge_p = big[:, 2400:2404]
        HA = big[:, 3000:3000 + U * P].bitcast(BF16).rearrange("p (s i) -> p s i", i=P)
        HB = big[:, 5000:5000 + U * (NC_ + 2)].bitcast(BF16).rearrange("p (s i) -> p s i", i=NC_ + 2)
        NCOL = NC_ + 1

        s_w = sem("s_w")
        a_idx, a_lr, a_mask, a_row, a_aggT, a_aggC, a_y, a_yc, a_ch, a_hot, a_hist = (
            sem("a_" + n) for n in "idx lr mask row aggT aggC y yc ch hot hist".split())
        a_got, a_put = pool_sems("a_got", U), pool_sems("a_put", U)

        OPS = GR + 1

        def last_segments(dve, weights):
            link(dve, "dve", nc.vector.tensor_tensor(lastc[:], keycol[:],
                                                     keyrow[:].rearrange("p (t i) -> p t i", i=P)[:, :, 0],
                                                     ALU.is_equal))
            link(dve, "dve", nc.vector.tensor_copy(whole[:], lastc[0:1, :]))
            if weights is not None:
                link(dve, "dve", nc.vector.tensor_tensor(lastc[:], lastc[:], weights[:], ALU.mult))
            link(dve, "dve", nc.vector.memset(lastc[0:1, :], 0.0))

        def running_sums(dve, g, tile, h, row0, local, carried, summed, made):
            for jj in range(OPS):
                j = GR * h + jj
                if jj < 2:
                    dve.wait_ge(summed, GR * g + (GR if jj else 1))
                dve.wait_ge(made, OPS * g + jj + 1)
                if jj == 0:
                    nc.vector.tensor_copy(row0(j), carried).then_inc(made, 1)
                else:
                    nc.vector.scalar_tensor_tensor(carried if jj == GR else row0(j), row0(j - 1),
                                                   whole[0:1, bass.ds(tile + jj - 1, 1)], local(jj - 1),
                                                   ALU.mult, ALU.add).then_inc(made, 1)

        def two_stages(eng, one, two, rest=lambda i, h: None):
            one(0, 0)
            rest(0, 0)
            with eng.Fori(0, IT - 1) as i:
                for h in range(2):
                    n = (i + h, 1 - h)
                    one(*n)
                    two(i, h)
                    rest(*n)
            one(IT - 1, 1)
            two(IT - 1, 0)
            rest(IT - 1, 1)
            two(IT - 1, 1)

        def edge_mask(t, slot, weights):
            return nc.vector.tensor_scalar(M[:, slot, :], keyrow[:, bass.ds(t * P, P)], keycol[:, bass.ds(t, 1)],
                                           weights[:, bass.ds(t, 1)], ALU.is_equal, ALU.mult)

        with nc.Block() as block:
            @block.sync
            def _(sp):
                sp.dma_start(wmat[:], w0).then_inc(s_w, 16)
                sp.wait_ge(s_w, 16)

            @block.gpsimd
            def _(pool):
                last_node = pool.to_reg(N - 1)

                def gather(i, h):
                    g = 2 * i + h
                    for j in range(GR * h, GR * h + GR):
                        steady(pool, g + 1)
                        if j % GR == 0:
                            pool.wait_ge(a_idx, g + 1)
                            pool.wait_ge(a_aggT, g + 1)
                        pool.indirect_dma_start(G[:, j, 0:D], None, x0, bass.IndirectOffsetOnAxis(
                            ap=ridx[:, j:j + 1], axis=0)).then_inc(a_got[j], 16)

                def scatter(i, h):
                    for j in range(GR * h, GR * h + GR):
                        steady(pool, 2 * i + h + 1)
                        if j % GR == 0:
                            pool.wait_ge(a_yc, 2 * i + h + 1)
                        pool.indirect_dma_start(agg, bass.IndirectOffsetOnAxis(ap=sidx[:, j:j + 1], axis=0),
                                                Y[:, j, :], None, bounds_check=last_node,
                                                oob_is_err=False).then_inc(a_put[j], 16)

                for h in range(2):
                    gather(0, h)
                with pool.Fori(0, IT - 1) as i:
                    for h in range(2):
                        gather(i + 1, h)
                        scatter(i, h)
                for h in range(2):
                    scatter(IT - 1, h)
                for j in range(U):
                    pool.wait_ge(a_put[j], 16 * IT)

            @block.vector
            def _(dve):
                nc.vector.tensor_copy(nod[:, 0, :], src_i[:, 0:T])
                link(dve, "dve", nc.vector.tensor_copy(nod[:, 1, :], dst_i[:, 0:T]))
                link(dve, "dve", nc.vector.tensor_scalar(tmp, nod, 1.0 / NC_, None, ALU.mult))
                link(dve, "dve", nc.vector.tensor_copy(tmp_i, tmp))
                link(dve, "dve", nc.vector.tensor_copy(hi, tmp_i))
                link(dve, "dve", nc.vector.scalar_tensor_tensor(lo, hi, -float(NC_), nod, ALU.mult, ALU.add))
                for op, lim, sg in ((ALU.is_lt, 0.0, 1.0), (ALU.is_ge, float(NC_), -1.0)):
                    link(dve, "dve", nc.vector.tensor_scalar(tmp, lo, lim, sg, op, ALU.mult))
                    link(dve, "dve", nc.vector.tensor_tensor(hi, hi, tmp, ALU.subtract))
                    link(dve, "dve", nc.vector.scalar_tensor_tensor(lo, tmp, float(NC_), lo, ALU.mult, ALU.add))
                link(dve, "dve", nc.vector.tensor_scalar(tail_m, nod, float(TAIL0), None, ALU.is_ge))
                link(dve, "dve", nc.vector.tensor_scalar(nod, nod, float(TAIL0), None, ALU.subtract))
                link(dve, "dve", nc.vector.tensor_tensor(nod, nod, hi, ALU.subtract))
                link(dve, "dve", nc.vector.tensor_tensor(nod, nod, tail_m, ALU.mult))
                link(dve, "dve", nc.vector.tensor_tensor(hi, hi, nod, ALU.add))
                link(dve, "dve", nc.vector.tensor_scalar(tmp, lo, -1.0, float(NC_), ALU.mult, ALU.add))
                link(dve, "dve", nc.vector.tensor_tensor(tmp, tmp, tail_m, ALU.mult))
                link(dve, "dve", nc.vector.tensor_tensor(lo, lo, tmp, ALU.add))
                link(dve, "dve", nc.vector.tensor_scalar(edge_p[:, 0:1], part_f[:, 0:1], 0.5, None, ALU.is_gt))
                link(dve, "dve", nc.vector.tensor_scalar(edge_p[:, 1:2], part_f[:, 0:1], TE + 0.5, None, ALU.is_lt))
                link(dve, "dve", nc.vector.tensor_tensor(edge_p[:, 0:1], edge_p[:, 0:1], edge_p[:, 1:2], ALU.mult))
                link(dve, "dve", nc.vector.tensor_scalar(edge_p[:, 2:3], edge_p[:, 0:1], 1.0, None, ALU.subtract))
                link(dve, "dve", nc.vector.tensor_scalar(hi, hi, edge_p[:, 0:1], edge_p[:, 2:3], ALU.mult, ALU.add))

                def one_hots(t, h):
                    for j in range(GR * h, GR * h + GR):
                        for k in range(2):
                            nc.vector.tensor_scalar(HA[:, 2 * j + k, :], iota_h[:, 0:P],
                                                    hip[:, k, bass.ds(t + j - GR * h, 1)], None, ALU.is_equal)
                            nc.vector.tensor_scalar(HB[:, 2 * j + k, 0:NCOL], iota_h[:, 0:NCOL],
                                                    lop[:, k, bass.ds(t + j - GR * h, 1)], None,
                                                    ALU.is_equal).then_inc(a_hot, 1)

                link(dve, "dve", nc.vector.memset(hip[:, :, T:TP], 0.0))
                link(dve, "dve", nc.vector.memset(lop[:, :, T:TP], 0.0))
                one_hots(0, 0)
                last_segments(dve, wcol)
                nc.vector.memset(carry[:], 0.0).then_inc(a_ch, 1)
                nc.vector.tensor_copy(lring[:], lastc[:, 0:U]).then_inc(a_lr, 2)
                credit(a_aggT, 2)
                nc.vector.tensor_copy(ridx[:], src_i[:, 0:U]).then_inc(a_idx, 2)
                for j in range(GR):
                    ins = edge_mask(j, j, wcol)
                ins.then_inc(a_mask, 1)
                with dve.Fori(0, IT) as i:
                    for h in range(2):
                        g = 2 * i + h
                        js = slice(GR * h, GR * h + GR)
                        running_sums(dve, g, U * i + GR * h, h, lambda j: G[0:1, j, 0:D],
                                     lambda jj: PS[0:1, CAR, jj, :], carry[:, 0:D], a_row, a_ch)
                        nc.vector.tensor_copy(lring[:, js], lastc[:, bass.ds(U * i + U + GR * h, GR)]).then_inc(a_lr, 1)
                        nc.vector.tensor_copy(ridx[:, js], src_i[:, bass.ds(U * i + U + GR * h, GR)]).then_inc(a_idx, 1)
                        for j in range(GR):
                            ins = edge_mask(U * i + GR * (h + 1) + j, GR * (1 - h) + j, wcol)
                        ins.then_inc(a_mask, 1)
                        dve.wait_ge(a_hist, 2 * (U * i + GR * h) + 2)
                        one_hots(U * i + GR * (h + 1), 1 - h)
                        steady(dve, 16 * i)
                        for q in range(GR * h, GR * h + GR):
                            dve.wait_ge(a_put[q], 16 * i)
                        nc.vector.tensor_copy(sidx[:, js], put_i[:, bass.ds(U * i + GR * h, GR)])
                        dve.wait_ge(a_y, g + 1)
                        nc.vector.tensor_copy(Y[:, js, :], PS[:, SUM + h, :, :]).then_inc(a_yc, 1)
                dve.wait_ge(a_hist, 2 * T + 5)
                nc.vector.tensor_copy(deg[:, 0, :], bank(ACC1, NCOL))
                nc.vector.tensor_copy(deg[:, 1, :], bank(ACC2, NCOL))

            @block.scalar
            def _(act):
                with act.Fori(0, IT) as i:
                    for h in range(2):
                        act.wait_ge(a_aggT, 2 * i + h + 3)
                        act.wait_ge(a_y, 2 * i + h)
                        nc.scalar.copy(HT[:], PS[:, PA + h, :, :]).then_inc(a_aggC, 1)

            @block.tensor
            def _(pe):
                accs = [bank(a, NCOL) for a in (ACC1, ACC2)]
                zb = zcol[:].bitcast(BF16)
                zr = zcol[:, 0:1].bitcast(BF16)[:, 0:1]
                for a in accs:
                    nc.tensor.matmul(a, zb[:, 0:P], zr.to_broadcast([P, NCOL]), start=True, stop=False,
                                     skip_group_check=True).then_inc(a_hist, 1)
                pe.wait_ge(s_w, 16)
                with pe.Fori(0, IT) as i:
                    for h in range(2):
                        g = 2 * i + h
                        for j in range(GR * h, GR * h + GR):
                            if j % GR == 0:
                                pe.wait_ge(a_lr, g + 1)
                                pe.wait_ge(a_ch, OPS * g + 1)
                            pe.wait_ge(a_got[j], 16 * i + 16)
                            nc.tensor.matmul(PS[0:1, CAR, j % GR, :], lring[:, j:j + 1], G[:, j, 0:D],
                                             start=True, stop=True).then_inc(a_row, 1)
                        for j in range(GR * h, GR * h + GR):
                            t = U * i + j
                            if j % GR == 0:
                                pe.wait_ge(a_mask, g + 1)
                            pe.wait_ge(a_ch, OPS * g + j % GR + 2)
                            ins = nc.tensor.matmul(PS[:, PA + h, j % GR, :], G[:, j, 0:D], M[:, j, :],
                                                   start=True, stop=True)
                            if j % GR == GR - 1:
                                ins.then_inc(a_aggT, 1)
                            for k in range(2):
                                s = 2 * j + k
                                pe.wait_ge(a_hot, 2 * t + k + 1)
                                nc.tensor.matmul(accs[k], HA[:, s, :], HB[:, s, 0:NCOL], start=False, stop=False,
                                                 skip_group_check=True).then_inc(a_hist, 1)
                        pe.wait_ge(a_aggC, g + 1)
                        for j in range(GR):
                            ins = nc.tensor.matmul(PS[:, SUM + h, j, :], HT[:, j, :], wmat[:], start=True, stop=True)
                        ins.then_inc(a_y, 1)
                pe.wait_ge(s_w, 16)
                for a in accs:
                    nc.tensor.matmul(a, zb[:, 0:P], zr.to_broadcast([P, NCOL]), start=False, stop=True,
                                     skip_group_check=True).then_inc(a_hist, 1)
                pe.wait_ge(a_ch, OPS * 2 * IT + 1)
                nc.tensor.matmul(PS[0:1, CAR, 0, 0:1], ones[:, 0:1], ones[:, 0:1], start=True, stop=True).then_inc(a_hist, 1)
        end_phase()

        cum = big[:, 0:NCOL]
        has = big[:, 400:400 + NCOL]
        qf = big[:, 800:800 + NCOL]
        qi = big[:, 1200:1200 + NCOL].bitcast(I32)
        rest = big[:, 1600:1600 + NCOL]
        lp_i = big[:, 2000:2000 + NCOL].bitcast(I32)
        before = big[:, 2400:2400 + P]
        upto = big[:, 2600:2600 + P]
        s_rows, s_pre, s_lp, s_lps, s_ns = (sem(n) for n in ("s_rows", "s_pre", "s_lp", "s_lps", "s_ns"))
        EMPTY = TE + 1

        with nc.Block() as block:
            @block.vector
            def _(dve):
                nc.vector.tensor_scalar(nsrc[:], deg[:, 0, :], 1.0, None, ALU.max).then_inc(s_ns, 1)
                link(dve, "dve", nc.vector.tensor_scalar(rin[:], deg[:, 1, :], 1.0, None, ALU.add))
                nc.vector.reciprocal(rin[:], rin[:])
                nc.vector.tensor_reduce(col[:, 0:1], deg[:, 1, 0:NC_], AX.X, ALU.add)
                nc.vector.tensor_scalar(before, iota_f[:, 0:P], part_f[:, 0:1], None, ALU.is_gt)
                nc.vector.tensor_scalar(upto, iota_f[:, 0:P], part_f[:, 0:1], None, ALU.is_ge).then_inc(s_rows, 1)
                dve.wait_ge(s_pre, 1)
                link(dve, "dve", nc.vector.tensor_copy(col[:, 1:3], PS[:, 0, 0, 0:2]))
                nc.vector.tensor_scalar(qf, iota_f[:, 0:NCOL], 0.0, 1.0, ALU.mult, ALU.add)
                link(dve, "dve", nc.vector.tensor_copy(cum[:, NC_:NCOL], col[:, 2:3]))
                link(dve, "dve", nc.vector.tensor_tensor_scan(cum[:, 0:NC_], qf[:, 0:NC_], deg[:, 1, 0:NC_],
                                                             col[:, 1:2], ALU.mult, ALU.add))
                link(dve, "dve", nc.vector.tensor_scalar(cum, cum, 1.0, None, ALU.subtract))
                link(dve, "dve", nc.vector.tensor_scalar(qf, cum, 1.0 / TE, None, ALU.mult))
                link(dve, "dve", nc.vector.tensor_copy(qi, qf))
                link(dve, "dve", nc.vector.tensor_copy(qf, qi))
                link(dve, "dve", nc.vector.scalar_tensor_tensor(rest, qf, -float(TE), cum, ALU.mult, ALU.add))
                link(dve, "dve", nc.vector.tensor_scalar(has, rest, 0.0, None, ALU.is_lt))
                link(dve, "dve", nc.vector.tensor_tensor(qf, qf, has, ALU.subtract))
                link(dve, "dve", nc.vector.tensor_scalar(has, rest, float(TE), None, ALU.is_ge))
                link(dve, "dve", nc.vector.tensor_tensor(qf, qf, has, ALU.add))
                link(dve, "dve", nc.vector.scalar_tensor_tensor(cum, qf, float(P - TE), cum, ALU.mult, ALU.add))
                link(dve, "dve", nc.vector.tensor_scalar(has, deg[:, 1, :], 0.5, None, ALU.is_gt))
                link(dve, "dve", nc.vector.tensor_scalar(cum, cum, 1.0 - EMPTY, None, ALU.add))
                link(dve, "dve", nc.vector.tensor_tensor(cum, cum, has, ALU.mult))
                link(dve, "dve", nc.vector.tensor_scalar(cum, cum, float(EMPTY), None, ALU.add))
                link(dve, "dve", nc.vector.tensor_tensor(cum[0:1, 0:1], cum[0:1, 0:1], has[0:1, 0:1], ALU.subtract))
                link(dve, "dve", nc.vector.tensor_scalar(cum[0:1, 0:1], cum[0:1, 0:1], 1.0, None, ALU.add))
                nc.vector.tensor_copy(lp_i, cum).then_inc(s_lp, 1)
                dve.wait_ge(s_ns, 2)
                link(dve, "dve", nc.vector.reciprocal(nsrc[:], nsrc[:]))
                link(dve, "dve", nc.vector.tensor_tensor(qf, nsrc[:], nsrc[:], ALU.mult))
                link(dve, "dve", nc.vector.tensor_scalar(has, deg[:, 0, :], 1.0, None, ALU.max))
                link(dve, "dve", nc.vector.tensor_tensor(qf, qf, has, ALU.mult))
                link(dve, "dve", nc.vector.tensor_scalar(qf, qf, -0.5, 1.5, ALU.mult, ALU.add))
                nc.vector.tensor_tensor(nsrc[:], nsrc[:], qf, ALU.mult).then_inc(s_ns, 1)

            @block.tensor
            def _(pe):
                pe.wait_ge(s_rows, 1)
                nc.tensor.matmul(PS[:, 0, 0, 0:1], before, col[:, 0:1], start=True, stop=True)
                nc.tensor.matmul(PS[:, 0, 0, 1:2], upto, deg[:, 1, NC_:NCOL], start=True, stop=False)
                nc.tensor.matmul(PS[:, 0, 0, 1:2], ones[:], col[:, 0:1], start=False, stop=True).then_inc(s_pre, 1)

            @block.scalar
            def _(act):
                act.wait_ge(s_ns, 1)
                nc.scalar.sqrt(nsrc[:], nsrc[:]).then_inc(s_ns, 1)

            @block.sync
            def _(sp):
                sp.wait_ge(s_lp, 1)
                with nc.allow_non_contiguous_dma(reason="the tail's column"):
                    sp.dma_start(lastpos[0:TAIL0, :].rearrange("(p n) o -> p (n o)", n=NC_),
                                 lp_i[:, 0:NC_]).then_inc(s_lps, 16)
                    sp.dma_start(lastpos[TAIL0:N, :], lp_i[0:TAIL, NC_:NCOL]).then_inc(s_lps, 16)
                sp.wait_ge(s_lps, 32)
        end_phase()

        def chunk(t, c, w):
            if c is None:
                return t[TAIL0:N, 0:w].unsqueeze(1)
            return t[0:TAIL0, :].rearrange("(p n) f -> p n f", n=NC_)[:, bass.ds(c * NJ, NJ), 0:w]

        def size(c):
            return (TAIL, 1) if c is None else (P, NJ)

        def columns(table, c):
            return table[0:TAIL, NC_:NCOL] if c is None else table[:, bass.ds(c * NJ, NJ)]

        def chunks(eng):
            with eng.Fori(0, CHUNKS // 2) as i:
                for s in range(2):
                    yield 2 * i + s, s, i
            yield None, 0, CHUNKS // 2

        def areas(widths, at=0):
            got = []
            for w in widths:
                got.append([big[:, at + s * NJ * w:at + (s + 1) * NJ * w].rearrange("p (n f) -> p n f", f=w)
                            for s in range(2)])
                at += 2 * NJ * w
            return got

        def ln_stats(dve, V, c, s, n, st):
            np_, nj = size(c)
            for j in range(nj):
                ins = nc.vector.bn_stats(st6[0:np_, j, :], V[0:np_, j, :])
            ins.then_inc(st[s], 1)
            steady(dve, 2 * n + 1)
            dve.wait_ge(st[s], 2 * n + 1)
            for j in range(nj):
                ins = nc.vector.bn_aggr(mv[0:np_, s, j, :], st6[0:np_, j, :])
            ins.then_inc(st[s], 1)

        def ln_scale(pool, c, s, n, st, ps, ready):
            np_, nj = size(c)
            steady(pool, 2 * n + 2)
            pool.wait_ge(st[s], 2 * n + 2)
            nc.gpsimd.tensor_scalar(rs[0:np_, s, 0:nj], mv[0:np_, s, 0:nj, 1], EPS, None, ALU.add)
            nc.gpsimd.tensor_scalar(nb[0:np_, s, 0:nj], mv[0:np_, s, 0:nj, 0], -1.0, None, ALU.mult).then_inc(ps[s], 1)
            pool.wait_ge(ps[s], 2 * n + 1)
            nc.gpsimd.tensor_tensor(rs[0:np_, s, 0:nj], rs[0:np_, s, 0:nj], minus_half[0:np_, 0:nj],
                                    ALU.pow).then_inc(ps[s], 1)
            pool.wait_ge(ps[s], 2 * n + 2)
            nc.gpsimd.tensor_tensor(nb[0:np_, s, 0:nj], nb[0:np_, s, 0:nj], rs[0:np_, s, 0:nj],
                                    ALU.mult).then_inc(ready[s], 1)

        def ln_apply(act, V, X, c, s, n, ready, stored, done):
            np_, nj = size(c)
            steady(act, n + 1, 16 * n)
            act.wait_ge(ready[s], n + 1)
            act.wait_ge(stored[s], 16 * n)
            for j in range(nj):
                ins = nc.scalar.activation(X[0:np_, j, 0:D], V[0:np_, j, :], ACT.Identity,
                                           scale=rs[0:np_, s, j:j + 1], bias=nb[0:np_, s, j:j + 1])
            ins.then_inc(done[s], 1)

        def norm_pass(tag, loads, V, X, xw, into, make_v, extra_x=None, pe_part=None, prelude=None,
                      pool_part=None):
            ld, vr, rdy, done, stored, st, xtra, used, ps = (sems(tag + n, 2) for n in (
                "_ld", "_v", "_rdy", "_x", "_st", "_s", "_xt", "_us", "_ps"))
            pre = sem(tag + "_pre")
            with nc.Block() as block:
                @block.sync
                def _(sp):
                    if prelude:
                        prelude[0](sp, pre)
                    for c, s, n in chunks(sp):
                        np_, nj = size(c)
                        sp.wait_ge(vr[s], n)
                        for buf, t, w in loads:
                            sp.dma_start(buf[s][0:np_, 0:nj, :], chunk(t, c, w)).then_inc(ld[s], 16)

                @block.vector
                def _(dve):
                    if prelude:
                        dve.wait_ge(pre, prelude[1])
                    for c, s, n in chunks(dve):
                        steady(dve, 16 * len(loads) * (n + 1), n)
                        dve.wait_ge(ld[s], 16 * len(loads) * (n + 1))
                        dve.wait_ge(done[s], n)
                        make_v(dve, c, s, n, used, vr)
                        dve.wait_ge(vr[s], n + 1)
                        ln_stats(dve, V[s], c, s, n, st)

                @block.scalar
                def _(act):
                    for c, s, n in chunks(act):
                        np_, nj = size(c)
                        if pe_part:
                            act.wait_ge(used[s], n)
                        ln_apply(act, V[s], X[s], c, s, n, rdy, stored, done)
                        if extra_x:
                            extra_x(act, c, s, n, xtra)
                            act.wait_ge(xtra[s], n + 1)
                        act.wait_ge(done[s], n + 1)
                        act.dma_start(chunk(into, c, xw), X[s][0:np_, 0:nj, 0:xw]).then_inc(stored[s], 16)
                    act.wait_ge(stored[0], 16 * (CHUNKS // 2 + 1))
                    act.wait_ge(stored[1], 16 * (CHUNKS // 2))

                if pe_part:
                    @block.tensor
                    def _(pe):
                        pe_part(pe, done, used)
                @block.gpsimd
                def _(pool):
                    for c, s, n in chunks(pool):
                        ln_scale(pool, c, s, n, st, ps, rdy)
                        if pool_part:
                            pool_part(pool, c, s, n)

        def wide(c_bias, np_, nj):
            return c_bias[0:np_, 0:D].unsqueeze(1).to_broadcast([np_, nj, D])

        XA, YA, XN, V = areas([D, D, D, D])
        m_sum = sem("m_sum")
        a_rel = sems("a_rel", 2)

        def load_bias0(sp, pre):
            sp.dma_start(bias[:], b0.partition_broadcast(P)).then_inc(pre, 16)

        def make_x1(dve, c, s, n, used, vr):
            np_, nj = size(c)
            y, x = YA[s][0:np_, 0:nj, :], XA[s][0:np_, 0:nj, :]
            nc.vector.tensor_tensor(y, y, wide(bias, np_, nj), ALU.add).then_inc(a_rel[s], 1)
            dve.wait_ge(a_rel[s], n + 1)
            nc.vector.scalar_tensor_tensor(V[s][0:np_, 0:nj, :], y, 0.0, x, ALU.max, ALU.add).then_inc(vr[s], 1)

        def sum_nodes(pe, done, used):
            nc.tensor.matmul(PS[:, ACC1, 0, 0:1], zcol[:], ones[:, 0:1], start=True, stop=False,
                             skip_group_check=True).then_inc(m_sum, 1)
            for c, s, n in chunks(pe):
                np_, nj = size(c)
                pe.wait_ge(done[s], n + 1)
                for j in range(nj):
                    ins = nc.tensor.matmul(PS[:, ACC1, 0, 0:1], XN[s][0:np_, j, :], ones[0:np_, 0:1], start=False,
                                           stop=False, skip_group_check=True)
                ins.then_inc(used[s], 1)
            nc.tensor.matmul(PS[:, ACC1, 0, 0:1], zcol[:], ones[:, 0:1], start=False, stop=True,
                             skip_group_check=True).then_inc(m_sum, 1)

        TC = T // (CHUNKS // 2)
        parts = ((0, TC - TC // 2), (TC - TC // 2, TC))
        assert T - TC * (CHUNKS // 2) <= parts[0][1]
        g_id, g_cp = sem("g_id"), sem("g_cp")
        g_got = pool_sems("g_got", TC)

        def found(pool, n, lo, hi):
            steady(pool, 16 * n + 16)
            for j in range(lo, hi):
                pool.wait_ge(g_got[j], 16 * n + 16)
            nc.gpsimd.tensor_copy(gidx[:, bass.ds(TC * n + lo, hi - lo)], PGOT[:, lo:hi]).then_inc(g_cp, 1)

        def positions(pool, c, s, n):
            lo, hi = parts[s] if c is not None else (0, T - TC * n)
            if s == 1:
                found(pool, n, *parts[0])
            steady(pool)
            nc.gpsimd.tensor_copy(PIDX[:, lo:hi], src_i[:, bass.ds(TC * n + lo, hi - lo)]).then_inc(g_id, 1)
            for j in range(lo, hi):
                steady(pool, 2 * n + s + 1)
                if j == lo:
                    pool.wait_ge(g_id, 2 * n + s + 1)
                pool.indirect_dma_start(PGOT[:, j:j + 1], None, lastpos, bass.IndirectOffsetOnAxis(
                    ap=PIDX[:, j:j + 1], axis=0)).then_inc(g_got[j], 16)
            if s == 1 or c is None:
                found(pool, n, lo, hi)
            if c is None:
                pool.wait_ge(g_cp, 2 * n + 1)
                nc.gpsimd.tensor_copy(gidx[:, T:TP], gidx[:, 0:U]).then_inc(g_cp, 1)

        norm_pass("A", [(XA, x0, D), (YA, agg, D)], V, XN, D, x1, make_x1, pe_part=sum_nodes,
                  prelude=(load_bias0, 16), pool_part=positions)
        end_phase()

        zt = big[:, 0:T * D]
        UR, HTR, SQ = (UO, UT), (OT, HT), (OT, HT)
        ZB_, HZB = (PA, PA + 1), (PB, PC)
        l_w, l_wr, l_col, l_base, l_idx, l_mask, l_lr, l_ch, l_row, l_sum, l_ev, l_xt, l_xc, l_yl, l_sq = (
            sem("l_" + n) for n in "w wr col base idx mask lr ch row sum ev xt xc yl sq".split())
        l_got = pool_sems("l_got", U)
        l_tab, l_u, l_h, l_z, l_hz = (sems("l_" + n, 2) for n in "tab u h z hz".split())

        def tab_in(k):
            return tabs[2] if k == 0 else tabs[(k + 1) % 2]

        def tab_out(k):
            return tabs[2] if k < 0 else tabs[k % 2]

        def rounds(l, k):
            return (l * NL + k) * IT

        def group_of(ring, h):
            return ring[:, GR * h:GR * h + GR, :]

        def zt_group(i, h):
            return zt[:, bass.ds((U * i + GR * h) * D, GR * D)].rearrange("p (s f) -> p s f", f=D)

        def l1_store(sp, l, k):
            n0 = rounds(l, k + 1)
            with sp.Fori(0, IT) as i:
                for h in range(2):
                    sp.wait_ge(l_ev, 2 * (n0 + i) + h + 1)
                    sp.dma_start(tab_out(k)[bass.ds((U * i + GR * h) * P, GR * P), :]
                                 .rearrange("(j p) f -> p j f", p=P), group_of(Y, h)).then_inc(l_tab[h], 16)

        def l1_gather(pool, l, k):
            r0 = rounds(l, k)
            steady(pool, 16 * rounds(l, k + 1))
            for h in range(2):
                pool.wait_ge(l_tab[h], 16 * rounds(l, k + 1))
            with pool.Fori(0, IT) as i:
                for j in range(U):
                    g = 2 * (r0 + i) + j // GR
                    steady(pool, g + 1)
                    if j % GR == 0:
                        pool.wait_ge(l_idx, g + 1)
                        pool.wait_ge(l_sum, g + 1)
                    pool.indirect_dma_start(G[:, j, 0:D], None, tab_in(k), bass.IndirectOffsetOnAxis(
                        ap=ridx[:, j:j + 1], axis=0)).then_inc(l_got[j], 16)

        def start_dve(dve):
            with dve.Fori(0, IT) as i:
                for h in range(2):
                    for j in range(GR * h, GR * h + GR):
                        nc.vector.scalar_tensor_tensor(zt[:, bass.ds((U * i + j) * D, D)], row_a[:],
                                                       isnode0[:, bass.ds(U * i + j, 1)],
                                                       bias[:], ALU.mult, ALU.add)
                    steady(dve, 16 * i)
                    dve.wait_ge(l_tab[h], 16 * i)
                    for j in range(GR * h, GR * h + GR):
                        ins = nc.vector.scalar_tensor_tensor(Y[:, j, :], row_b[:],
                                                             isnode0[:, bass.ds(U * i + j, 1)],
                                                             bias[:], ALU.mult, ALU.add)
                    ins.then_inc(l_ev, 1)

        def turn_act(act, l):
            steady(act, 2 * IT * l)
            act.wait_ge(l_xc, 2 * IT * l)
            with act.Fori(0, IT) as i:
                f = IT * (l - 1) + i
                for h in range(2):
                    steady(act, f)
                    act.wait_ge(l_h[h], f)
                    nc.scalar.activation(UR[h][:], zt_group(i, h), ACT.Identity, scale=scol[:, 0:1],
                                         bias=tcol[:, 0:1]).then_inc(l_u[h], 1)

        def turn_dve(dve, l):
            with dve.Fori(0, IT) as i:
                f = IT * (l - 1) + i
                for h in range(2):
                    dve.wait_ge(l_u[h], f + 1)
                    dve.wait_ge(l_hz[h], f)
                    nc.vector.scalar_tensor_tensor(HTR[h][:], UR[h][:], 0.01, UR[h][:], ALU.mult,
                                                   ALU.max).then_inc(l_h[h], 1)
                for h in range(2):
                    dve.wait_ge(l_z[h], f + 1)
                    nc.vector.tensor_tensor(zt_group(i, h), PS[:, ZB_[h], :, :], wide(bias, P, GR), ALU.add)
                    dve.wait_ge(l_hz[h], f + 1)
                    dve.wait_ge(l_tab[h], 16 * (rounds(l, 0) + i))
                    nc.vector.tensor_tensor(group_of(Y, h), PS[:, HZB[h], :, :], wide(bias, P, GR),
                                            ALU.add).then_inc(l_ev, 1)

        def turn_pe(pe, l):
            with pe.Fori(0, IT) as i:
                for h in range(2):
                    pe.wait_ge(l_h[h], IT * (l - 1) + i + 1)
                    for j in range(GR):
                        ins = nc.tensor.matmul(PS[:, ZB_[h], j, :], HTR[h][:, j, :], wmat[:], start=True, stop=True)
                    ins.then_inc(l_z[h], 1)
                    for j in range(GR):
                        ins = nc.tensor.matmul(PS[:, HZB[h], j, :], HTR[h][:, j, :], wplus[:], start=True, stop=True)
                    ins.then_inc(l_hz[h], 1)

        def l1_dve(dve, l, k):
            r0 = rounds(l, k)
            last = k == NL - 1
            with dve.Fori(0, IT) as i:
                for h in range(2):
                    g = 2 * (r0 + i) + h
                    running_sums(dve, g, U * i + GR * h, h, lambda j: G[0:1, j, 0:D],
                                 lambda jj: PS[0:1, CAR, jj, :], carry[:, 0:D], l_row, l_ch)
                    nc.vector.tensor_copy(lring[:, GR * h:GR * h + GR],
                                          lastc[:, bass.ds(U * i + U + GR * h, GR)]).then_inc(l_lr, 1)
                    nc.vector.tensor_copy(ridx[:, GR * h:GR * h + GR],
                                          gidx[:, bass.ds(U * i + U + GR * h, GR)]).then_inc(l_idx, 1)
                    for j in range(GR):
                        ins = edge_mask(U * i + GR * (h + 1) + j, GR * (1 - h) + j, wccol)
                    ins.then_inc(l_mask, 1)
                    dve.wait_ge(l_sum, g + 3)
                    if last:
                        nc.vector.tensor_copy(group_of(Y, h), PS[:, SUM + h, :, :]).then_inc(l_yl, 1)
                        dve.wait_ge(l_yl, 2 * (IT * l + i) + h + 1)
                        nc.vector.tensor_tensor(SQ[h][:], group_of(Y, h), group_of(Y, h), ALU.mult).then_inc(l_sq, 1)
                    else:
                        dve.wait_ge(l_tab[h], 16 * (rounds(l, k + 1) + i))
                        nc.vector.tensor_tensor(group_of(Y, h), PS[:, SUM + h, :, :], zt_group(i, h),
                                                ALU.add).then_inc(l_ev, 1)

        def last_act(act, l):
            with act.Fori(0, IT) as i:
                for h in range(2):
                    steady(act, 2 * (IT * l + i) + h + 1)
                    act.wait_ge(l_xt, 2 * (IT * l + i) + h + 1)
                    nc.scalar.copy(zt_group(i, h), PS[:, PA + h, :, :]).then_inc(l_xc, 1)

        def node_sums(pe, tile, h):
            for j in range(GR):
                here = ends[:, bass.ds(GR + tile + j, 1), :].rearrange("p a b -> p (a b)")
                nc.tensor.matmul(PS[:, ACC1, 0, 0:2], Y[:, GR * h + j, :], here, start=False, stop=False,
                                 skip_group_check=True)
                nc.tensor.matmul(PS[:, ACC2, 0, 0:2], SQ[h][:, j, :], here, start=False, stop=False,
                                 skip_group_check=True)

        def l1_pe(pe, l, k):
            r0 = rounds(l, k)
            last = k == NL - 1
            with pe.Fori(0, IT) as i:
                for h in range(2):
                    g = 2 * (r0 + i) + h
                    gl = 2 * (IT * l + i) + h
                    js = range(GR * h, GR * h + GR)
                    for j in js:
                        if j % GR == 0:
                            pe.wait_ge(l_lr, g + 1)
                            pe.wait_ge(l_ch, OPS * g + 1)
                        pe.wait_ge(l_got[j], 16 * (r0 + i) + 16)
                        nc.tensor.matmul(PS[0:1, CAR, j % GR, :], lring[:, j:j + 1], G[:, j, 0:D],
                                         start=True, stop=True).then_inc(l_row, 1)
                    for j in js:
                        if j % GR == 0:
                            pe.wait_ge(l_mask, g + 1)
                            if last and h == 0:
                                pe.wait_ge(l_xc, 2 * (IT * l + i))
                        pe.wait_ge(l_ch, OPS * g + j % GR + 2)
                        if last:
                            ins = nc.tensor.matmul(PS[:, PA + h, j % GR, :], G[:, j, 0:D], M[:, j, :],
                                                   start=True, stop=True)
                            if j % GR == GR - 1:
                                ins.then_inc(l_xt, 1)
                        ins = nc.tensor.matmul(PS[:, SUM + h, j % GR, :], M[:, j, :], G[:, j, 0:D],
                                               start=True, stop=True)
                    ins.then_inc(l_sum, 1)
                    if last:
                        pe.wait_ge(l_sq, gl)
                        node_sums(pe, U * i + GR * (h - 1), 1 - h)
            if last:
                pe.wait_ge(l_sq, 2 * IT * (l + 1))
                node_sums(pe, T - GR, 1)

        l_acc, l_m = sem("l_acc"), sem("l_m")
        NCOEF = 7
        l_pw = sem("l_pw")

        def inverse_deviation(pool, l):
            steady(pool, NCOEF * (l - 1) + 4)
            pool.wait_ge(l_col, NCOEF * (l - 1) + 4)
            nc.gpsimd.tensor_tensor(col[:, 3:4], col[:, 1:2], minus_half[:, 0:1], ALU.pow).then_inc(l_pw, 1)


        def coefficients(dve, l):
            v = NCOEF * (l - 1)
            dve.wait_ge(l_acc, 4 * (l - 1) + 4)
            nc.vector.tensor_scalar(col[:, 0:1], PS[:, ACC1, 0, 0:1], 1.0 / N, None, ALU.mult)
            nc.vector.tensor_copy(rcol[:], PS[:, ACC1, 0, 1:2])
            nc.vector.tensor_scalar(col[:, 1:2], PS[:, ACC2, 0, 0:1], 1.0 / N, None, ALU.mult).then_inc(l_col, 1)
            dve.wait_ge(l_col, v + 1)
            nc.vector.tensor_tensor(col[:, 2:3], col[:, 0:1], col[:, 0:1], ALU.mult).then_inc(l_col, 1)
            dve.wait_ge(l_col, v + 2)
            nc.vector.tensor_tensor(col[:, 1:2], col[:, 1:2], col[:, 2:3], ALU.subtract).then_inc(l_col, 1)
            dve.wait_ge(l_col, v + 3)
            nc.vector.tensor_scalar(col[:, 1:2], col[:, 1:2], EPS, None, ALU.add).then_inc(l_col, 1)
            dve.wait_ge(l_pw, l)
            nc.vector.tensor_tensor(scol[:], col[:, 3:4], gb[:, 0, bass.ds(l - 1, 1)], ALU.mult).then_inc(l_col, 1)
            dve.wait_ge(l_col, v + 5)
            nc.vector.tensor_tensor(col[:, 2:3], col[:, 0:1], scol[:], ALU.mult).then_inc(l_col, 1)
            dve.wait_ge(l_col, v + 6)
            nc.vector.tensor_tensor(tcol[:], gb[:, 1, bass.ds(l - 1, 1)], col[:, 2:3], ALU.subtract).then_inc(l_col, 1)
            dve.wait_ge(l_col, v + 7)

        def over_layers(eng, program):
            program(0)
            with eng.Fori(1, NL) as l:
                program(l)

        s_gb, l_rb, l_fin = sem("s_gb"), sem("l_rb"), sem("l_fin")
        with nc.Block() as block:
            @block.sync
            def _(sp):
                with nc.allow_non_contiguous_dma(reason="ten short columns"):
                    sp.dma_start(gb[:, 0, :], gamma.rearrange("l f -> f l")).then_inc(s_gb, 16)
                    sp.dma_start(gb[:, 1, :], beta.rearrange("l f -> f l")).then_inc(s_gb, 16)

                def layer(l):
                    if isinstance(l, int):
                        wl, bl = w1[l], b1[l]
                    else:
                        wl = w1.rearrange("l i o -> (l i) o")[bass.ds(l * D, D), :]
                        bl = b1[bass.ds(l, 1), :].rearrange("a f -> (a f)")
                    sp.wait_ge(l_ev, 2 * NL * IT * l)
                    sp.dma_start(wmat[:], wl).then_inc(l_w, 16)
                    sp.dma_start(bias[:], bl.partition_broadcast(P)).then_inc(l_w, 16)
                    for k in range(-1, NL - 1):
                        l1_store(sp, l, k)
                over_layers(sp, layer)
                for h in range(2):
                    sp.wait_ge(l_tab[h], 16 * NL * NL * IT)

            @block.gpsimd
            def _(pool):
                def layer(l):
                    if not isinstance(l, int):
                        inverse_deviation(pool, l)
                    for k in range(NL):
                        l1_gather(pool, l, k)
                over_layers(pool, layer)
                inverse_deviation(pool, NL)

            @block.vector
            def _(dve):
                last_segments(dve, wccol)
                nc.vector.memset(carry[:], 0.0).then_inc(l_ch, 1)
                credit(l_sum, 2)
                nc.vector.tensor_copy(lring[:], lastc[:, 0:U]).then_inc(l_lr, 2)
                nc.vector.tensor_copy(ridx[:], gidx[:, 0:U]).then_inc(l_idx, 2)
                for j in range(GR):
                    ins = edge_mask(j, j, wccol)
                ins.then_inc(l_mask, 1)
                dve.wait_ge(s_gb, 32)

                def layer(l):
                    if isinstance(l, int):
                        link(dve, "dve", nc.vector.tensor_scalar(mcol[:], PS[:, ACC1, 0, 0:1], 1.0 / N, None, ALU.mult))
                        nc.vector.tensor_scalar(HT[:, 0, :], ones[:], mcol[:, 0:1], None, ALU.mult).then_inc(l_base, 1)
                        dve.wait_ge(l_w, 32)
                        nc.vector.tensor_tensor(wplus[:], wmat[:], ident[:], ALU.add).then_inc(l_wr, 1)
                        dve.wait_ge(l_m, 2)
                        nc.vector.tensor_copy(row_a[:], PS[:, PB, 0, :])
                        link(dve, "dve", nc.vector.tensor_copy(row_b[:], PS[:, PB, 1, :]))
                        link(dve, "dve", nc.vector.memset(HT[:], 0.0))
                        start_dve(dve)
                    else:
                        coefficients(dve, l)
                        dve.wait_ge(l_w, 32 * l + 32)
                        nc.vector.tensor_tensor(wplus[:], wmat[:], ident[:], ALU.add).then_inc(l_wr, 1)
                        turn_dve(dve, l)
                    for k in range(NL):
                        l1_dve(dve, l, k)
                over_layers(dve, layer)
                coefficients(dve, NL)
                link(dve, "dve", nc.vector.tensor_tensor(col[:, 4:5], rcol[:], scol[:], ALU.mult))
                link(dve, "dve", nc.vector.tensor_tensor(col[:, 4:5], col[:, 4:5], tcol[:], ALU.add))
                link(dve, "dve", nc.vector.tensor_scalar(col[:, 5:6], col[:, 4:5], 0.01, None, ALU.mult))
                link(dve, "dve", nc.vector.tensor_tensor(col[:, 4:5], col[:, 4:5], col[:, 5:6], ALU.max))
                nc.vector.tensor_scalar(HT[:, 0, :], ones[:], col[:, 4:5], None, ALU.mult).then_inc(l_rb, 1)
                dve.wait_ge(l_fin, 1)
                nc.vector.tensor_copy(row_a[:], PS[:, PB, 0, :])

            @block.scalar
            def _(act):
                def layer(l):
                    if not isinstance(l, int):
                        steady(act, NCOEF * l)
                        act.wait_ge(l_col, NCOEF * l)
                        turn_act(act, l)
                    last_act(act, l)
                over_layers(act, layer)

            @block.tensor
            def _(pe):
                def layer(l):
                    if isinstance(l, int):
                        pe.wait_ge(l_wr, 1)
                        pe.wait_ge(l_base, 1)
                        nc.tensor.matmul(PS[:, PB, 0, :], HT[:, 0, :], wmat[:], start=True, stop=True).then_inc(l_m, 1)
                        nc.tensor.matmul(PS[:, PB, 1, :], HT[:, 0, :], wplus[:], start=True,
                                         stop=True).then_inc(l_m, 1)
                    else:
                        steady(pe, l + 1)
                        pe.wait_ge(l_wr, l + 1)
                        turn_pe(pe, l)
                    for k in range(NL):
                        if k == NL - 1:
                            for a in (ACC1, ACC2):
                                nc.tensor.matmul(PS[:, a, 0, 0:2], zcol[:], ones[:, 0:2], start=True, stop=False,
                                                 skip_group_check=True).then_inc(l_acc, 1)
                        l1_pe(pe, l, k)
                    for a in (ACC1, ACC2):
                        nc.tensor.matmul(PS[:, a, 0, 0:2], zcol[:], ones[:, 0:2], start=False, stop=True,
                                         skip_group_check=True).then_inc(l_acc, 1)
                over_layers(pe, layer)
                pe.wait_ge(l_rb, 1)
                nc.tensor.matmul(PS[:, PB, 0, :], HT[:, 0, :], ident[:], start=True, stop=True).then_inc(l_fin, 1)
        end_phase()

        XB, VB, X2 = areas([D, D, D + 1])

        def make_x2(dve, c, s, n, used, vr):
            np_, nj = size(c)
            x = XB[s][0:np_, 0:nj, :]
            nc.vector.tensor_tensor(VB[s][0:np_, 0:nj, :], x, wide(row_a, np_, nj), ALU.add).then_inc(vr[s], 1)

        def norm_column(act, c, s, n, xtra):
            np_, nj = size(c)
            steady(act)
            nc.scalar.copy(X2[s][0:np_, 0:nj, D], columns(nsrc, c)).then_inc(xtra[s], 1)

        norm_pass("B", [(XB, x1, D)], VB, X2, D + 1, x2n, make_x2, extra_x=norm_column)
        end_phase()

        CW = 2 * D
        CMB = big[:, 0:U * CW].rearrange("p (s f) -> p s f", f=CW)
        at = U * CW
        AT, ET, T1, T2 = (big[:, at + 512 * k:at + 512 * k + 512].rearrange("p (s f) -> p s f", f=D) for k in range(4))
        at += 2048
        W2, WE, B2, BE = (big[:, at + D * k:at + D * k + D] for k in range(4))
        cnt, root, inv = (big[:, at + 512 + 16 * k:at + 520 + 16 * k] for k in range(3))
        at += 600
        one_e = big[:, at:at + T]
        in_cnt = big[0:1, at + T:at + 2 * T]
        loc_cnt = big[0:1, at + 2 * T:at + 3 * T]
        SUME, SUMX, CNT = 2, 3, 4
        c_w, c_one, c_lc, c_idx, c_lr, c_mask, c_ch, c_row, c_sum, c_evac, c_cnt, c_root, c_inv, c_wm, c_t, c_y = (
            sem("c_" + n) for n in "w one lc idx lr mask ch row sum evac cnt root inv wm t y".split())
        c_got, c_put, c_ea = pool_sems("c_got", U), pool_sems("c_put", U), sems("c_ea", 2)

        def plain_mask(t, slot):
            return nc.vector.tensor_scalar(M[:, slot, :], keyrow[:, bass.ds(t * P, P)], keycol[:, bass.ds(t, 1)],
                                           None, ALU.is_equal)

        with nc.Block() as block:
            @block.sync
            def _(sp):
                sp.dma_start(W2, w2).then_inc(c_w, 16)
                sp.dma_start(WE, we).then_inc(c_w, 16)
                sp.dma_start(BE, be.partition_broadcast(P)).then_inc(c_w, 16)
                sp.wait_ge(c_one, 1)
                with sp.Fori(0, IT) as i:
                    for h in range(2):
                        sp.wait_ge(c_ch, OPS * (2 * i + h))
                        sp.dma_start(CMB[1:TE + 1, GR * h:GR * h + GR, D:2 * D],
                                     ea[bass.ds((U * i + GR * h) * TE, GR * TE), :]
                                     .rearrange("(j p) f -> p j f", p=TE)).then_inc(c_ea[h], 16)

            @block.gpsimd
            def _(pool):
                last_node = pool.to_reg(N - 1)

                def gather(i, h):
                    g = 2 * i + h
                    for j in range(GR * h, GR * h + GR):
                        steady(pool, g + 1)
                        if j % GR == 0:
                            pool.wait_ge(c_idx, g + 1)
                        pool.indirect_dma_start(G[:, j, 0:D + 1], None, x2n, bass.IndirectOffsetOnAxis(
                            ap=ridx[:, j:j + 1], axis=0)).then_inc(c_got[j], 16)

                def scatter(i, h):
                    for j in range(GR * h, GR * h + GR):
                        steady(pool, 2 * i + h + 1)
                        if j % GR == 0:
                            pool.wait_ge(c_y, 2 * i + h + 1)
                        pool.indirect_dma_start(agg, bass.IndirectOffsetOnAxis(ap=sidx[:, j:j + 1], axis=0),
                                                Y[:, j, :], None, bounds_check=last_node,
                                                oob_is_err=False).then_inc(c_put[j], 16)

                for h in range(2):
                    gather(0, h)
                with pool.Fori(0, IT - 1) as i:
                    for h in range(2):
                        gather(i + 1, h)
                        scatter(i, h)
                for h in range(2):
                    scatter(IT - 1, h)
                for j in range(U):
                    pool.wait_ge(c_put[j], 16 * IT)

            @block.vector
            def _(dve):
                nc.vector.memset(CMB, 1.0).then_inc(c_one, 1)
                last_segments(dve, None)
                nc.vector.memset(carry[:], 0.0).then_inc(c_ch, 1)
                nc.vector.memset(in_cnt[:, 0:1], 0.0).then_inc(c_lc, 1)
                dve.wait_ge(c_lc, 2)
                link(dve, "dve", nc.vector.tensor_copy(loc_cnt, bank(CNT, T)[0:1, :]))
                link(dve, "dve", nc.vector.tensor_tensor_scan(loc_cnt, whole[:, 0:T], loc_cnt, 0.0, ALU.mult, ALU.add))
                link(dve, "dve", nc.vector.tensor_copy(in_cnt[:, 1:T], loc_cnt[:, 0:T - 1]))
                link(dve, "dve", nc.vector.memset(one_e, 1.0))
                link(dve, "dve", nc.vector.tensor_copy(one_e[0:1, :], in_cnt))
                nc.vector.tensor_copy(lring[:], lastc[:, 0:U]).then_inc(c_lr, 2)
                nc.vector.tensor_copy(ridx[:], src_i[:, 0:U]).then_inc(c_idx, 2)
                for j in range(GR):
                    ins = plain_mask(j, j)
                ins.then_inc(c_mask, 1)
                dve.wait_ge(c_w, 48)
                dve.wait_ge(c_one, 1)

                def normed(i, h):
                    g = 2 * i + h
                    js = slice(GR * h, GR * h + GR)
                    steady(dve, 16 * i + 16)
                    for j in range(GR * h, GR * h + GR):
                        dve.wait_ge(c_got[j], 16 * i + 16)
                        nc.vector.tensor_scalar(CMB[:, j, 0:D], G[:, j, 0:D], G[:, j, D:D + 1], None,
                                                ALU.mult).then_inc(c_one, 1)
                    nc.vector.tensor_copy(ridx[:, js], src_i[:, bass.ds(U * i + U + GR * h, GR)]).then_inc(c_idx, 1)

                def summed(i, h):
                    g = 2 * i + h
                    js = slice(GR * h, GR * h + GR)
                    running_sums(dve, g, U * i + GR * h, h, lambda j: CMB[0:1, j, :]
                                 .rearrange("p (k f) -> p k f", k=2),
                                 lambda jj: PS[0:1, 0:2, jj, :], carry[:].rearrange("p (k f) -> p k f", k=2),
                                 c_row, c_ch)
                    nc.vector.tensor_copy(lring[:, js], lastc[:, bass.ds(U * i + U + GR * h, GR)]).then_inc(c_lr, 1)
                    for j in range(GR):
                        ins = plain_mask(U * i + GR * (h + 1) + j, GR * (1 - h) + j)
                    ins.then_inc(c_mask, 1)

                def finished(i, h):
                    g = 2 * i + h
                    js = slice(GR * h, GR * h + GR)
                    dve.wait_ge(c_sum, g + 1)
                    nc.vector.tensor_copy(cnt[:, 0:GR], PS[:, CNT + h, 0, 0:GR])
                    nc.vector.tensor_scalar(root[:, 0:GR], PS[:, CNT + h, 0, 0:GR], 1.0, None, ALU.max).then_inc(c_cnt, 1)
                    dve.wait_ge(c_root, g + 1)
                    nc.vector.reciprocal(inv, root).then_inc(c_inv, 1)
                    dve.wait_ge(c_wm, g + 1)
                    for j in range(GR):
                        nc.vector.scalar_tensor_tensor(T1[:, j, :], BE, cnt[:, j:j + 1], PS[:, PC, j, :],
                                                       ALU.mult, ALU.add)
                    dve.wait_ge(c_inv, g + 1)
                    for j in range(GR):
                        ins = nc.vector.tensor_scalar(T2[:, j, :], PS[:, 6, j, :], inv[:, GR + j:GR + j + 1], None,
                                                      ALU.mult)
                    ins.then_inc(c_t, 1)
                    steady(dve, 16 * i)
                    for j in range(GR * h, GR * h + GR):
                        dve.wait_ge(c_put[j], 16 * i)
                    nc.vector.tensor_copy(sidx[:, js], put_i[:, bass.ds(U * i + GR * h, GR)])
                    dve.wait_ge(c_t, g + 1)
                    for j in range(GR):
                        ins = nc.vector.scalar_tensor_tensor(Y[:, GR * h + j, :], T1[:, j, :], inv[:, j:j + 1],
                                                             T2[:, j, :], ALU.mult, ALU.add)
                    ins.then_inc(c_y, 1)

                def to_sums(i, h):
                    normed(i, h)
                    summed(i, h)
                two_stages(dve, to_sums, finished)

            @block.scalar
            def _(act):
                with act.Fori(0, IT) as i:
                    for h in range(2):
                        g = 2 * i + h
                        act.wait_ge(c_sum, g + 1)
                        act.wait_ge(c_wm, g)
                        nc.scalar.copy(AT, PS[:, SUMX, :, :])
                        nc.scalar.copy(ET, PS[:, SUME, :, :]).then_inc(c_evac, 1)
                        act.wait_ge(c_cnt, g + 1)
                        nc.scalar.sqrt(root[:, GR:2 * GR], root[:, 0:GR]).then_inc(c_root, 1)

            @block.tensor
            def _(pe):
                pe.wait_ge(c_lc, 1)
                nc.tensor.matmul(bank(CNT, T)[0:1, :], ones[:, 0:1], lastc[:, 0:T], start=True, stop=True).then_inc(c_lc, 1)
                pe.wait_ge(c_w, 48)

                def last_sums(i, h):
                    g = 2 * i + h
                    for j in range(GR * h, GR * h + GR):
                        if j % GR == 0:
                            pe.wait_ge(c_lr, g + 1)
                            pe.wait_ge(c_ch, OPS * g + 1)
                            pe.wait_ge(c_ea[h], 16 * i + 16)
                        pe.wait_ge(c_one, U * i + j + 2)
                        for k in range(2):
                            ins = nc.tensor.matmul(PS[0:1, k, j % GR, :], lring[:, j:j + 1],
                                                   CMB[:, j, k * D:k * D + D], start=True, stop=True)
                        ins.then_inc(c_row, 1)

                def sums(i, h):
                    g = 2 * i + h
                    for j in range(GR * h, GR * h + GR):
                        if j % GR == 0:
                            pe.wait_ge(c_mask, g + 1)
                            pe.wait_ge(c_evac, g)
                        pe.wait_ge(c_ch, OPS * g + j % GR + 2)
                        nc.tensor.matmul(PS[:, SUMX, j % GR, :], CMB[:, j, 0:D], M[:, j, :], start=True, stop=True)
                        nc.tensor.matmul(PS[:, SUME, j % GR, :], CMB[:, j, D:CW], M[:, j, :], start=True, stop=True)
                        ins = nc.tensor.matmul(PS[:, CNT + h, 0, j % GR:j % GR + 1], M[:, j, :],
                                               one_e[:, bass.ds(U * i + j, 1)], start=True, stop=True)
                    ins.then_inc(c_sum, 1)

                def products(i, h):
                    g = 2 * i + h
                    pe.wait_ge(c_evac, g + 1)
                    pe.wait_ge(c_y, g)
                    for j in range(GR):
                        nc.tensor.matmul(PS[:, 6, j, :], AT[:, j, :], W2, start=True, stop=True)
                        ins = nc.tensor.matmul(PS[:, PC, j, :], ET[:, j, :], WE, start=True, stop=True)
                    ins.then_inc(c_wm, 1)
                two_stages(pe, last_sums, products, sums)
        end_phase()

        DX = D + 2 * HEADS
        X2L, YL, VC, X3, O3 = areas([D + 1, D, D, D, DX])
        at = 2 * NJ * (4 * D + 1 + DX)
        W2 = big[:, at:at + D]
        B2 = big[:, at + D:at + 2 * D]
        LW = big[:, at + 2 * D:at + 5 * D].rearrange("p (b i) -> p b i", b=3)
        W3 = big[:, at + 5 * D:at + 6 * D]
        W3X = big[:, at + 6 * D:at + 6 * D + DX]
        B3X = big[:, at + 8 * D:at + 8 * D + DX]
        IDA = big[:, at + 10 * D:at + 10 * D + DX]
        B3C = big[:, at + 12 * D:at + 13 * D]
        at += 13 * D
        AC = big[:, at:at + 9].rearrange("p (k b) -> p k b", k=3)
        CF = big[:, at + 16:at + 19]
        A3 = big[:, at + 32:at + 35]
        R1 = big[:, at + 40:at + 40 + NJ]
        at += 60
        BT = big[:, at:at + NJ * D].rearrange("p (j f) -> p j f", f=D)
        d_w, d_p, d_m, d_ready, d_r1, d_r1b = (sem("d_" + n) for n in "w p m ready r1 r1b".split())
        d_ld, d_x2y, d_st, d_ps, d_rdy, d_x3, d_o, d_sx, d_so = (sems("dd_" + n, 2) for n in (
            "ld x2y st ps rdy x3 o sx so".split()))
        d_t, d_tc, d_z, d_v1, d_u, d_uc, d_q, d_oc = (sem("d_" + n) for n in "t tc z v1 u uc q oc".split())
        TR, UB = (HT, OT), (5, CAR)
        QA, QB = -(-NJ // 4), -(-NJ // 3)

        def groups(c, w):
            nj = size(c)[1]
            return [(q, range(w * q, min(nj, w * q + w))) for q in range(-(-nj // w))]

        def before_chunk(c, per):
            return per * (CHUNKS if c is None else c)

        def lagged(eng, one, two):
            one(0, 0, 0)
            with eng.Fori(0, CHUNKS // 2 - 1) as i:
                for s in range(2):
                    one(2 * i + s + 1, 1 - s, i + s)
                    two(2 * i + s, s, i)
            m = CHUNKS // 2 - 1
            one(CHUNKS - 1, 1, m)
            two(CHUNKS - 2, 0, m)
            one(None, 0, m + 1)
            two(CHUNKS - 1, 1, m)
            two(None, 0, m + 1)

        with nc.Block() as block:
            @block.sync
            def _(sp):
                with nc.allow_non_contiguous_dma(reason="short columns"):
                    sp.dma_start(W2, w2).then_inc(d_w, 16)
                    sp.dma_start(B2, b2.partition_broadcast(P)).then_inc(d_w, 16)
                    sp.dma_start(LW, linw.rearrange("b o i -> o b i")).then_inc(d_w, 16)
                    sp.dma_start(CF, coef.partition_broadcast(P)).then_inc(d_w, 16)
                    sp.dma_start(AC[:, 0, :], asrc.rearrange("b q h c -> (q h c) b")).then_inc(d_w, 16)
                    sp.dma_start(AC[:, 1, :], adst.rearrange("b q h c -> (q h c) b")).then_inc(d_w, 16)
                    sp.dma_start(AC[:, 2, :], linb.rearrange("b o -> o b")).then_inc(d_w, 16)
                for c, s, n in chunks(sp):
                    np_, nj = size(c)
                    sp.wait_ge(d_t, before_chunk(c, QA))
                    sp.wait_ge(d_st[s], 2 * n)
                    sp.dma_start(X2L[s][0:np_, 0:nj, :], chunk(x2n, c, D + 1)).then_inc(d_ld[s], 16)
                    sp.dma_start(YL[s][0:np_, 0:nj, :], chunk(agg, c, D)).then_inc(d_ld[s], 16)

            @block.gpsimd
            def _(pool):
                pool.wait_ge(d_ready, 1)

                def add(c, s, n):
                    np_, nj = size(c)
                    y, b = YL[s][0:np_, 0:nj, :], BT[0:np_, 0:nj, :]
                    steady(pool, 32 * n + 32)
                    nc.gpsimd.tensor_copy(R1[0:np_, 0:nj], columns(nsrc, c)).then_inc(d_r1, 1)
                    pool.wait_ge(d_ld[s], 32 * n + 32)
                    nc.gpsimd.tensor_tensor(y, y, X2L[s][0:np_, 0:nj, 0:D], ALU.add).then_inc(d_x2y[s], 1)
                    steady(pool, 2 * n + s + 1)
                    pool.wait_ge(d_r1, 2 * n + s + 1)
                    nc.gpsimd.tensor_tensor(b, wide(B2, np_, nj), R1[0:np_, 0:nj].unsqueeze(2)
                                            .to_broadcast([np_, nj, D]), ALU.mult).then_inc(d_r1b, 1)
                    steady(pool, 2 * n + s + 1, 2 * n + 1)
                    pool.wait_ge(d_r1b, 2 * n + s + 1)
                    pool.wait_ge(d_x2y[s], 2 * n + 1)
                    nc.gpsimd.tensor_tensor(y, y, b, ALU.add).then_inc(d_x2y[s], 1)

                def scale(c, s, n):
                    ln_scale(pool, c, s, n, d_st, d_ps, d_rdy)
                lagged(pool, add, scale)

            @block.vector
            def _(dve):
                credit(d_t, QA)
                dve.wait_ge(d_w, 16 * 7)
                nc.vector.tensor_scalar(W3, LW[:, 0, :], CF[:, 0:1], None, ALU.mult)
                link(dve, "dve", nc.vector.tensor_scalar(A3, AC[:, :, 0], CF[:, 0:1], None, ALU.mult))
                for b in (1, 2):
                    nc.vector.scalar_tensor_tensor(W3, LW[:, b, :], CF[:, b:b + 1], W3, ALU.mult, ALU.add)
                    link(dve, "dve", nc.vector.scalar_tensor_tensor(A3, AC[:, :, b], CF[:, b:b + 1], A3,
                                                                    ALU.mult, ALU.add))
                nc.vector.tensor_scalar(B3C, ones[:], A3[:, 2:3], None, ALU.mult)
                nc.vector.tensor_copy(IDA[:, 0:D], ident[:])
                nc.vector.tensor_scalar(nsrc[:], rin[:], 1.0, None, ALU.add)
                link(dve, "dve", nc.vector.memset(IDA[:, D:DX], 0.0))
                for k in range(2):
                    for q in range(HEADS):
                        r = slice(CH * q, CH * q + CH)
                        link(dve, "dve", nc.vector.tensor_copy(IDA[r, D + HEADS * k + q:D + HEADS * k + q + 1],
                                                               A3[r, k:k + 1]))
                nc.vector.tensor_copy(col[:, 6:7], ones[:, 0:1]).then_inc(d_p, 1)
                dve.wait_ge(d_m, 1)
                nc.vector.tensor_copy(W3X, bank(PA, DX))
                nc.vector.tensor_copy(B3X, bank(PA + 1, DX)).then_inc(d_ready, 1)
                dve.wait_ge(d_ready, 1)

                def rows(c, s, n):
                    np_, nj = size(c)
                    steady(dve, n, 2 * n + 2)
                    dve.wait_ge(d_x3[s], n)
                    dve.wait_ge(d_x2y[s], 2 * n + 2)
                    for q, js in groups(c, 4):
                        dve.wait_ge(d_z, before_chunk(c, QA) + q + 1)
                        for j in js:
                            rc = rin[0:np_, NC_:NCOL] if c is None else rin[:, bass.ds(c * NJ + j, 1)]
                            ins = nc.vector.scalar_tensor_tensor(VC[s][0:np_, j, :], PS[0:np_, SUM + q % 2, j % 4, :],
                                                                 rc, YL[s][0:np_, j, :], ALU.mult, ALU.add)
                        ins.then_inc(d_v1, 1)
                    dve.wait_ge(d_v1, before_chunk(c, QA) + len(groups(c, 4)))
                    ln_stats(dve, VC[s], c, s, n, d_st)

                def transformed(c, s, n):
                    np_, nj = size(c)
                    dve.wait_ge(d_so[s], 32 * n)
                    for q, js in groups(c, 3):
                        dve.wait_ge(d_q, before_chunk(c, QB) + q + 1)
                        ins = nc.vector.tensor_tensor(
                            O3[s][0:np_, js[0]:js[-1] + 1, :],
                            bank(6 + q % 2, 3 * DX).rearrange("p (j f) -> p j f", f=DX)[0:np_, 0:len(js), :],
                            B3X[0:np_, :].unsqueeze(1).to_broadcast([np_, len(js), DX]), ALU.add)
                        ins.then_inc(d_oc, 1)
                    dve.wait_ge(d_oc, before_chunk(c, QB) + len(groups(c, 3)))
                    nc.vector.memset(col[0:1, 7:8], 0.0).then_inc(d_o[s], 1)
                lagged(dve, rows, transformed)

            @block.scalar
            def _(act):
                def turned(c, s, n):
                    np_, nj = size(c)
                    for q, js in groups(c, 4):
                        g = before_chunk(c, QA) + q
                        act.wait_ge(d_t, g + QA + 1)
                        if not isinstance(g, int) or g >= 2:
                            act.wait_ge(d_z, g - 1 if q else g)
                        nc.scalar.copy(TR[q % 2][:, 0:len(js), 0:np_],
                                       PS[:, PA + q % 2, 0:len(js), 0:np_]).then_inc(d_tc, 1)

                def normed(c, s, n):
                    np_, nj = size(c)
                    act.wait_ge(d_o[s], n)
                    ln_apply(act, VC[s], X3[s], c, s, n, d_rdy, d_sx, d_x3)
                    act.wait_ge(d_x3[s], n + 1)
                    act.dma_start(chunk(x3, c, D), X3[s][0:np_, 0:nj, :]).then_inc(d_sx[s], 16)
                    for q, js in groups(c, 3):
                        g = before_chunk(c, QB) + q
                        act.wait_ge(d_u, g + 1)
                        if not isinstance(g, int) or g >= 2:
                            act.wait_ge(d_q, g - 1 if q else g)
                        nc.scalar.copy(UR[q % 2][:, 0:len(js), 0:np_],
                                       PS[:, UB[q % 2], 0:len(js), 0:np_]).then_inc(d_uc, 1)
                    act.wait_ge(d_o[s], n + 1)
                    act.dma_start(chunk(xt_d, c, D + HEADS), O3[s][0:np_, 0:nj, 0:D + HEADS]).then_inc(d_so[s], 16)
                    act.dma_start(chunk(ad_d, c, HEADS), O3[s][0:np_, 0:nj, D + HEADS:DX]).then_inc(d_so[s], 16)
                lagged(act, turned, normed)
                for s in range(2):
                    act.wait_ge(d_sx[s], 16 * (CHUNKS // 2 + 1 - s))
                    act.wait_ge(d_so[s], 32 * (CHUNKS // 2 + 1 - s))

            @block.tensor
            def _(pe):
                pe.wait_ge(d_p, 1)
                nc.tensor.transpose(PS[:, PA, 0, :], W3, ident[:])
                nc.tensor.matmul(PS[:, PA, 1, 0:2 * HEADS], W3, IDA[:, D:DX], start=True, stop=True)
                nc.tensor.matmul(bank(PA + 1, DX), B3C, IDA, start=True, stop=True).then_inc(d_m, 1)
                pe.wait_ge(d_ready, 1)

                def two_steps(gs, turned, product):
                    for k, (q, js) in enumerate(gs):
                        turned(q, js)
                        if k:
                            product(*gs[k - 1])
                    product(*gs[-1])

                def turn(c, s, n):
                    np_, nj = size(c)

                    def turned(q, js):
                        for j in js:
                            ins = nc.tensor.transpose(PS[:, PA + q % 2, j % 4, 0:np_], X2L[s][0:np_, j, 0:D],
                                                      ident[0:np_, 0:np_])
                        ins.then_inc(d_t, 1)

                    def product(q, js):
                        g = before_chunk(c, QA) + q
                        pe.wait_ge(d_tc, g + 1)
                        if not isinstance(g, int) or g >= 2:
                            pe.wait_ge(d_v1, g - 1 if q else g)
                        for j in js:
                            ins = nc.tensor.matmul(PS[0:np_, SUM + q % 2, j % 4, :], TR[q % 2][:, j % 4, 0:np_], W2,
                                                   start=True, stop=True)
                        ins.then_inc(d_z, 1)
                    pe.wait_ge(d_ld[s], 32 * n + 32)
                    two_steps(groups(c, 4), turned, product)

                def transform(c, s, n):
                    np_, nj = size(c)

                    def turned(q, js):
                        for j in js:
                            ins = nc.tensor.transpose(PS[:, UB[q % 2], j % 3, 0:np_], X3[s][0:np_, j, :],
                                                      ident[0:np_, 0:np_])
                        ins.then_inc(d_u, 1)

                    def product(q, js):
                        g = before_chunk(c, QB) + q
                        pe.wait_ge(d_uc, g + 1)
                        if not isinstance(g, int) or g >= 2:
                            pe.wait_ge(d_oc, g - 1 if q else g)
                        for j in js:
                            ins = nc.tensor.matmul(bank(6 + q % 2, 512)[0:np_, (j % 3) * DX:(j % 3 + 1) * DX],
                                                   UR[q % 2][:, j % 3, 0:np_], W3X, start=True, stop=True)
                        ins.then_inc(d_q, 1)
                    pe.wait_ge(d_x3[s], n + 1)
                    two_steps(groups(c, 3), turned, product)
                lagged(pe, turn, transform)
        end_phase()

        XW = D + HEADS
        xts = big[:, 0:T * XW].rearrange("p (t f) -> p t f", f=XW)
        AL = sb("AL", [P, T, HEADS])
        AD = sb("AD", [P, U, HEADS])
        e_idx, e_cp = sem("e_idx"), sem("e_cp")
        e_got, e_gad = pool_sems("e_got", U), pool_sems("e_gad", U)
        with nc.Block() as block:
            @block.gpsimd
            def _(pool):
                with pool.Fori(0, IT) as i:
                    for j in range(U):
                        steady(pool, 2 * i + j // GR + 1)
                        if j % GR == 0:
                            pool.wait_ge(e_idx, 2 * i + j // GR + 1)
                            pool.wait_ge(e_cp, 2 * i + j // GR + 1)
                        pool.indirect_dma_start(G[:, j, 0:XW], None, xt_d, bass.IndirectOffsetOnAxis(
                            ap=ridx[:, j:j + 1], axis=0)).then_inc(e_got[j], 16)
                        steady(pool)
                        pool.indirect_dma_start(AD[:, j, :], None, ad_d, bass.IndirectOffsetOnAxis(
                            ap=sidx[:, j:j + 1], axis=0)).then_inc(e_gad[j], 16)

            @block.vector
            def _(dve):
                nc.vector.tensor_copy(ridx[:], src_i[:, 0:U])
                nc.vector.tensor_copy(sidx[:], dst_i[:, 0:U]).then_inc(e_idx, 2)
                credit(e_cp, 2)
                with dve.Fori(0, IT) as i:
                    for h in range(2):
                        js = slice(GR * h, GR * h + GR)
                        steady(dve, 16 * i + 16)
                        for q in range(GR * h, GR * h + GR):
                            dve.wait_ge(e_got[q], 16 * i + 16)
                            dve.wait_ge(e_gad[q], 16 * i + 16)
                        nc.vector.tensor_tensor(AL[:, bass.ds(U * i + GR * h, GR), :], G[:, js, D:XW], AD[:, js, :],
                                                ALU.add)
                        nc.vector.tensor_copy(ridx[:, js], src_i[:, bass.ds(U * i + U + GR * h, GR)])
                        nc.vector.tensor_copy(sidx[:, js], dst_i[:, bass.ds(U * i + U + GR * h, GR)]).then_inc(e_idx, 1)

            @block.scalar
            def _(act):
                with act.Fori(0, IT) as i:
                    for h in range(2):
                        steady(act, 16 * i + 16)
                        for q in range(GR * h, GR * h + GR):
                            act.wait_ge(e_got[q], 16 * i + 16)
                        nc.scalar.copy(xts[:, bass.ds(U * i + GR * h, GR), :], G[:, GR * h:GR * h + GR, :]).then_inc(e_cp, 1)

        HG = 2 * HEADS
        ALT = sb("ALT", [TG, 2, HEADS, P])
        FW = sb("FW", [TG, 2, HEADS, P])
        pen = sb("pen", [TG, 2, P])
        tpen = sb("tpen", [TG, 2, HEADS])
        tval = sb("tval", [TG, 2, HEADS])
        run4 = sb("run4", [HEADS, 3, T])
        cin = sb("cin", [TG, 2, HEADS])
        em = sb("em", [P, 4])
        f_al, f_t, f_v, f_tv, f_c, f_b, f_s, f_st, f_x, f_e = (sem("f_" + n) for n in "al t v tv c b s st x e".split())
        with nc.Block() as block:
            @block.vector
            def _(dve):
                a2 = AL[:].rearrange("p t h -> p (t h)")
                link(dve, "dve", nc.vector.scalar_tensor_tensor(a2, a2, 0.2, a2, ALU.mult, ALU.max))
                link(dve, "dve", nc.vector.tensor_scalar(em[:, 0:1], part_f[:, 0:1], 0.5, None, ALU.is_gt))
                link(dve, "dve", nc.vector.tensor_scalar(em[:, 1:2], part_f[:, 0:1], TE + 0.5, None, ALU.is_lt))
                link(dve, "dve", nc.vector.tensor_tensor(em[:, 0:1], em[:, 0:1], em[:, 1:2], ALU.mult))
                link(dve, "dve", nc.vector.tensor_scalar(em[:, 2:3], em[:, 0:1], -1.0, BIG, ALU.add, ALU.mult))
                nc.vector.tensor_scalar(a2, a2, em[:, 0:1], em[:, 2:3], ALU.mult, ALU.add).then_inc(f_al, 1)
                dve.wait_ge(f_t, 1)
                nc.vector.tensor_copy(ALT[:], PS[0:TG, 0:2, :, :])
                link(dve, "dve", nc.vector.memset(FW[:], 0.0))
                first, last = 1, TE
                for back in range(2):
                    link(dve, "dve", nc.vector.tensor_scalar(pen[:], (endrow if back else newseg)[:], -BIG, None,
                                                             ALU.mult))
                    sl = slice(last, first - 1, -1) if back else slice(first, last + 1)
                    for rescan in range(2):
                        for g in range(2):
                            for q in range(HEADS):
                                o = FW[:, g, q, sl]
                                nc.vector.tensor_tensor_scan(
                                    o, pen[:, g, sl], (FW if back else ALT)[:, g, q, sl],
                                    cin[:, g, q:q + 1] if rescan else -BIG, ALU.add, ALU.max)
                        link(dve, "dve", nc.vector.memset(col[:, 7:8], 0.0))
                        if rescan:
                            continue
                        nc.vector.tensor_copy(tval[:], FW[:, :, :, (first if back else last)])
                        for q in range(HEADS):
                            nc.vector.tensor_reduce(tpen[:, :, q], pen[:, :, first:last + 1], AX.X, ALU.min)
                        nc.vector.memset(col[:, 7:8], 0.0).then_inc(f_v, 1)
                        dve.wait_ge(f_tv, back + 1)
                        link(dve, "dve", nc.vector.tensor_copy(run4[:, 0:2, :], PS[0:HEADS, 2:4, :, :].rearrange(
                            "p a b c -> p a (b c)")[:, :, 0:T]))
                        t_all = slice(T - 1, None, -1) if back else slice(0, T)
                        link(dve, "dve", nc.vector.tensor_tensor_scan(run4[:, 2, t_all], run4[:, 0, t_all],
                                                                     run4[:, 1, t_all], -BIG, ALU.add, ALU.max))
                        if back:
                            nc.vector.tensor_copy(run4[:, 0, 0:T - 1], run4[:, 2, 1:T])
                            nc.vector.memset(run4[:, 0, T - 1:T], -BIG).then_inc(f_c, 1)
                        else:
                            nc.vector.tensor_copy(run4[:, 0, 1:T], run4[:, 2, 0:T - 1])
                            nc.vector.memset(run4[:, 0, 0:1], -BIG).then_inc(f_c, 1)
                        dve.wait_ge(f_b, back + 1)
                        link(dve, "dve", nc.vector.tensor_copy(cin[:].rearrange("p g q -> p (g q)"),
                                                               PS[0:TG, 4, 0, 0:HG]))
                nc.vector.memset(col[:, 7:8], 0.0).then_inc(f_s, 1)
                dve.wait_ge(f_st, 1)
                for g in range(2):
                    for q in range(HEADS):
                        ins = nc.vector.tensor_tensor(AL[:, TG * g:TG * g + TG, q], AL[:, TG * g:TG * g + TG, q],
                                                      PS[:, 5 + g, q, 0:TG], ALU.subtract)
                ins.then_inc(f_x, 1)

            @block.tensor
            def _(pe):
                pe.wait_ge(f_al, 1)
                for g in range(2):
                    for q in range(HEADS):
                        ins = nc.tensor.transpose(PS[0:TG, g, q, :], AL[:, TG * g:TG * g + TG, q], ident[:])
                ins.then_inc(f_t, 1)
                for back in range(2):
                    pe.wait_ge(f_v, back + 1)
                    for k, v in enumerate((tpen, tval)):
                        for g in range(2):
                            ins = nc.tensor.transpose(bank(2 + k)[0:HEADS, TG * g:TG * g + TG], v[:, g, :],
                                                      ident[0:TG, 0:TG])
                    ins.then_inc(f_tv, 1)
                    pe.wait_ge(f_c, back + 1)
                    for g in range(2):
                        ins = nc.tensor.transpose(PS[0:TG, 4, 0, HEADS * g:HEADS * g + HEADS],
                                                  run4[:, 0, TG * g:TG * g + TG], ident[0:HEADS, 0:HEADS])
                    ins.then_inc(f_b, 1)
                pe.wait_ge(f_s, 1)
                for g in range(2):
                    for q in range(HEADS):
                        ins = nc.tensor.transpose(PS[:, 5 + g, q, 0:TG], FW[:, g, q, :], ident[0:TG, 0:TG])
                ins.then_inc(f_st, 1)

            @block.scalar
            def _(act):
                act.wait_ge(f_x, 1)
                nc.scalar.activation(AL[:].rearrange("p t h -> p (t h)"), AL[:].rearrange("p t h -> p (t h)"),
                                     ACT.Exp).then_inc(f_e, 1)

        den = sb("den", [P, 2, GR * HEADS])
        h_mask, h_lr, h_z, h_ch, h_row, h_sum, h_d, h_y = (sem("h_" + n) for n in "mask lr z ch row sum d y".split())
        h_put = pool_sems("h_put", U)

        def local_sum(jj):
            return bank((CAR, PB)[jj // 2])[0:1, XW * (jj % 2):XW * (jj % 2) + XW]

        with nc.Block() as block:
            @block.gpsimd
            def _(pool):
                last_node = pool.to_reg(N - 1)
                with pool.Fori(0, IT) as i:
                    for j in range(U):
                        steady(pool, 2 * i + j // GR + 1)
                        if j % GR == 0:
                            pool.wait_ge(h_y, 2 * i + j // GR + 1)
                        pool.indirect_dma_start(agg, bass.IndirectOffsetOnAxis(ap=sidx[:, j:j + 1], axis=0),
                                                Y[:, j, :], None, bounds_check=last_node,
                                                oob_is_err=False).then_inc(h_put[j], 16)
                for j in range(U):
                    pool.wait_ge(h_put[j], 16 * IT)

            @block.vector
            def _(dve):
                last_segments(dve, None)
                nc.vector.memset(carry[:], 0.0).then_inc(h_ch, 1)
                nc.vector.tensor_copy(lring[:], lastc[:, 0:U]).then_inc(h_lr, 2)
                for j in range(GR):
                    ins = plain_mask(j, j)
                ins.then_inc(h_mask, 1)

                def weighted(i, h):
                    g = 2 * i + h
                    js = slice(GR * h, GR * h + GR)
                    for j in range(GR * h, GR * h + GR):
                        t = U * i + j
                        nc.vector.tensor_tensor(
                            G[:, j, 0:D].rearrange("p (q c) -> p q c", c=CH),
                            big[:, bass.ds(t * XW, D)].rearrange("p (q c) -> p q c", c=CH),
                            AL[:, bass.ds(t, 1), :].rearrange("p a q -> p (a q)").unsqueeze(2)
                            .to_broadcast([P, HEADS, CH]), ALU.mult)
                    steady(dve)
                    nc.vector.tensor_copy(G[:, js, D:XW], AL[:, bass.ds(U * i + GR * h, GR), :]).then_inc(h_z, 1)

                def summed(i, h):
                    g = 2 * i + h
                    js = slice(GR * h, GR * h + GR)
                    running_sums(dve, g, U * i + GR * h, h, lambda j: G[0:1, j, :], local_sum, carry[:, 0:XW],
                                 h_row, h_ch)
                    nc.vector.tensor_copy(lring[:, js], lastc[:, bass.ds(U * i + U + GR * h, GR)]).then_inc(h_lr, 1)
                    for j in range(GR):
                        ins = plain_mask(U * i + GR * (h + 1) + j, GR * (1 - h) + j)
                    ins.then_inc(h_mask, 1)

                def finished(i, h):
                    g = 2 * i + h
                    js = slice(GR * h, GR * h + GR)
                    dve.wait_ge(h_sum, g + 1)
                    nc.vector.tensor_scalar(den[:, h, :], PS[:, PA + h, 0, 0:GR * HEADS], 1e-16, None,
                                            ALU.add).then_inc(h_d, 1)
                    dve.wait_ge(h_d, 2 * g + 1)
                    nc.vector.reciprocal(den[:, h, :], den[:, h, :]).then_inc(h_d, 1)
                    steady(dve, 16 * i)
                    for q in range(GR * h, GR * h + GR):
                        dve.wait_ge(h_put[q], 16 * i)
                    nc.vector.tensor_copy(sidx[:, js], put_i[:, bass.ds(U * i + GR * h, GR)])
                    dve.wait_ge(h_d, 2 * g + 2)
                    nc.vector.tensor_tensor(
                        Y[:, GR * h:GR * h + GR, :].rearrange("p s (q c) -> p (s q) c", c=CH),
                        bank(SUM + h).rearrange("p (s c) -> p s c", c=CH),
                        den[:, h, :].unsqueeze(2).to_broadcast([P, GR * HEADS, CH]), ALU.mult).then_inc(h_y, 1)
                two_stages(dve, weighted, finished, summed)

            @block.tensor
            def _(pe):
                with pe.Fori(0, IT) as i:
                    for h in range(2):
                        g = 2 * i + h
                        for j in range(GR * h, GR * h + GR):
                            if j % GR == 0:
                                pe.wait_ge(h_lr, g + 1)
                                pe.wait_ge(h_ch, OPS * g + 1)
                                pe.wait_ge(h_z, g + 1)
                            nc.tensor.matmul(local_sum(j % GR), lring[:, j:j + 1], G[:, j, :],
                                             start=True, stop=True).then_inc(h_row, 1)
                        for j in range(GR * h, GR * h + GR):
                            if j % GR == 0:
                                pe.wait_ge(h_mask, g + 1)
                            pe.wait_ge(h_ch, OPS * g + j % GR + 2)
                            nc.tensor.matmul(PS[:, PA + h, 0, HEADS * (j % GR):HEADS * (j % GR) + HEADS], M[:, j, :],
                                             G[:, j, D:XW], start=True, stop=True)
                            ins = nc.tensor.matmul(PS[:, SUM + h, j % GR, :], M[:, j, :], G[:, j, 0:D],
                                                   start=True, stop=True)
                        ins.then_inc(h_sum, 1)
        end_phase()

        XA, YA, XN, V = areas([D, D, D, D])

        def make_out(dve, c, s, n, used, vr):
            np_, nj = size(c)
            nc.vector.tensor_tensor(V[s][0:np_, 0:nj, :], XA[s][0:np_, 0:nj, :], YA[s][0:np_, 0:nj, :],
                                    ALU.add).then_inc(vr[s], 1)

        norm_pass("D", [(XA, x3, D), (YA, agg, D)], V, XN, D, out, make_out)


_INS = ["x", "src", "dst", "edge_attr_128", "edge_weight", "L0_gnn_weight", "L0_gnn_bias", "L1_gnn_W", "L1_gnn_b",
        "L1_gnn_gamma", "L1_gnn_beta", "L2_gnn_W", "L2_gnn_b", "L2_gnn_We", "L2_gnn_be", "L3_gnn_coeffs_t",
        "L3_gnn_lin_weight", "L3_gnn_lin_bias", "L3_gnn_att_src", "L3_gnn_att_dst"]


def kernel(**inputs):
    import numpy as _np
    import concourse.bacc as _bacc
    from concourse import mybir as _mybir
    from concourse.bass_utils import run_bass_kernel_spmd as _run

    nc = _bacc.Bacc("TRN2", target_bir_lowering=False, num_devices=1)
    arrays, args = {}, []
    for name in _INS:
        a = _np.ascontiguousarray(inputs[name])
        arrays[f"in_{name}"] = a
        args.append(nc.dram_tensor(f"in_{name}", a.shape, _mybir.dt.from_np(a.dtype), kind="ExternalInput").ap())
    out = nc.dram_tensor("out_0", (N, D), F32, kind="ExternalOutput").ap()
    build(nc, *args, out)
    r = _run(nc, [arrays], core_ids=[0])
    return r.results[0]["out_0"]
```
